# Optimizing a Trainium2 kernel written in Bass

```python
import numpy as np
import jax
import jax.numpy as jnp

def _softmax(x, axis=-1):
    return jax.nn.softmax(x, axis=axis)

def _gelu(x):
    return jax.nn.gelu(x, approximate=True)

def _silu(x):
    return jax.nn.silu(x)

def _sigmoid(x):
    return jax.nn.sigmoid(x)

def _layernorm(x, axis=-1, eps=1e-05):
    m = jnp.mean(x, axis=axis, keepdims=True)
    v = jnp.var(x, axis=axis, keepdims=True)
    return (x - m) / jnp.sqrt(v + eps)

def _scatter_add(tgt, idx, src, axis=0):
    return tgt.at[idx].add(src)

def _segment_sum(src, seg, n):
    return jax.ops.segment_sum(src, seg, n)
kernel_name = 'mk_perceiver_d1_seqx_r4_1d2953'

def setup_inputs(seed: int=0):
    np.random.seed(seed)
    _w = jnp.asarray

    def _rec_inputs():
        import jax
        import jax.numpy as jnp
        _rk = jax.random.key(seed)
        x = -0.0003929 + 0.9999 * jax.random.normal(jax.random.fold_in(_rk, 1), (2, 64, 512), jnp.float32)
        _lenS = 64 - jax.random.randint(jax.random.fold_in(_rk, 7), (2,), 0, max(1, 64 // 4) + 1, jnp.int32)
        _lenS2 = 1024 - jax.random.randint(jax.random.fold_in(_rk, 8), (2,), 0, max(1, 1024 // 4) + 1, jnp.int32)
        _ctx_1024P = jax.random.normal(jax.random.fold_in(_rk, 11), (2, 16, 256), jnp.float32)
        _ctx_1024c = jax.random.dirichlet(jax.random.fold_in(_rk, 511), 0.3 * jnp.ones((16,), jnp.float32), (2, 1024))
        _ctx_1024t = jnp.einsum('bsk,bkd->bsd', _ctx_1024c, _ctx_1024P)
        _ctx_1024t = _ctx_1024t * jax.lax.rsqrt(jnp.mean(jnp.square(_ctx_1024t)) + 1e-12) * 0.953939
        ctx_1024 = -0.000494167 + 1.00018 * (_ctx_1024t + 0.3 * jax.random.normal(jax.random.fold_in(_rk, 611), (2, 1024, 256), jnp.float32))
        _validS = jnp.arange(64)[None, :] < _lenS[:, None]
        _validS2 = jnp.arange(1024)[None, :] < _lenS2[:, None]
        _causal = jnp.tril(jnp.ones((64, 64), dtype=bool))
        mask_BxS2_bf1 = jnp.ones((2, 1024), dtype=bool)
        return (x, ctx_1024, mask_BxS2_bf1)
    x, ctx_1024, mask_BxS2_bf1 = _rec_inputs()

    def _L0_xattn_setup():
        import jax, jax.numpy as jnp
        import numpy as np
        N_HEADS = 16
        N_KV_HEADS = 8
        HEAD_DIM = 128
        D_TEXT = 512
        D_VISION = 256
        GROUPS = N_HEADS // N_KV_HEADS
        key = jax.random.key(seed)
        ks = jax.random.split(key, 6)
        B, T_text, T_vis = (4, 512, 144)
        text_hidden = jax.random.normal(ks[0], (B, T_text, D_TEXT), dtype=jnp.float32)
        vision_tokens = jax.random.normal(ks[1], (B, T_vis, D_VISION), dtype=jnp.float32)
        vision_mask = jnp.ones((B, T_vis), dtype=bool)
        s = 0.02
        Wq = jax.random.normal(ks[2], (D_TEXT, N_HEADS * HEAD_DIM), dtype=jnp.float32) * s
        Wk = jax.random.normal(ks[3], (D_VISION, N_KV_HEADS * HEAD_DIM), dtype=jnp.float32) * s
        Wv = jax.random.normal(ks[4], (D_VISION, N_KV_HEADS * HEAD_DIM), dtype=jnp.float32) * s
        Wo = jax.random.normal(ks[5], (N_HEADS * HEAD_DIM, D_TEXT), dtype=jnp.float32) * s
        return {'text_hidden': text_hidden, 'vision_tokens': vision_tokens, 'vision_mask': vision_mask, 'Wq': Wq, 'Wk': Wk, 'Wv': Wv, 'Wo': Wo}
    _L0_xattn_all = _L0_xattn_setup()
    _L0_xattn_in = {k: v for k, v in _L0_xattn_all.items() if k in ('Wq', 'Wk', 'Wv', 'Wo')}
    del _L0_xattn_all

    def _L0_attn_setup():
        import jax, jax.numpy as jnp
        import numpy as np
        from jax import lax
        D_MODEL = 512
        D_STATE = 64
        D_CONV = 4
        EXPAND = 2
        HEADDIM = 64
        D_INNER = D_MODEL * EXPAND
        NHEADS = D_INNER // HEADDIM
        CONV_DIM = D_INNER + 2 * D_STATE
        D_IN_PROJ = 2 * D_INNER + 2 * D_STATE + NHEADS
        NUM_EXPERTS = 8
        TOP_K = 2
        D_FF = 4 * D_MODEL
        BATCH = 2
        SEQ = 128
        EPS = 1e-06

        def rmsnorm(x, w):
            return x * lax.rsqrt(jnp.mean(x * x, axis=-1, keepdims=True) + EPS) * w

        def silu(x):
            return x * jax.nn.sigmoid(x)

        def mamba2(x, in_proj_w, conv_w, conv_b, dt_bias, A_log, Dp, ssm_norm_w, out_proj_w):
            Bsz, L, _ = x.shape
            zxbcdt = x @ in_proj_w.T
            z, xBC, dt = jnp.split(zxbcdt, [D_INNER, D_INNER + CONV_DIM], axis=-1)
            xBC = lax.conv_general_dilated(xBC.transpose(0, 2, 1), conv_w[:, None, :], (1,), [(D_CONV - 1, 0)], feature_group_count=CONV_DIM)
            xBC = silu((xBC + conv_b[None, :, None]).transpose(0, 2, 1))
            xs, Bm, Cm = jnp.split(xBC, [D_INNER, D_INNER + D_STATE], axis=-1)
            dt = jax.nn.softplus(dt + dt_bias)
            A = -jnp.exp(A_log)
            xh = xs.reshape(Bsz, L, NHEADS, HEADDIM)

            def step(h, inp):
                dt_t, x_t, B_t, C_t = inp
                dA = jnp.exp(dt_t * A)
                h = h * dA[:, :, None, None] + dt_t[:, :, None, None] * x_t[..., None] * B_t[:, None, None, :]
                y = jnp.einsum('bhpn,bn->bhp', h, C_t)
                return (h, y)
            h0 = jnp.zeros((Bsz, NHEADS, HEADDIM, D_STATE), x.dtype)
            _, ys = lax.scan(step, h0, (dt.transpose(1, 0, 2), xh.transpose(1, 0, 2, 3), Bm.transpose(1, 0, 2), Cm.transpose(1, 0, 2)))
            y = ys.transpose(1, 0, 2, 3) + Dp[None, None, :, None] * xh
            y = y.reshape(Bsz, L, D_INNER)
            y = rmsnorm(y * silu(z), ssm_norm_w)
            return y @ out_proj_w.T

        def moe(x, gate_w, w1, w2):
            T = x.shape[0] * x.shape[1]
            xf = x.reshape(T, D_MODEL)
            logits = xf @ gate_w.T
            vals, idx = lax.top_k(logits, TOP_K)
            wts = jax.nn.softmax(vals, axis=-1)
            combine = jnp.sum(jax.nn.one_hot(idx, NUM_EXPERTS, dtype=x.dtype) * wts[..., None], axis=1)
            h = silu(jnp.einsum('td,efd->tef', xf, w1))
            eo = jnp.einsum('tef,edf->ted', h, w2)
            out = jnp.einsum('ted,te->td', eo, combine)
            probs = jax.nn.softmax(logits, axis=-1)
            lb = NUM_EXPERTS * jnp.sum(jnp.mean(probs, axis=0) ** 2)
            return (out.reshape(x.shape), lb)

        def safety(x, sp1_w, sp1_b, sp2_w, sp2_b, harm_w, harm_b, unc_w, unc_b, tox_w, tox_b):
            f = silu(x @ sp1_w.T + sp1_b) @ sp2_w.T + sp2_b
            harm = f @ harm_w.T + harm_b
            unc = jax.nn.sigmoid(f @ unc_w.T + unc_b)[..., 0]
            tox = jax.nn.sigmoid(f @ tox_w.T + tox_b)[..., 0]
            hs = jax.nn.sigmoid(harm)
            return (hs.max(-1), jnp.argmax(hs, -1), unc, tox, harm)

        def _reference_tuple_inner(x, in_proj_w, conv_w, conv_b, dt_bias, A_log, D, ssm_norm_w, out_proj_w, norm_mamba_w, norm_moe_w, gate_w, w1, w2, sp1_w, sp1_b, sp2_w, sp2_b, harm_w, harm_b, unc_w, unc_b, tox_w, tox_b):
            residual = x
            h = rmsnorm(x, norm_mamba_w)
            h = mamba2(h, in_proj_w, conv_w, conv_b, dt_bias, A_log, D, ssm_norm_w, out_proj_w) + residual
            x_moe, lb_loss = moe(rmsnorm(h, norm_moe_w), gate_w, w1, w2)
            h = h + x_moe
            risk_vals, risk_idx, unc, tox, harm = safety(h, sp1_w, sp1_b, sp2_w, sp2_b, harm_w, harm_b, unc_w, unc_b, tox_w, tox_b)
            return (h, risk_vals, risk_idx, unc, tox, harm, lb_loss)
        ks = jax.random.split(jax.random.key(seed), 24)
        s = 0.02
        n = lambda k, shape, sc=s: jax.random.normal(k, shape, jnp.float32) * sc
        return {'x': jax.random.normal(ks[0], (BATCH, SEQ, D_MODEL), jnp.float32), 'in_proj_w': n(ks[1], (D_IN_PROJ, D_MODEL)), 'conv_w': n(ks[2], (CONV_DIM, D_CONV), 0.1), 'conv_b': n(ks[3], (CONV_DIM,), 0.01), 'dt_bias': n(ks[4], (NHEADS,), 0.1), 'A_log': jnp.log(jax.random.uniform(ks[5], (NHEADS,), jnp.float32, 1.0, 16.0)), 'D': jnp.ones((NHEADS,), jnp.float32), 'ssm_norm_w': jnp.ones((D_INNER,), jnp.float32), 'out_proj_w': n(ks[6], (D_MODEL, D_INNER)), 'norm_mamba_w': jnp.ones((D_MODEL,), jnp.float32), 'norm_moe_w': jnp.ones((D_MODEL,), jnp.float32), 'gate_w': n(ks[7], (NUM_EXPERTS, D_MODEL)), 'w1': n(ks[8], (NUM_EXPERTS, D_FF, D_MODEL)), 'w2': n(ks[9], (NUM_EXPERTS, D_MODEL, D_FF)), 'sp1_w': n(ks[10], (D_MODEL // 2, D_MODEL)), 'sp1_b': jnp.zeros((D_MODEL // 2,), jnp.float32), 'sp2_w': n(ks[11], (128, D_MODEL // 2)), 'sp2_b': jnp.zeros((128,), jnp.float32), 'harm_w': n(ks[12], (5, 128)), 'harm_b': jnp.zeros((5,), jnp.float32), 'unc_w': n(ks[13], (1, 128)), 'unc_b': jnp.zeros((1,), jnp.float32), 'tox_w': n(ks[14], (1, 128)), 'tox_b': jnp.zeros((1,), jnp.float32)}
    _L0_attn_all = _L0_attn_setup()
    _L0_attn_in = {k: v for k, v in _L0_attn_all.items() if k in ('in_proj_w', 'conv_w', 'conv_b', 'dt_bias', 'A_log', 'D', 'ssm_norm_w', 'out_proj_w', 'norm_mamba_w', 'norm_moe_w', 'gate_w', 'w1', 'w2', 'sp1_w', 'sp1_b', 'sp2_w', 'sp2_b', 'harm_w', 'harm_b', 'unc_w', 'unc_b', 'tox_w', 'tox_b')}
    del _L0_attn_all

    def _L0_ffn_setup():
        import jax, jax.numpy as jnp
        import numpy as np
        H = 512
        NH = 32
        KVH = 4
        HD = 128
        E = 32
        TOPK = 8
        I = 256
        EPS = 1e-05
        THETA = 10000.0

        def _rmsnorm(x, w, eps=EPS):
            xf = x.astype(jnp.float32)
            var = jnp.mean(xf * xf, axis=-1, keepdims=True)
            return (w * (xf * jax.lax.rsqrt(var + eps))).astype(x.dtype)

        def _rope(x, pos):
            d = x.shape[-1]
            inv_freq = 1.0 / THETA ** (jnp.arange(0, d, 2, dtype=jnp.float32) / d)
            ang = pos.astype(jnp.float32)[:, None] * inv_freq[None, :]
            cos = jnp.cos(ang)[None, :, None, :]
            sin = jnp.sin(ang)[None, :, None, :]
            x1, x2 = jnp.split(x, 2, axis=-1)
            return jnp.concatenate([x1 * cos - x2 * sin, x1 * sin + x2 * cos], axis=-1)
        key = jax.random.key(seed)
        ks = jax.random.split(key, 16)
        s = 0.02
        n = lambda k, shape: jax.random.normal(k, shape, dtype=jnp.float32) * s
        return {'hidden_states': jax.random.normal(ks[0], (1, 128, H), dtype=jnp.float32), 'ln1_w': jnp.ones((H,), jnp.float32), 'ln2_w': jnp.ones((H,), jnp.float32), 'Wq': n(ks[1], (H, NH * HD)), 'Wk': n(ks[2], (H, KVH * HD)), 'Wv': n(ks[3], (H, KVH * HD)), 'Wo': n(ks[4], (NH * HD, H)), 'Wr': n(ks[5], (H, E)), 'expert_bias': jax.random.normal(ks[6], (E,), dtype=jnp.float32) * 0.1, 'Wg': n(ks[7], (E, H, I)), 'Wu': n(ks[8], (E, H, I)), 'Wd': n(ks[9], (E, I, H)), 'Wsg': n(ks[10], (H, I)), 'Wsu': n(ks[11], (H, I)), 'Wsd': n(ks[12], (I, H))}
    _L0_ffn_all = _L0_ffn_setup()
    _L0_ffn_in = {k: v for k, v in _L0_ffn_all.items() if k in ('ln1_w', 'ln2_w', 'Wq', 'Wk', 'Wv', 'Wo', 'Wr', 'expert_bias', 'Wg', 'Wu', 'Wd', 'Wsg', 'Wsu', 'Wsd')}
    del _L0_ffn_all
    return {'x': x, 'ctx_1024': ctx_1024, 'mask_BxS2_bf1': mask_BxS2_bf1, 'L0_xattn_Wq': _L0_xattn_in['Wq'], 'L0_xattn_Wk': _L0_xattn_in['Wk'], 'L0_xattn_Wv': _L0_xattn_in['Wv'], 'L0_xattn_Wo': _L0_xattn_in['Wo'], 'L0_attn_in_proj_w': _L0_attn_in['in_proj_w'], 'L0_attn_conv_w': _L0_attn_in['conv_w'], 'L0_attn_conv_b': _L0_attn_in['conv_b'], 'L0_attn_dt_bias': _L0_attn_in['dt_bias'], 'L0_attn_A_log': _L0_attn_in['A_log'], 'L0_attn_D': _L0_attn_in['D'], 'L0_attn_ssm_norm_w': _L0_attn_in['ssm_norm_w'], 'L0_attn_out_proj_w': _L0_attn_in['out_proj_w'], 'L0_attn_norm_mamba_w': _L0_attn_in['norm_mamba_w'], 'L0_attn_norm_moe_w': _L0_attn_in['norm_moe_w'], 'L0_attn_gate_w': _L0_attn_in['gate_w'], 'L0_attn_w1': _L0_attn_in['w1'], 'L0_attn_w2': _L0_attn_in['w2'], 'L0_attn_sp1_w': _L0_attn_in['sp1_w'], 'L0_attn_sp1_b': _L0_attn_in['sp1_b'], 'L0_attn_sp2_w': _L0_attn_in['sp2_w'], 'L0_attn_sp2_b': _L0_attn_in['sp2_b'], 'L0_attn_harm_w': _L0_attn_in['harm_w'], 'L0_attn_harm_b': _L0_attn_in['harm_b'], 'L0_attn_unc_w': _L0_attn_in['unc_w'], 'L0_attn_unc_b': _L0_attn_in['unc_b'], 'L0_attn_tox_w': _L0_attn_in['tox_w'], 'L0_attn_tox_b': _L0_attn_in['tox_b'], 'L0_ffn_ln1_w': _L0_ffn_in['ln1_w'], 'L0_ffn_ln2_w': _L0_ffn_in['ln2_w'], 'L0_ffn_Wq': _L0_ffn_in['Wq'], 'L0_ffn_Wk': _L0_ffn_in['Wk'], 'L0_ffn_Wv': _L0_ffn_in['Wv'], 'L0_ffn_Wo': _L0_ffn_in['Wo'], 'L0_ffn_Wr': _L0_ffn_in['Wr'], 'L0_ffn_expert_bias': _L0_ffn_in['expert_bias'], 'L0_ffn_Wg': _L0_ffn_in['Wg'], 'L0_ffn_Wu': _L0_ffn_in['Wu'], 'L0_ffn_Wd': _L0_ffn_in['Wd'], 'L0_ffn_Wsg': _L0_ffn_in['Wsg'], 'L0_ffn_Wsu': _L0_ffn_in['Wsu'], 'L0_ffn_Wsd': _L0_ffn_in['Wsd']}

def reference(x, ctx_1024, mask_BxS2_bf1, L0_xattn_Wq, L0_xattn_Wk, L0_xattn_Wv, L0_xattn_Wo, L0_attn_in_proj_w, L0_attn_conv_w, L0_attn_conv_b, L0_attn_dt_bias, L0_attn_A_log, L0_attn_D, L0_attn_ssm_norm_w, L0_attn_out_proj_w, L0_attn_norm_mamba_w, L0_attn_norm_moe_w, L0_attn_gate_w, L0_attn_w1, L0_attn_w2, L0_attn_sp1_w, L0_attn_sp1_b, L0_attn_sp2_w, L0_attn_sp2_b, L0_attn_harm_w, L0_attn_harm_b, L0_attn_unc_w, L0_attn_unc_b, L0_attn_tox_w, L0_attn_tox_b, L0_ffn_ln1_w, L0_ffn_ln2_w, L0_ffn_Wq, L0_ffn_Wk, L0_ffn_Wv, L0_ffn_Wo, L0_ffn_Wr, L0_ffn_expert_bias, L0_ffn_Wg, L0_ffn_Wu, L0_ffn_Wd, L0_ffn_Wsg, L0_ffn_Wsu, L0_ffn_Wsd):
    import jax
    import jax.numpy as jnp

    def _L0_xattn_ref(text_hidden, vision_tokens, vision_mask, Wq, Wk, Wv, Wo):
        import jax, jax.numpy as jnp
        import numpy as np
        N_HEADS = 16
        N_KV_HEADS = 8
        HEAD_DIM = 128
        D_TEXT = 512
        D_VISION = 256
        GROUPS = N_HEADS // N_KV_HEADS
        B, T_text, _ = text_hidden.shape
        T_vis = vision_tokens.shape[1]
        scale = jnp.float32(np.sqrt(HEAD_DIM))
        q = (text_hidden @ Wq).reshape(B, T_text, N_HEADS, HEAD_DIM).transpose(0, 2, 1, 3)
        k = (vision_tokens @ Wk).reshape(B, T_vis, N_KV_HEADS, HEAD_DIM).transpose(0, 2, 1, 3)
        v = (vision_tokens @ Wv).reshape(B, T_vis, N_KV_HEADS, HEAD_DIM).transpose(0, 2, 1, 3)
        k = jnp.repeat(k, GROUPS, axis=1)
        v = jnp.repeat(v, GROUPS, axis=1)
        scores = jnp.einsum('bhtd,bhsd->bhts', q, k) / scale
        mask = vision_mask[:, None, None, :]
        scores = jnp.where(mask, scores, -jnp.inf)
        attn = jax.nn.softmax(scores, axis=-1)
        attn = jnp.nan_to_num(attn, nan=0.0)
        out = jnp.einsum('bhts,bhsd->bhtd', attn, v)
        out = out.transpose(0, 2, 1, 3).reshape(B, T_text, N_HEADS * HEAD_DIM)
        return out @ Wo

    def _L0_attn_ref(x, in_proj_w, conv_w, conv_b, dt_bias, A_log, D, ssm_norm_w, out_proj_w, norm_mamba_w, norm_moe_w, gate_w, w1, w2, sp1_w, sp1_b, sp2_w, sp2_b, harm_w, harm_b, unc_w, unc_b, tox_w, tox_b):
        import jax, jax.numpy as jnp
        import numpy as np
        from jax import lax
        D_MODEL = 512
        D_STATE = 64
        D_CONV = 4
        EXPAND = 2
        HEADDIM = 64
        D_INNER = D_MODEL * EXPAND
        NHEADS = D_INNER // HEADDIM
        CONV_DIM = D_INNER + 2 * D_STATE
        D_IN_PROJ = 2 * D_INNER + 2 * D_STATE + NHEADS
        NUM_EXPERTS = 8
        TOP_K = 2
        D_FF = 4 * D_MODEL
        BATCH = 2
        SEQ = 128
        EPS = 1e-06

        def rmsnorm(x, w):
            return x * lax.rsqrt(jnp.mean(x * x, axis=-1, keepdims=True) + EPS) * w

        def silu(x):
            return x * jax.nn.sigmoid(x)

        def mamba2(x, in_proj_w, conv_w, conv_b, dt_bias, A_log, Dp, ssm_norm_w, out_proj_w):
            Bsz, L, _ = x.shape
            zxbcdt = x @ in_proj_w.T
            z, xBC, dt = jnp.split(zxbcdt, [D_INNER, D_INNER + CONV_DIM], axis=-1)
            xBC = lax.conv_general_dilated(xBC.transpose(0, 2, 1), conv_w[:, None, :], (1,), [(D_CONV - 1, 0)], feature_group_count=CONV_DIM)
            xBC = silu((xBC + conv_b[None, :, None]).transpose(0, 2, 1))
            xs, Bm, Cm = jnp.split(xBC, [D_INNER, D_INNER + D_STATE], axis=-1)
            dt = jax.nn.softplus(dt + dt_bias)
            A = -jnp.exp(A_log)
            xh = xs.reshape(Bsz, L, NHEADS, HEADDIM)

            def step(h, inp):
                dt_t, x_t, B_t, C_t = inp
                dA = jnp.exp(dt_t * A)
                h = h * dA[:, :, None, None] + dt_t[:, :, None, None] * x_t[..., None] * B_t[:, None, None, :]
                y = jnp.einsum('bhpn,bn->bhp', h, C_t)
                return (h, y)
            h0 = jnp.zeros((Bsz, NHEADS, HEADDIM, D_STATE), x.dtype)
            _, ys = lax.scan(step, h0, (dt.transpose(1, 0, 2), xh.transpose(1, 0, 2, 3), Bm.transpose(1, 0, 2), Cm.transpose(1, 0, 2)))
            y = ys.transpose(1, 0, 2, 3) + Dp[None, None, :, None] * xh
            y = y.reshape(Bsz, L, D_INNER)
            y = rmsnorm(y * silu(z), ssm_norm_w)
            return y @ out_proj_w.T

        def moe(x, gate_w, w1, w2):
            T = x.shape[0] * x.shape[1]
            xf = x.reshape(T, D_MODEL)
            logits = xf @ gate_w.T
            vals, idx = lax.top_k(logits, TOP_K)
            wts = jax.nn.softmax(vals, axis=-1)
            combine = jnp.sum(jax.nn.one_hot(idx, NUM_EXPERTS, dtype=x.dtype) * wts[..., None], axis=1)
            h = silu(jnp.einsum('td,efd->tef', xf, w1))
            eo = jnp.einsum('tef,edf->ted', h, w2)
            out = jnp.einsum('ted,te->td', eo, combine)
            probs = jax.nn.softmax(logits, axis=-1)
            lb = NUM_EXPERTS * jnp.sum(jnp.mean(probs, axis=0) ** 2)
            return (out.reshape(x.shape), lb)

        def safety(x, sp1_w, sp1_b, sp2_w, sp2_b, harm_w, harm_b, unc_w, unc_b, tox_w, tox_b):
            f = silu(x @ sp1_w.T + sp1_b) @ sp2_w.T + sp2_b
            harm = f @ harm_w.T + harm_b
            unc = jax.nn.sigmoid(f @ unc_w.T + unc_b)[..., 0]
            tox = jax.nn.sigmoid(f @ tox_w.T + tox_b)[..., 0]
            hs = jax.nn.sigmoid(harm)
            return (hs.max(-1), jnp.argmax(hs, -1), unc, tox, harm)

        def _reference_tuple_inner(x, in_proj_w, conv_w, conv_b, dt_bias, A_log, D, ssm_norm_w, out_proj_w, norm_mamba_w, norm_moe_w, gate_w, w1, w2, sp1_w, sp1_b, sp2_w, sp2_b, harm_w, harm_b, unc_w, unc_b, tox_w, tox_b):
            residual = x
            h = rmsnorm(x, norm_mamba_w)
            h = mamba2(h, in_proj_w, conv_w, conv_b, dt_bias, A_log, D, ssm_norm_w, out_proj_w) + residual
            x_moe, lb_loss = moe(rmsnorm(h, norm_moe_w), gate_w, w1, w2)
            h = h + x_moe
            risk_vals, risk_idx, unc, tox, harm = safety(h, sp1_w, sp1_b, sp2_w, sp2_b, harm_w, harm_b, unc_w, unc_b, tox_w, tox_b)
            return (h, risk_vals, risk_idx, unc, tox, harm, lb_loss)
        return _reference_tuple_inner(x, in_proj_w, conv_w, conv_b, dt_bias, A_log, D, ssm_norm_w, out_proj_w, norm_mamba_w, norm_moe_w, gate_w, w1, w2, sp1_w, sp1_b, sp2_w, sp2_b, harm_w, harm_b, unc_w, unc_b, tox_w, tox_b)[0]

    def _L0_ffn_ref(hidden_states, ln1_w, ln2_w, Wq, Wk, Wv, Wo, Wr, expert_bias, Wg, Wu, Wd, Wsg, Wsu, Wsd):
        import jax, jax.numpy as jnp
        import numpy as np
        H = 512
        NH = 32
        KVH = 4
        HD = 128
        E = 32
        TOPK = 8
        I = 256
        EPS = 1e-05
        THETA = 10000.0

        def _rmsnorm(x, w, eps=EPS):
            xf = x.astype(jnp.float32)
            var = jnp.mean(xf * xf, axis=-1, keepdims=True)
            return (w * (xf * jax.lax.rsqrt(var + eps))).astype(x.dtype)

        def _rope(x, pos):
            d = x.shape[-1]
            inv_freq = 1.0 / THETA ** (jnp.arange(0, d, 2, dtype=jnp.float32) / d)
            ang = pos.astype(jnp.float32)[:, None] * inv_freq[None, :]
            cos = jnp.cos(ang)[None, :, None, :]
            sin = jnp.sin(ang)[None, :, None, :]
            x1, x2 = jnp.split(x, 2, axis=-1)
            return jnp.concatenate([x1 * cos - x2 * sin, x1 * sin + x2 * cos], axis=-1)
        B, S, _ = hidden_states.shape
        resid = hidden_states
        h = _rmsnorm(hidden_states, ln1_w)
        pos = jnp.arange(S)
        q = (h @ Wq).reshape(B, S, NH, HD)
        k = (h @ Wk).reshape(B, S, KVH, HD)
        v = (h @ Wv).reshape(B, S, KVH, HD)
        q = _rope(q, pos)
        k = _rope(k, pos)
        rep = NH // KVH
        k = jnp.repeat(k, rep, axis=2)
        v = jnp.repeat(v, rep, axis=2)
        scores = jnp.einsum('bqhd,bkhd->bhqk', q, k) / jnp.sqrt(jnp.float32(HD))
        causal = jnp.tril(jnp.ones((S, S), dtype=bool))
        scores = jnp.where(causal[None, None], scores, jnp.float32(-1000000000.0))
        attn = jax.nn.softmax(scores, axis=-1)
        o = jnp.einsum('bhqk,bkhd->bqhd', attn, v).reshape(B, S, NH * HD) @ Wo
        x = resid + o
        resid = x
        h = _rmsnorm(x, ln2_w)
        t = h.reshape(-1, H)
        T = t.shape[0]
        router_scores = jax.nn.sigmoid(t @ Wr)
        _, idx = jax.lax.top_k(router_scores + expert_bias[None, :], TOPK)
        w = jnp.take_along_axis(router_scores, idx, axis=1)
        w = w / jnp.sum(w, axis=-1, keepdims=True)
        wfull = jnp.zeros((T, E), jnp.float32).at[jnp.arange(T)[:, None], idx].set(w)
        g = jnp.einsum('th,ehi->tei', t, Wg)
        u = jnp.einsum('th,ehi->tei', t, Wu)
        act = jax.nn.silu(g) * u
        moe = jnp.einsum('tei,te,eih->th', act, wfull, Wd)
        shared = jax.nn.silu(t @ Wsg) * (t @ Wsu) @ Wsd
        return resid + (moe + shared).reshape(B, S, H)
    x = x + _L0_xattn_ref(_layernorm(x, axis=-1), ctx_1024, mask_BxS2_bf1, L0_xattn_Wq, L0_xattn_Wk, L0_xattn_Wv, L0_xattn_Wo)
    x = x + _L0_attn_ref(_layernorm(x, axis=-1), L0_attn_in_proj_w, L0_attn_conv_w, L0_attn_conv_b, L0_attn_dt_bias, L0_attn_A_log, L0_attn_D, L0_attn_ssm_norm_w, L0_attn_out_proj_w, L0_attn_norm_mamba_w, L0_attn_norm_moe_w, L0_attn_gate_w, L0_attn_w1, L0_attn_w2, L0_attn_sp1_w, L0_attn_sp1_b, L0_attn_sp2_w, L0_attn_sp2_b, L0_attn_harm_w, L0_attn_harm_b, L0_attn_unc_w, L0_attn_unc_b, L0_attn_tox_w, L0_attn_tox_b)
    x = x + _L0_ffn_ref(_layernorm(x, axis=-1), L0_ffn_ln1_w, L0_ffn_ln2_w, L0_ffn_Wq, L0_ffn_Wk, L0_ffn_Wv, L0_ffn_Wo, L0_ffn_Wr, L0_ffn_expert_bias, L0_ffn_Wg, L0_ffn_Wu, L0_ffn_Wd, L0_ffn_Wsg, L0_ffn_Wsu, L0_ffn_Wsd)
    return x

_drawn_inputs = setup_inputs


def setup_inputs(seed=0):
    import zlib

    import numpy as np

    out = dict(_drawn_inputs(seed))
    spreads = {'L0_attn_D': (1.0, 0.2),
     'L0_attn_ssm_norm_w': (1.0, 0.2),
     'L0_attn_norm_mamba_w': (1.0, 0.2),
     'L0_attn_norm_moe_w': (1.0, 0.2),
     'L0_attn_sp1_b': (0.0, 0.1),
     'L0_attn_sp2_b': (0.0, 0.1),
     'L0_attn_harm_b': (0.0, 0.1),
     'L0_ffn_ln1_w': (1.0, 0.6),
     'L0_ffn_ln2_w': (1.0, 0.6)}
    factors = {'L0_xattn_Wq': 5.577,
     'L0_xattn_Wk': 5.09,
     'L0_attn_dt_bias': 8.0,
     'L0_attn_A_log': 64.0,
     'L0_ffn_Wq': 5.688,
     'L0_ffn_Wk': 5.694,
     'L0_ffn_Wr': 8.0,
     'L0_ffn_expert_bias': 8.0,
     'L0_ffn_Wg': 8.0,
     'L0_ffn_Wu': 8.0,
     'L0_ffn_Wd': 8.0,
     'L0_ffn_Wsg': 4.733,
     'L0_ffn_Wsu': 4.633,
     'L0_ffn_Wsd': 4.626}
    for name, (base, spread) in spreads.items():
        noise = np.random.default_rng([zlib.crc32(name.encode()), seed]).standard_normal(out[name].shape)
        drawn = base * np.exp(spread * noise) if base else spread * noise
        out[name] = jnp.asarray(drawn.astype(out[name].dtype))
    for name, factor in factors.items():
        out[name] = (out[name] * factor).astype(out[name].dtype)
    return out
```

```python
from contextlib import ExitStack

import concourse.bass as bass
from concourse import mybir

F32 = mybir.dt.float32
U8 = mybir.dt.uint8
ALU = mybir.AluOpType
ACT = mybir.ActivationFunctionType

P = 128
B, S, D = 2, 64, 512
T = B * S
KD = D // P
S2, DC = 1024, 256
KC, SC = DC // P, S2 // P
XKV, XD = 8, 128
DI, DS, MH, HP = 1024, 64, 16, 64
XC = DI // P
CC = XC + 2
TAPS = 4
PAD = S + TAPS - 1
E1, FF1 = 8, 2048
N1 = FF1 // 512
STEPS1 = E1 * N1
AH, AKV, AD = 32, 4, 128
UNITS = AH // 4
E2, FF2 = 32, 256
STEPS2 = E2 + 1
CHUNK = 2048
SLOTS = 8
QKW, VOW = KD * 2 * XD + DC, KC * XD + 2 * D
MASKED = -1.0e30
LN_EPS, MIX_EPS, FFN_EPS = 1e-5, 1e-6, 1e-5
A_LOG_TOP, DECAY_BOTTOM = 80.0, -120.0

C_IN, C_OUT = 0, KD
C_W1 = C_OUT + 2


C_ATT = C_W1 + 2 * STEPS1
C_FFN = C_ATT + 2 + 2 * UNITS
CHUNKS = C_FFN + 2 * STEPS2

V_MIX, V_MOE, V_SSM, V_LN1, V_LN2 = 0, KD, 2 * KD, 2 * KD + XC, 3 * KD + XC
V_TAP = 4 * KD + XC
V_CB = V_TAP + CC * TAPS
V_GATE = V_CB + CC
V_ROUTE = V_GATE + KD * E1
V_BCDT = V_ROUTE + KD * E2
BCDT = 2 * DS + MH
VECS = V_BCDT + KD * BCDT
R_DT, R_A, R_D, R_EB = 0, MH, 2 * MH, 3 * MH
ROWS = 3 * MH + E2


def up_chunk(base, s):
    return base + s if isinstance(s, int) and s < 2 else base - 2 + 2 * s


def down_chunk(base, s, steps):
    return base + steps + s if isinstance(s, int) and s >= steps - 2 else base + 3 + 2 * s


def build(nc, x, mask, ctx, ctxT, qk, vo, vecs, rows, rope, in_w, out_w, w1, w2, wkv, wq, wo, gu, dn, out):
    stack = ExitStack()
    with stack:
        def sem(name):
            return stack.enter_context(nc.semaphore(name))

        def sb(name, shape, dt=F32, scope=stack):
            return scope.enter_context(nc.sbuf_tensor(name, shape, dt))

        PS = stack.enter_context(nc.psum_tensor("PS", [P, 8, 512], F32))

        ring = sb("ring", [P, SLOTS, CHUNK])
        vec = sb("vec", [P, VECS])
        row = sb("row", [P, ROWS])
        ident = sb("ident", [P, P])
        tri = sb("tri", [P, P])
        later = sb("later", [P, P])
        amask = sb("amask", [P, P])
        xt = sb("xt", [P, D])
        res = sb("res", [P, D])
        mid = sb("mid", [P, D])
        nrm = sb("nrm", [P, D])
        junk = sb("junk", [P, D])
        nT = sb("nT", [P, KD, P])
        st = sb("st", [P, 8])
        bnst = sb("bnst", [P, 6])
        mv = sb("mv", [P, 2])
        epsc = sb("epsc", [P, 2])
        cw = sb("cw", [P, E2 + 1])
        r8 = sb("r8", [P, 16])
        rsc = sb("rsc", [P, 4, E2])
        h_sig = sb("h_sig", [P, 2, 512])
        h_act = sb("h_act", [P, 2, 512])
        hT = sb("hT", [P, 2, 4, P])
        xpad = sb("xpad", [P, CC, B, PAD])

        rp = sb("rp", [P, 2, AD])

        with ExitStack() as scope:
            cT = sb("cT", [P, B, KC, S2], scope=scope)
            cx = sb("cx", [P, B, SC, DC], scope=scope)
            mask8 = sb("mask8", [P, B, S2], U8, scope=scope)
            madd = sb("madd", [P, B, S2], scope=scope)
            sc_sb = sb("sc_sb", [P, B, S2], scope=scope)
            pr = sb("pr", [P, B, S2], scope=scope)
            pT = sb("pT", [P, B, SC, P], scope=scope)
            qk_sb = sb("qk_sb", [P, QKW], scope=scope)
            vo_sb = sb("vo_sb", [P, VOW], scope=scope)
            q_sb = sb("q_sb", [P, 2 * XD], scope=scope)
            qT = sb("qT", [P, 2 * T], scope=scope)
            qp = sb("qp", [P, KC, B, P], scope=scope)
            co = sb("co", [P, B, DC], scope=scope)
            coT = sb("coT", [P, KC, B, P], scope=scope)
            oT = sb("oT", [P, 2, T], scope=scope)
            xmax = sb("xmax", [P, B], scope=scope)
            nbias = sb("nbias", [P, B], scope=scope)
            xsum = sb("xsum", [P, B], scope=scope)
            xrec = sb("xrec", [P, B], scope=scope)
            xval = sb("xval", [P, B], scope=scope)
            held = sb("held", [P, 1], scope=scope)

        with ExitStack() as scope:
            zs = sb("zs", [P, DI], scope=scope)
            x_sb = sb("x_sb", [P, DI], scope=scope)
            bc_sb = sb("bc_sb", [P, BCDT], scope=scope)
            cacc = sb("cacc", [P, CC, T], scope=scope)
            csig = sb("csig", [P, CC, T], scope=scope)
            cact = sb("cact", [P, CC, T], scope=scope)
            xdt = sb("xdt", [P, MH, HP], scope=scope)
            xD_ = sb("xD_", [P, MH, HP], scope=scope)
            dts = sb("dts", [P, 8, MH], scope=scope)
            wdec = sb("wdec", [P, MH, T], scope=scope)
            dec = sb("dec", [P, MH, T], scope=scope)
            gm = sb("gm", [P, P], scope=scope)
            y_sb = sb("y_sb", [P, DI], scope=scope)
            ysq = sb("ysq", [P, DI], scope=scope)
            yT = sb("yT", [P, XC, P], scope=scope)

        with ExitStack() as scope:
            ra = sb("ra", [P, 2, 4, AD], scope=scope)
            rb = sb("rb", [P, 2, 4, AD], scope=scope)
            rq = sb("rq", [P, 2, 4, AD], scope=scope)
            aqT = sb("aqT", [P, 2, 4, T], scope=scope)
            akT = sb("akT", [P, AKV, T], scope=scope)
            av = sb("av", [P, AKV, AD], scope=scope)
            asc = sb("asc", [P, 2, 4, T], scope=scope)
            apr = sb("apr", [P, 2, 4, T], scope=scope)
            apn = sb("apn", [P, 2, 4, T], scope=scope)
            apT = sb("apT", [P, 4, T], scope=scope)
            aoT = sb("aoT", [P, 4, T], scope=scope)
            amx = sb("amx", [P, 2, 4], scope=scope)
            anb = sb("anb", [P, 2, 4], scope=scope)
            asm = sb("asm", [P, 2, 4], scope=scope)
            arc = sb("arc", [P, 2, 4], scope=scope)

        ACC = PS[:, 0, :]
        x_scores = [PS[:, 1:3, :].rearrange("p a n -> p (a n)"), PS[:, 3:5, :].rearrange("p a n -> p (a n)")]
        x_ctxo = [PS[:, 1, 0:DC], PS[:, 3, 0:DC]]
        x_qp = PS[:, 2, :]
        x_tr = [PS[:, 5, :], PS[:, 6, :]]
        x_ma, x_mb = PS[:, 7, 0:256], PS[:, 7, 256:512]

        L = {n: sem("ld_" + n) for n in ("x", "qk", "vo", "mask", "cT0", "cT1", "cx0", "cx1", "vec", "row", "rope")}
        ring_loaded = [sem(f"ring_loaded{i}") for i in range(SLOTS)]
        ring_used = sem("ring_used")
        s_out = sem("s_out")
        s_const = sem("s_const")
        s_pool = sem("s_pool")
        s_dve = sem("s_dve")
        s_act = sem("s_act")
        var_ready = sem("var_ready")
        rstd_ready = sem("rstd_ready")
        norm_ready = sem("norm_ready")
        nT_made = sem("nT_made")
        nT_ready = sem("nT_ready")
        acc_ready = sem("acc_ready")
        mid_ready = sem("mid_ready")
        sc_ready, s_max, nb_ready, exp_done = sem("sc_ready"), sem("s_max"), sem("nb_ready"), sem("exp_done")
        q_ready, q_copied = sem("q_ready"), sem("q_copied")
        qT_ready, qT_copied = sem("qT_ready"), sem("qT_copied")
        qp_ready, qp_copied = sem("qp_ready"), sem("qp_copied")
        pT_ready, pT_copied = sem("pT_ready"), sem("pT_copied")
        co_ready, co_copied = sem("co_ready"), sem("co_copied")
        coT_ready, coT_copied = sem("coT_ready"), sem("coT_copied")
        oT_ready, oT_copied, wo_done = sem("oT_ready"), sem("oT_copied"), sem("wo_done")
        x_dve = sem("x_dve")
        M = {n: sem("m_" + n) for n in ("zx", "bcdt", "x_sb", "bc_sb", "xT", "bcT", "pad", "conv", "csig", "cact", "g", "gm",
                                        "expA", "abs", "expd", "u", "lnu", "dtA", "wdec", "dsum", "decay", "xtok", "xdt",
                                        "zsig", "zraw", "A", "mdec", "y", "yg", "yT", "yTs", "outp", "logit", "rexp", "cw")}
        sig_ready, act_ready, hT_made, hT_ready = (sem(n) for n in ("sig_ready", "act_ready", "hT_made", "hT_ready"))
        gsig_ready, gs_ready, a_ready, aT_made, aT_ready = (sem(n) for n in ("gsig_ready", "gs_ready", "a_ready", "aT_made", "aT_ready"))
        A = {n: sem("a_" + n) for n in ("kv", "v", "krope", "kT", "kTs", "q", "ropes", "rope", "qT", "qTs", "s", "max", "nb", "exp",
                                        "rec", "pn", "pT", "pTs", "o", "os", "logit", "rsig", "cw")}

        def wait_chunk(eng, slot, lap):
            eng.wait_ge(ring_loaded[slot], lap * 16 + 16)

        block = stack.enter_context(nc.Block())

        @block.sync
        def _(sp):
            def load(dst, src, s):
                sp.dma_start(dst, src).then_inc(s, 16)

            def ring_load(c, src, lap=None, free=None):
                slot = c % SLOTS
                if c >= SLOTS:
                    sp.wait_ge(ring_used, (c - SLOTS + 1) if free is None else free)
                n = src.shape[-1]
                sp.dma_start(ring[:, slot, 0:n], src).then_inc(ring_loaded[slot], 16)

            load(xt[:], x, L["x"])
            load(row[:], rows.to_broadcast([P, ROWS]), L["row"])
            load(qk_sb[:], qk[0], L["qk"])
            load(mask8[:].rearrange("p b s -> p (b s)"), mask.to_broadcast([P, B * S2]), L["mask"])
            load(cT[:, 0], ctxT[:, 0], L["cT0"])
            load(cT[:, 1], ctxT[:, 1], L["cT1"])
            load(cx[:, 0], ctx[:, 0], L["cx0"])
            load(cx[:, 1], ctx[:, 1], L["cx1"])
            load(vo_sb[:], vo[0], L["vo"])
            load(vec[:], vecs, L["vec"])
            load(rp[:], rope, L["rope"])
            sp.wait_ge(qp_ready, 1)
            load(qk_sb[:], qk[1], L["qk"])
            stream = [in_w[k] for k in range(KD)] + [out_w[0], out_w[1]]
            stream += [w1[0], w1[1], w1[2], w2[0], w1[3], w2[1]]
            for c in range(SLOTS):
                ring_load(c, stream[c])
            with sp.Fori(1, XKV - 1) as j:
                sp.wait_ge(qp_ready, j + 1)
                load(qk_sb[:], qk[bass.ds(j + 1, 1)].rearrange("a p n -> p (a n)"), L["qk"])
                sp.wait_ge(wo_done, j)
                load(vo_sb[:], vo[bass.ds(j, 1)].rearrange("a p n -> p (a n)"), L["vo"])
            sp.wait_ge(wo_done, XKV - 1)
            load(vo_sb[:], vo[XKV - 1], L["vo"])
            for c in range(SLOTS, len(stream)):
                ring_load(c, stream[c])
            with sp.Fori(1, E1) as e:
                for t in range(N1):
                    c = up_chunk(C_W1, 4 + t)
                    ring_load(c, w1[bass.ds(e * 4 + t, 1)].rearrange("a p n -> p (a n)"),
                              free=(e - 1) * 8 + (c - SLOTS + 1))
                    ring_load(c + 1, w2[bass.ds(e * 4 + t - 2, 1)].rearrange("a p n -> p (a n)"),
                              free=(e - 1) * 8 + (c - SLOTS + 2))
            stream = [(down_chunk(C_W1, s, STEPS1), w2[s]) for s in (STEPS1 - 2, STEPS1 - 1)]
            stream += [(C_ATT, wkv[0]), (C_ATT + 1, wkv[1])]
            for s in range(UNITS + 2):
                if s < UNITS:
                    stream.append((up_chunk(C_ATT + 2, s), wq[s]))
                if s >= 2:
                    stream.append((down_chunk(C_ATT + 2, s - 2, UNITS), wo[s - 2]))
            for s in range(5):
                stream.append((up_chunk(C_FFN, s), gu[s]))
                if s >= 2:
                    stream.append((down_chunk(C_FFN, s - 2, STEPS2), dn[s - 2]))
            for c, src in stream:
                ring_load(c, src)
            with sp.Fori(0, (STEPS2 - 5) // 4) as i:
                for t in range(4):
                    c = up_chunk(C_FFN, 5 + t)
                    ring_load(c, gu[bass.ds(i * 4 + 5 + t, 1)].rearrange("a p n -> p (a n)"),
                              free=i * 8 + (c - SLOTS + 1))
                    ring_load(c + 1, dn[bass.ds(i * 4 + 3 + t, 1)].rearrange("a p n -> p (a n)"),
                              free=i * 8 + (c - SLOTS + 2))
            for s in (STEPS2 - 2, STEPS2 - 1):
                ring_load(down_chunk(C_FFN, s, STEPS2), dn[s])
            sp.wait_ge(mid_ready, 5)
            sp.dma_start(out, mid[:]).then_inc(s_out, 16)
            sp.wait_ge(s_out, 16)

        @block.gpsimd
        def _(pool):
            nc.gpsimd.memset(ident[:], 0.0).then_inc(s_pool, 1)
            nc.gpsimd.memset(tri[:], 1.0).then_inc(s_pool, 1)
            nc.gpsimd.memset(later[:], 1.0).then_inc(s_pool, 1)
            nc.gpsimd.memset(amask[:], 0.0).then_inc(s_pool, 1)
            nc.gpsimd.memset(xpad[:], 0.0).then_inc(s_pool, 1)
            nc.gpsimd.memset(epsc[:, 0:1], LN_EPS).then_inc(s_pool, 1)
            nc.gpsimd.memset(epsc[:, 1:2], MIX_EPS).then_inc(s_pool, 1)
            nc.gpsimd.memset(cw[:, E2:E2 + 1], 1.0).then_inc(s_pool, 1)
            pool.wait_ge(s_pool, 8)

            def select(m, cmp, fill, base, pattern, mul):
                return nc.gpsimd.affine_select(out=m, in_=m, compare_op=cmp, fill=fill, base=base,
                                               pattern=pattern, channel_multiplier=mul)

            select(ident[:], ALU.not_equal, 1.0, 0, [[-1, P]], 1).then_inc(s_const, 1)
            select(later[:], ALU.is_gt, 0.0, 0, [[-1, P]], 1).then_inc(s_const, 1)
            select(tri[:], ALU.is_ge, 0.0, 0, [[1, P]], -1).then_inc(s_pool, 1)
            select(amask[:], ALU.is_ge, MASKED, 0, [[-1, P]], 1).then_inc(s_pool, 1)
            pool.wait_ge(s_pool, 10)
            select(tri[:, S:T], ALU.is_ge, 0.0, -S, [[0, S]], 1).then_inc(s_const, 1)
            select(amask[:, 0:S], ALU.is_ge, MASKED, S - 1, [[0, S]], -1).then_inc(s_const, 1)
            pool.wait_ge(s_const, 4)
            pool.wait_ge(M["dtA"], 1)
            nc.gpsimd.tensor_tensor(wdec[:], tri[:].rearrange("p (o t) -> p o t", o=1).to_broadcast([P, MH, T]),
                                    dts[:, 7, :].rearrange("p (h o) -> p h o", o=1).to_broadcast([P, MH, T]),
                                    ALU.mult).then_inc(M["wdec"], 1)

        @block.tensor
        def _(pe):
            mm = nc.tensor.matmul

            def transpose_norm(n, bank):
                pe.wait_ge(norm_ready, n)
                for k in range(KD):
                    i = nc.tensor.transpose(bank[:, k * P:(k + 1) * P], nrm[:, k * P:(k + 1) * P], ident[:])
                i.then_inc(nT_made, 1)

            def x_q(j):
                pe.wait_ge(L["qk"], j * 16 + 16)
                w = qk_sb[:, 0:KD * 256].rearrange("p (k n) -> p k n", k=KD)
                for k in range(KD):
                    i = mm(x_tr[0][:, 0:256], nT[:, k, :], w[:, k, :], start=(k == 0), stop=(k == KD - 1))
                i.then_inc(q_ready, 1)

            def x_qT(j):
                pe.wait_ge(q_copied, j + 1)
                for h in range(2):
                    i = nc.tensor.transpose(x_ma[:, h * P:(h + 1) * P], q_sb[:, h * P:(h + 1) * P], ident[:])
                i.then_inc(qT_ready, 1)

            def x_qproj(j):
                pe.wait_ge(qT_copied, j + 1)
                for kc in range(KC):
                    i = mm(x_qp[:, kc * 256:(kc + 1) * 256].rearrange("p (b h q) -> p b h q", b=B, h=2),
                           qk_sb[:, KD * 256 + kc * P:KD * 256 + (kc + 1) * P],
                           qT[:].rearrange("p (h b q) -> p b h q", b=B, h=2), start=True, stop=True)
                i.then_inc(qp_ready, 1)

            def x_score(j, b):
                for n in range(2):
                    for kc in range(KC):
                        i = mm(x_scores[b][:, n * 512:(n + 1) * 512], qp[:, kc, b, :], cT[:, b, kc, n * 512:(n + 1) * 512],
                               start=(kc == 0), stop=(kc == KC - 1))
                i.then_inc(sc_ready, 1)

            def x_probT(j, b):
                pe.wait_ge(exp_done, j * 2 + b + 1)
                if b or not isinstance(j, int) or j:
                    pe.wait_ge(pT_copied, j * 4 + 2 * b)
                for n in range(2):
                    for c in range(4):
                        s = n * 4 + c
                        i = nc.tensor.transpose(x_tr[n][:, c * P:(c + 1) * P], pr[:, b, s * P:(s + 1) * P], ident[:])
                    i.then_inc(pT_ready, 1)

            def x_mix(j, b):
                for s in range(SC):
                    if s % 4 == 0:
                        pe.wait_ge(pT_copied, j * 4 + 2 * b + 1 + s // 4)
                    i = mm(x_ctxo[b], pT[:, b, s, :], cx[:, b, s, :], start=(s == 0), stop=(s == SC - 1))
                i.then_inc(co_ready, 1)

            def x_coT(j, b):
                pe.wait_ge(co_copied, j * 2 + b + 1)
                dst = x_mb if b else x_ma
                for kc in range(KC):
                    i = nc.tensor.transpose(dst[:, kc * P:(kc + 1) * P], co[:, b, kc * P:(kc + 1) * P], ident[:])
                i.then_inc(coT_ready, 1)

            def x_value(j):
                pe.wait_ge(coT_copied, j * 2 + 2)
                pe.wait_ge(L["vo"], j * 16 + 16)
                for kc in range(KC):
                    i = mm(x_ma.rearrange("p (h b q) -> p h b q", h=2, b=B), vo_sb[:, kc * P:(kc + 1) * P],
                           coT[:, kc].rearrange("p b (h q) -> p h b q", h=2), start=(kc == 0), stop=(kc == KC - 1))
                i.then_inc(oT_ready, 1)

            def x_out(j, last=False):
                pe.wait_ge(oT_copied, j + 1)
                for h in range(2):
                    i = mm(ACC, oT[:, h, :], vo_sb[:, KC * P + h * D:KC * P + (h + 1) * D], start=False,
                           stop=last and h == 1, skip_group_check=True)
                i.then_inc(wo_done, 1)

            def x_head(j, prev, nxt):
                pe.wait_ge(qp_copied, j + 1)
                x_score(j, 0)
                if prev:
                    pe.wait_ge(coT_copied, j * 2 - 1)
                    x_coT(j - 1, 1)
                x_score(j, 1)
                if prev:
                    x_value(j - 1)
                if nxt:
                    x_q(j + 1)
                if prev:
                    x_out(j - 1)
                if nxt:
                    pe.wait_ge(q_copied, j + 2)
                x_probT(j, 0)
                if nxt:
                    x_qT(j + 1)
                if not prev:
                    pe.wait_ge(L["cx0"], 16)
                x_mix(j, 0)
                x_probT(j, 1)
                if nxt:
                    x_qproj(j + 1)
                if not prev:
                    pe.wait_ge(L["cx1"], 16)
                x_mix(j, 1)
                x_coT(j, 0)

            pe.wait_ge(s_const, 4)
            transpose_norm(1, PS[:, 1, :])
            mm(ACC, ident[:], xt[:], start=True, stop=False, skip_group_check=True)
            pe.wait_ge(nT_ready, 1)
            x_q(0)
            x_qT(0)
            x_qproj(0)
            pe.wait_ge(L["cT0"], 16)
            pe.wait_ge(L["cT1"], 16)
            x_head(0, False, True)
            with pe.Fori(1, XKV - 1) as j:
                x_head(j, True, True)
            x_head(XKV - 1, True, False)
            pe.wait_ge(coT_copied, XKV * 2 - 1)
            x_coT(XKV - 1, 1)
            x_value(XKV - 1)
            x_out(XKV - 1, last=True)

            transpose_norm(2, PS[:, 7, :])
            pe.wait_ge(nT_ready, 2)
            pe.wait_ge(L["vec"], 16)
            for k in range(KD):
                for n in range(4):
                    if n == 0:
                        wait_chunk(pe, C_IN + k, 0)
                    i = mm(PS[:, 1 + n, :], nT[:, k, :], ring[:, C_IN + k, n * 512:(n + 1) * 512],
                           start=(k == 0), stop=(k == KD - 1))
                i.then_inc(ring_used, 1)
                i = mm(PS[:, 5, 0:BCDT], nT[:, k, :], vec[:, V_BCDT + k * BCDT:V_BCDT + (k + 1) * BCDT],
                       start=(k == 0), stop=(k == KD - 1))
            i.then_inc(M["zx"], 1)
            pe.wait_ge(M["bc_sb"], 1)
            for n in range(2):
                i = nc.tensor.transpose(PS[0:DS, 5, 256 + n * P:256 + (n + 1) * P], bc_sb[:, n * DS:(n + 1) * DS], ident[:])
            i.then_inc(M["bcT"], 1)
            for n in range(2):
                pe.wait_ge(M["x_sb"], n + 1)
                for c in range(4):
                    f = n * 4 + c
                    i = nc.tensor.transpose(PS[:, 6 + n, c * P:(c + 1) * P], x_sb[:, f * P:(f + 1) * P], ident[:])
                i.then_inc(M["xT"], 1)
            pe.wait_ge(M["wdec"], 1)
            pe.wait_ge(M["zsig"], 1)
            pe.wait_ge(M["x_sb"], 2)
            for n in range(4):
                i = mm(PS[:, 1 + n, :], later[:], wdec[:, n * 4:(n + 1) * 4, :], start=True, stop=True)
                i.then_inc(M["dsum"], 1)
            pe.wait_ge(M["cact"], 1)
            mm(PS[:, 5, 0:P], cact[0:DS, XC, :], cact[0:DS, XC + 1, :], start=True, stop=True).then_inc(M["g"], 1)
            for n in range(2):
                for c in range(4):
                    i = nc.tensor.transpose(PS[:, 6 + n, c * P:(c + 1) * P], cact[:, n * 4 + c, :], ident[:])
                i.then_inc(M["xtok"], 1)
            pe.wait_ge(M["xdt"], 2)
            pe.wait_ge(M["mdec"], 1)
            for h in range(MH):
                i = mm(PS[:, 1 + h // 8, (h % 8) * HP:(h % 8 + 1) * HP], dec[:, h, :], xdt[:, h, :], start=True, stop=True)
                if h % 8 == 7:
                    i.then_inc(M["y"], 1)
            for n in range(2):
                pe.wait_ge(M["yg"], n + 1)
                for c in range(4):
                    f = n * 4 + c
                    i = nc.tensor.transpose(PS[:, 3 + n, c * P:(c + 1) * P], y_sb[:, f * P:(f + 1) * P], ident[:])
                i.then_inc(M["yT"], 1)
            for n in range(2):
                wait_chunk(pe, C_OUT + n, 0)
                pe.wait_ge(M["yTs"], n + 1)
                for c in range(4):
                    i = mm(PS[:, 5, :], yT[:, n * 4 + c, :], ring[:, C_OUT + n, c * D:(c + 1) * D],
                           start=(n == 0 and c == 0), stop=(n == 1 and c == 3))
                i.then_inc(ring_used, 1)

            transpose_norm(3, PS[:, 6, :])
            mm(ACC, ident[:], xt[:], start=True, stop=False, skip_group_check=True)
            pe.wait_ge(mid_ready, 2)
            mm(ACC, ident[:], mid[:], start=False, stop=False, skip_group_check=True)
            pe.wait_ge(nT_ready, 3)
            for k in range(KD):
                i = mm(PS[:, 7, 0:E1], nT[:, k, :], vec[:, V_GATE + k * E1:V_GATE + (k + 1) * E1],
                       start=(k == 0), stop=(k == KD - 1))
            i.then_inc(M["logit"], 1)

            def up(s, par, slot, lap):
                wait_chunk(pe, slot, lap)
                for k in range(KD):
                    i = mm(PS[:, 1 + par, :], nT[:, k, :], ring[:, slot, k * 512:(k + 1) * 512],
                           start=(k == 0), stop=(k == KD - 1))
                i.then_inc(ring_used, 1)

            def down(s, par, slot, lap, last=False):
                wait_chunk(pe, slot, lap)
                pe.wait_ge(hT_ready, s + 1)
                for c in range(4):
                    i = mm(ACC, hT[:, par, c, :], ring[:, slot, c * D:(c + 1) * D], start=False,
                           stop=last and c == 3, skip_group_check=True)
                i.then_inc(ring_used, 1)

            def turn(s, par):
                pe.wait_ge(act_ready, s + 1)
                for c in range(4):
                    i = nc.tensor.transpose(PS[:, 3 + par, c * P:(c + 1) * P], h_act[:, par, c * P:(c + 1) * P], ident[:])
                i.then_inc(hT_made, 1)

            def moe_step(s, t, i=0):
                cu, cd = up_chunk(C_W1, t), down_chunk(C_W1, t - 2, STEPS1)
                if t < STEPS1:
                    up(s, t % 2, cu % SLOTS, i + cu // SLOTS)
                if t >= 2:
                    down(s - 2, t % 2, cd % SLOTS, i + cd // SLOTS, last=(t == STEPS1 + 1))
                if 1 <= t <= STEPS1:
                    turn(s - 1, (t + 1) % 2)

            for s in range(4):
                moe_step(s, s)
            with pe.Fori(1, E1) as e:
                for t in range(4):
                    moe_step(e * 4 + t, 4 + t, e - 1)
            for s in (STEPS1, STEPS1 + 1):
                moe_step(s, s)

            transpose_norm(4, PS[:, 7, :])
            pe.wait_ge(mid_ready, 3)
            mm(ACC, ident[:], res[:], start=True, stop=False, skip_group_check=True)
            pe.wait_ge(nT_ready, 4)
            for n in range(2):
                c0 = C_ATT + n
                wait_chunk(pe, c0 % SLOTS, c0 // SLOTS)
                for k in range(KD):
                    i = mm(PS[:, 4 + n, :], nT[:, k, :], ring[:, c0 % SLOTS, k * 512:(k + 1) * 512],
                           start=(k == 0), stop=(k == KD - 1))
                i.then_inc(ring_used, 1)

            def a_q(u):
                c0 = up_chunk(C_ATT + 2, u)
                wait_chunk(pe, c0 % SLOTS, c0 // SLOTS)
                if u >= 2:
                    pe.wait_ge(A["ropes"], u)
                for k in range(KD):
                    i = mm(PS[:, 1 + u % 2, :], nT[:, k, :], ring[:, c0 % SLOTS, k * 512:(k + 1) * 512],
                           start=(k == 0), stop=(k == KD - 1))
                i.then_inc(ring_used, 1)

            def a_kT():
                pe.wait_ge(A["krope"], 1)
                for c in range(AKV):
                    i = nc.tensor.transpose(PS[:, 6, c * P:(c + 1) * P], rq[:, 1, c, :], ident[:])
                i.then_inc(A["kT"], 1)

            def a_qT(u):
                pe.wait_ge(A["rope"], u + 1)
                if u:
                    pe.wait_ge(A["qTs"], u)
                for c in range(4):
                    i = nc.tensor.transpose(PS[:, 3, c * P:(c + 1) * P], rq[:, u % 2, c, :], ident[:])
                i.then_inc(A["qT"], 1)

            def a_scores(u):
                pe.wait_ge(A["qTs"], u + 1)
                pe.wait_ge(A["kTs"], 1)
                if u < 2:
                    pe.wait_ge(A["v"], 1)
                for c in range(4):
                    i = mm(PS[:, 4 + u % 2, c * P:(c + 1) * P], aqT[:, u % 2, c, :], akT[:, u // 2, :], start=True, stop=True)
                i.then_inc(A["s"], 1)

            def a_probT(u):
                pe.wait_ge(A["pn"], u + 1)
                pe.wait_ge(A["kTs"], 1)
                if u:
                    pe.wait_ge(A["pTs"], u)
                for c in range(4):
                    i = nc.tensor.transpose(PS[:, 6, c * P:(c + 1) * P], apn[:, u % 2, c, :], ident[:])
                i.then_inc(A["pT"], 1)

            def a_value(u):
                pe.wait_ge(A["pTs"], u + 1)
                if u:
                    pe.wait_ge(A["os"], u)
                mm(PS[:, 7, :], av[:, u // 2, :], apT[:], start=True, stop=True).then_inc(A["o"], 1)

            def a_out(u):
                c0 = down_chunk(C_ATT + 2, u, UNITS)
                wait_chunk(pe, c0 % SLOTS, c0 // SLOTS)
                pe.wait_ge(A["os"], u + 1)
                for c in range(4):
                    i = mm(ACC, aoT[:, c, :], ring[:, c0 % SLOTS, c * D:(c + 1) * D], start=False,
                           stop=(u == UNITS - 1 and c == 3), skip_group_check=True)
                i.then_inc(ring_used, 1)

            for s in range(UNITS + 2):
                if s < UNITS:
                    a_q(s)
                if s == 0:
                    a_kT()
                if s >= 2:
                    a_probT(s - 2)
                if 1 <= s <= UNITS:
                    a_qT(s - 1)
                if s >= 2:
                    a_value(s - 2)
                if 1 <= s <= UNITS:
                    a_scores(s - 1)
                if s >= 2:
                    a_out(s - 2)

            transpose_norm(5, PS[:, 6, :])
            mm(ACC, ident[:], xt[:], start=True, stop=False, skip_group_check=True)
            pe.wait_ge(mid_ready, 4)
            mm(ACC, ident[:], mid[:], start=False, stop=False, skip_group_check=True)
            pe.wait_ge(nT_ready, 5)
            for k in range(KD):
                i = mm(PS[:, 7, 0:E2], nT[:, k, :], vec[:, V_ROUTE + k * E2:V_ROUTE + (k + 1) * E2],
                       start=(k == 0), stop=(k == KD - 1))
            i.then_inc(A["logit"], 1)

            def ffn_step(s, t, i=0):
                if t < STEPS2:
                    c = up_chunk(C_FFN, t)
                    wait_chunk(pe, c % SLOTS, i + c // SLOTS)
                    for k in range(KD):
                        x_ = mm(PS[:, 1 + t % 2, :], nT[:, k, :], ring[:, c % SLOTS, k * 512:(k + 1) * 512],
                                start=(k == 0), stop=(k == KD - 1))
                    x_.then_inc(ring_used, 1)
                if t >= 2:
                    c = down_chunk(C_FFN, t - 2, STEPS2)
                    wait_chunk(pe, c % SLOTS, i + c // SLOTS)
                    pe.wait_ge(aT_ready, s - 1)
                    for n in range(2):
                        x_ = mm(ACC, hT[:, t % 2, n, :], ring[:, c % SLOTS, n * D:(n + 1) * D], start=False,
                                stop=(t == STEPS2 + 1 and n == 1), skip_group_check=True)
                    x_.then_inc(ring_used, 1)
                if 1 <= t <= STEPS2:
                    pe.wait_ge(a_ready, s)
                    for n in range(2):
                        x_ = nc.tensor.transpose(PS[:, 3 + (t + 1) % 2, n * P:(n + 1) * P],
                                                 h_act[:, (t + 1) % 2, n * P:(n + 1) * P], ident[:])
                    x_.then_inc(aT_made, 1)

            for s in range(5):
                ffn_step(s, s)
            with pe.Fori(0, (STEPS2 - 5) // 4) as i:
                for t in range(4):
                    ffn_step(i * 4 + 5 + t, 5 + t, i)
            for s in (STEPS2, STEPS2 + 1):
                ffn_step(s, s)

        @block.scalar
        def _(act):
            steps = [0]
            act_fn = nc.scalar.activation

            def settled(ins):
                steps[0] += 1
                ins.then_inc(s_act, 1)
                act.wait_ge(s_act, steps[0])

            def rstd(n, col, scale, eps):
                act.wait_ge(var_ready, n)
                settled(act_fn(st[:, 6:7], st[:, col:col + 1], ACT.Ln, bias=epsc[:, eps:eps + 1], scale=scale))
                act_fn(st[:, col + 1:col + 2], st[:, 6:7], ACT.Exp, scale=-0.5).then_inc(rstd_ready, 1)

            act.wait_ge(s_const, 4)
            rstd(1, 0, 1.0, 0)
            XS = float(XD) ** -0.5

            def x_exp(j, b):
                act.wait_ge(nb_ready, j * 2 + b + 1)
                act_fn(pr[:, b, :], sc_sb[:, b, :], ACT.Exp, bias=nbias[:, b:b + 1], scale=XS,
                       accum_out=xsum[:, b:b + 1]).then_inc(exp_done, 1)

            def x_copies(j, what):
                if what == 0:
                    act.wait_ge(q_ready, j + 1)
                    nc.scalar.copy(q_sb[:], x_tr[0][:, 0:256]).then_inc(q_copied, 1)
                if what == 1:
                    act.wait_ge(qT_ready, j + 1)
                    nc.scalar.copy(qT[:], x_ma).then_inc(qT_copied, 1)
                if what == 2:
                    act.wait_ge(qp_ready, j + 1)
                    nc.scalar.copy(qp[:].rearrange("p a b q -> p (a b q)"), x_qp).then_inc(qp_copied, 1)

            for w in range(3):
                x_copies(0, w)

            def x_head(j, nxt):
                x_exp(j, 0)
                if nxt:
                    x_copies(j + 1, 0)
                x_exp(j, 1)
                if nxt:
                    x_copies(j + 1, 1)
                    x_copies(j + 1, 2)

            x_head(0, True)
            with act.Fori(1, XKV - 1) as j:
                x_head(j, True)
            x_head(XKV - 1, False)

            rstd(2, 0, 1.0, 0)
            rstd(3, 2, 1.0 / D, 1)
            act.wait_ge(L["row"], 16)
            act.wait_ge(M["expA"], 1)
            act_fn(dts[:, 0, :], dts[:, 0, :], ACT.Exp).then_inc(M["A"], 1)
            act.wait_ge(M["zx"], 1)
            for n in range(2):
                nc.scalar.copy(x_sb[:, n * 512:(n + 1) * 512], PS[:, 3 + n, :]).then_inc(M["x_sb"], 1)
            act.wait_ge(M["abs"], 1)
            act_fn(dts[:, 3, :], dts[:, 2, :], ACT.Exp, scale=-1.0).then_inc(M["expd"], 1)
            act.wait_ge(M["u"], 1)
            act_fn(dts[:, 5, :], dts[:, 4, :], ACT.Ln).then_inc(M["lnu"], 1)
            act_fn(zs[:], PS[:, 1:3, :].rearrange("p a n -> p (a n)"), ACT.Sigmoid).then_inc(M["zraw"], 1)
            act.wait_ge(M["conv"], 1)
            act_fn(csig[:], cacc[:], ACT.Sigmoid).then_inc(M["csig"], 1)
            for n in range(4):
                act.wait_ge(M["dsum"], n + 1)
                act_fn(dec[:, n * 4:(n + 1) * 4, :], PS[:, 1 + n, :].rearrange("p (h t) -> p h t", h=4),
                       ACT.Exp).then_inc(M["decay"], 1)
            rstd(4, 4, 1.0 / DI, 1)
            rstd(5, 2, 1.0 / D, 1)
            act.wait_ge(M["rexp"], 1)
            act_fn(r8[:, 8:16], rsc[:, 1, 0:8], ACT.Exp).then_inc(M["rexp"], 1)

            def hidden_sigmoid(s, par):
                act.wait_ge(ring_used, up_chunk(C_W1, s) + 1)
                act_fn(h_sig[:, par, :], PS[:, 1 + par, :], ACT.Sigmoid).then_inc(sig_ready, 1)

            for s in range(4):
                hidden_sigmoid(s, s % 2)
            with act.Fori(1, E1) as e:
                for t in range(4):
                    hidden_sigmoid(e * 4 + t, t % 2)

            rstd(6, 0, 1.0, 0)
            rstd(7, 2, 1.0 / D, 0)
            act.wait_ge(ring_used, C_ATT + 2)
            nc.scalar.copy(av[:].rearrange("p g d -> p (g d)"), PS[:, 5, :]).then_inc(A["v"], 1)
            AS = float(AD) ** -0.5

            def a_exp(u):
                act.wait_ge(A["nb"], u + 1)
                for c in range(4):
                    i = act_fn(apr[:, u % 2, c, :], asc[:, u % 2, c, :], ACT.Exp, bias=anb[:, u % 2, c:c + 1], scale=AS,
                               accum_out=asm[:, u % 2, c:c + 1])
                i.then_inc(A["exp"], 1)

            def a_copy_T(u):
                act.wait_ge(A["qT"], u + 1)
                nc.scalar.copy(aqT[:, u % 2].rearrange("p h t -> p (h t)"), PS[:, 3, :]).then_inc(A["qTs"], 1)

            def a_copy_o(u):
                act.wait_ge(A["o"], u + 1)
                nc.scalar.copy(aoT[:].rearrange("p h t -> p (h t)"), PS[:, 7, :]).then_inc(A["os"], 1)

            for s in range(UNITS + 2):
                if 1 <= s <= UNITS:
                    a_copy_T(s - 1)
                if s >= 2:
                    a_copy_o(s - 2)
                if 1 <= s <= UNITS:
                    a_exp(s - 1)
            rstd(8, 2, 1.0 / D, 0)

            act.wait_ge(A["logit"], 1)
            act_fn(rsc[:, 0, :], PS[:, 7, 0:E2], ACT.Sigmoid).then_inc(A["rsig"], 1)

            def gate_sigmoid(s, par):
                act.wait_ge(ring_used, up_chunk(C_FFN, s) + 1)
                act_fn(h_sig[:, par, 0:FF2], PS[:, 1 + par, 0:FF2], ACT.Sigmoid).then_inc(gsig_ready, 1)

            for s in range(5):
                gate_sigmoid(s, s % 2)
            with act.Fori(0, (STEPS2 - 5) // 4) as i:
                for t in range(4):
                    gate_sigmoid(i * 4 + 5 + t, (5 + t) % 2)

        @block.vector
        def _(dve):
            V = nc.vector
            steps = [0]

            def settled(ins):
                steps[0] += 1
                ins.then_inc(s_dve, 1)
                dve.wait_ge(s_dve, steps[0])

            def layer_norm(n, rn, dst, done):
                settled(V.bn_stats(bnst[:], xt[:]))
                settled(V.bn_aggr(mv[:], bnst[:]))
                V.tensor_copy(st[:, 0:1], mv[:, 1:2]).then_inc(var_ready, 1)
                dve.wait_ge(rstd_ready, rn)
                V.tensor_scalar(dst, xt[:], mv[:, 0:1], st[:, 1:2], ALU.subtract, ALU.mult).then_inc(done[0], 1)
                dve.wait_ge(*done)

            def rms_norm(src, rn, norm_n):
                V.tensor_tensor_reduce(out=junk[:], in0=src, in1=src, scale=1.0, scalar=0.0, op0=ALU.mult, op1=ALU.add,
                                       accum_out=st[:, 2:3]).then_inc(var_ready, 1)
                dve.wait_ge(rstd_ready, rn)
                V.tensor_scalar(nrm[:], src, st[:, 3:4], None, ALU.mult).then_inc(norm_ready, 1)

            def copy_nT(n, bank, v):
                dve.wait_ge(nT_made, n)
                src = bank.rearrange("p (k t) -> p k t", k=KD)
                if v is None:
                    V.tensor_copy(nT[:], src).then_inc(nT_ready, 1)
                else:
                    V.tensor_tensor(nT[:], src, vec[:, v:v + KD].rearrange("p (k o) -> p k o", o=1).to_broadcast([P, KD, T]),
                                    ALU.mult).then_inc(nT_ready, 1)

            dve.wait_ge(L["x"], 16)
            layer_norm(1, 1, nrm[:], (norm_ready, 1))
            copy_nT(1, PS[:, 1, :], None)
            dve.wait_ge(L["mask"], 16)
            settled(V.tensor_scalar(madd[:], mask8[:], -MASKED, MASKED, ALU.mult, ALU.add))
            XS = float(XD) ** -0.5

            def x_max(j, b):
                dve.wait_ge(sc_ready, j * 2 + b + 1)
                V.memset(held[:], 0.0)
                V.tensor_tensor_reduce(out=sc_sb[:, b, :], in0=x_scores[b], in1=madd[:, b, :], scale=1.0, scalar=2 * MASKED,
                                       op0=ALU.add, op1=ALU.max, accum_out=xmax[:, b:b + 1]).then_inc(s_max, 1)
                dve.wait_ge(s_max, j * 2 + b + 1)
                V.tensor_scalar(nbias[:, b:b + 1], xmax[:, b:b + 1], -XS, None, ALU.mult).then_inc(nb_ready, 1)

            def x_recip(j, b):
                dve.wait_ge(exp_done, j * 2 + b + 1)
                V.reciprocal(xrec[:, b:b + 1], xsum[:, b:b + 1]).then_inc(x_dve, 1)
                V.tensor_scalar(xval[:, b:b + 1], xmax[:, b:b + 1], MASKED / 2, None, ALU.is_gt).then_inc(x_dve, 1)

            def x_pT(j, b):
                for n in range(2):
                    dve.wait_ge(pT_ready, j * 4 + 2 * b + n + 1)
                    V.tensor_copy(pT[:, b, n * 4:(n + 1) * 4, :].rearrange("p c q -> p (c q)"), x_tr[n]).then_inc(pT_copied, 1)

            def x_co(j, b):
                dve.wait_ge(co_ready, j * 2 + b + 1)
                dve.wait_ge(x_dve, j * 4 + 2 * b + 2)
                V.tensor_scalar(co[:, b, :], x_ctxo[b], xrec[:, b:b + 1], xval[:, b:b + 1], ALU.mult,
                                ALU.mult).then_inc(co_copied, 1)

            def x_coT(j, b):
                dve.wait_ge(coT_ready, j * 2 + b + 1)
                V.tensor_copy(coT[:, :, b, :], (x_mb if b else x_ma).rearrange("p (k q) -> p k q", k=KC)).then_inc(coT_copied, 1)

            def x_oT(j):
                dve.wait_ge(oT_ready, j + 1)
                if not isinstance(j, int) or j:
                    dve.wait_ge(wo_done, j)
                V.tensor_copy(oT[:].rearrange("p h t -> p (h t)"), x_ma).then_inc(oT_copied, 1)

            def x_head(j, prev):
                x_max(j, 0)
                if prev:
                    x_coT(j - 1, 1)
                x_max(j, 1)
                if prev:
                    if prev == 1:
                        x_oT(0)
                    else:
                        x_oT(j - 1)
                x_recip(j, 0)
                x_pT(j, 0)
                x_recip(j, 1)
                x_pT(j, 1)
                x_co(j, 0)
                x_co(j, 1)
                x_coT(j, 0)

            x_head(0, 0)
            x_head(1, 1)
            with dve.Fori(2, XKV) as j:
                x_head(j, 2)
            x_coT(XKV - 1, 1)
            x_oT(XKV - 1)

            dve.wait_ge(wo_done, XKV)
            settled(V.tensor_copy(xt[:], ACC))
            layer_norm(2, 2, res[:], (mid_ready, 1))
            rms_norm(res[:], 3, 2)
            dve.wait_ge(L["vec"], 16)
            copy_nT(2, PS[:, 7, :], V_MIX)
            dve.wait_ge(L["row"], 16)
            V.tensor_scalar(dts[:, 0, :], row[:, R_A:R_A + MH], A_LOG_TOP, None, ALU.min).then_inc(M["expA"], 1)
            dve.wait_ge(M["zx"], 1)
            V.tensor_copy(bc_sb[:], PS[:, 5, 0:BCDT]).then_inc(M["bc_sb"], 1)
            dve.wait_ge(M["bc_sb"], 1)
            settled(V.tensor_tensor(dts[:, 1, :], bc_sb[:, 2 * DS:BCDT], row[:, R_DT:R_DT + MH], ALU.add))
            settled(V.tensor_scalar(dts[:, 2, :], dts[:, 1, :], -1.0, None, ALU.mult))
            V.tensor_tensor(dts[:, 2, :], dts[:, 1, :], dts[:, 2, :], ALU.max).then_inc(M["abs"], 1)
            dve.wait_ge(M["expd"], 1)
            V.tensor_scalar(dts[:, 4, :], dts[:, 3, :], 1.0, None, ALU.add).then_inc(M["u"], 1)
            dve.wait_ge(M["u"], 1)
            settled(V.tensor_scalar(dts[:, 6, :], dts[:, 4, :], -1.0, None, ALU.add))
            settled(V.tensor_scalar(dts[:, 2, :], dts[:, 6, :], 0.0, None, ALU.is_equal))
            settled(V.tensor_tensor(dts[:, 6, :], dts[:, 6, :], dts[:, 2, :], ALU.add))
            settled(V.reciprocal(dts[:, 6, :], dts[:, 6, :]))
            dve.wait_ge(M["lnu"], 1)
            dve.wait_ge(M["A"], 1)
            settled(V.tensor_tensor(dts[:, 5, :], dts[:, 5, :], dts[:, 2, :], ALU.add))
            settled(V.tensor_tensor(dts[:, 5, :], dts[:, 5, :], dts[:, 6, :], ALU.mult))
            settled(V.tensor_tensor(dts[:, 5, :], dts[:, 5, :], dts[:, 3, :], ALU.mult))
            settled(V.scalar_tensor_tensor(out=dts[:, 1, :], in0=dts[:, 1, :], scalar=0.0, in1=dts[:, 5, :], op0=ALU.max,
                                           op1=ALU.add))
            settled(V.tensor_tensor(dts[:, 7, :], dts[:, 1, :], dts[:, 0, :], ALU.mult))
            V.tensor_scalar(dts[:, 7, :], dts[:, 7, :], -1.0, DECAY_BOTTOM, ALU.mult, ALU.max).then_inc(M["dtA"], 1)
            dve.wait_ge(M["zraw"], 1)
            V.tensor_tensor(zs[:], zs[:], PS[:, 1:3, :].rearrange("p a n -> p (a n)"), ALU.mult).then_inc(M["zsig"], 1)
            dve.wait_ge(s_const, 4)
            dve.wait_ge(M["bcT"], 1)
            settled(V.tensor_copy(xpad[0:DS, XC:CC, :, TAPS - 1:PAD],
                                  PS[0:DS, 5, 256:512].rearrange("p (c b t) -> p c b t", c=2, b=B)))
            for n in range(2):
                dve.wait_ge(M["xT"], n + 1)
                settled(V.tensor_copy(xpad[:, n * 4:(n + 1) * 4, :, TAPS - 1:PAD],
                                      PS[:, 6 + n, :].rearrange("p (c b t) -> p c b t", c=4, b=B)))
            for c in range(CC):
                M_ = P if c < XC else DS
                cc = cacc[0:M_, c, :].rearrange("p (b t) -> p b t", b=B)
                i = V.tensor_scalar(cc, xpad[0:M_, c, :, 0:S], vec[0:M_, V_TAP + c * TAPS:V_TAP + c * TAPS + 1],
                                    vec[0:M_, V_CB + c:V_CB + c + 1], ALU.mult, ALU.add)
            i = V.memset(cacc[DS:P, XC:CC, :], 0.0)
            settled(i)
            for k in range(1, TAPS):
                for c in range(CC):
                    M_ = P if c < XC else DS
                    cc = cacc[0:M_, c, :].rearrange("p (b t) -> p b t", b=B)
                    i = V.scalar_tensor_tensor(out=cc, in0=xpad[0:M_, c, :, k:k + S],
                                               scalar=vec[0:M_, V_TAP + c * TAPS + k:V_TAP + c * TAPS + k + 1], in1=cc,
                                               op0=ALU.mult, op1=ALU.add)
                if k < TAPS - 1:
                    settled(i)
            i.then_inc(M["conv"], 1)
            dve.wait_ge(M["csig"], 1)
            V.tensor_tensor(cact[:], cacc[:], csig[:], ALU.mult).then_inc(M["cact"], 1)
            dve.wait_ge(M["g"], 1)
            V.tensor_tensor(gm[:], PS[:, 5, 0:P], tri[:], ALU.mult).then_inc(M["gm"], 1)
            for n in range(2):
                dve.wait_ge(M["xtok"], n + 1)
                src = PS[:, 6 + n, :].rearrange("p (h d) -> p h d", h=8)
                for dst, w, s_ in ((xdt, dts[:, 1, n * 8:(n + 1) * 8], M["xdt"]), (xD_, row[:, R_D + n * 8:R_D + (n + 1) * 8], None)):
                    i = V.tensor_tensor(dst[:, n * 8:(n + 1) * 8, :], src,
                                        w.rearrange("p (h o) -> p h o", o=1).to_broadcast([P, 8, HP]), ALU.mult)
                    i.then_inc(s_ or s_dve, 1)
                steps[0] += 1
            dve.wait_ge(M["gm"], 1)
            dve.wait_ge(M["decay"], 4)
            V.tensor_tensor(dec[:], dec[:], gm[:].rearrange("p (o t) -> p o t", o=1).to_broadcast([P, MH, T]),
                            ALU.mult).then_inc(M["mdec"], 1)
            for n in range(2):
                dve.wait_ge(M["y"], n + 1)
                h = slice(n * 512, (n + 1) * 512)
                settled(V.tensor_tensor(y_sb[:, h], PS[:, 1 + n, :], xD_[:, n * 8:(n + 1) * 8, :].rearrange("p h d -> p (h d)"),
                                        ALU.add))
                V.tensor_tensor(y_sb[:, h], y_sb[:, h], zs[:, h], ALU.mult).then_inc(M["yg"], 1)
            dve.wait_ge(M["yg"], 2)
            V.tensor_tensor_reduce(out=ysq[:], in0=y_sb[:], in1=y_sb[:], scale=1.0, scalar=0.0, op0=ALU.mult, op1=ALU.add,
                                   accum_out=st[:, 4:5]).then_inc(var_ready, 1)
            for n in range(2):
                dve.wait_ge(M["yT"], n + 1)
                V.tensor_tensor(yT[:, n * 4:(n + 1) * 4, :], PS[:, 3 + n, :].rearrange("p (c t) -> p c t", c=4),
                                vec[:, V_SSM + n * 4:V_SSM + (n + 1) * 4].rearrange("p (c o) -> p c o", o=1).to_broadcast([P, 4, T]),
                                ALU.mult).then_inc(M["yTs"], 1)
            dve.wait_ge(rstd_ready, 4)
            dve.wait_ge(ring_used, C_OUT + 2)
            V.scalar_tensor_tensor(out=mid[:], in0=PS[:, 5, :], scalar=st[:, 5:6], in1=res[:], op0=ALU.mult,
                                   op1=ALU.add).then_inc(mid_ready, 1)
            dve.wait_ge(mid_ready, 2)
            rms_norm(mid[:], 5, 3)
            copy_nT(3, PS[:, 6, :], V_MOE)

            dve.wait_ge(M["logit"], 1)
            settled(V.memset(rsc[:, 0, :], MASKED))
            settled(V.tensor_copy(rsc[:, 0, 0:E1], PS[:, 7, 0:E1]))
            settled(V.max(r8[:, 0:8], rsc[:, 0, 0:E1]))
            V.tensor_scalar(rsc[:, 1, 0:E1], rsc[:, 0, 0:E1], r8[:, 0:1], None, ALU.subtract).then_inc(M["rexp"], 1)
            settled(V.memset(r8[:, 2:8], MASKED))
            settled(V.match_replace(rsc[:, 2, 0:16], r8[:, 0:8], rsc[:, 0, 0:16], 2 * MASKED))
            settled(V.tensor_tensor(rsc[:, 3, 0:E1], rsc[:, 2, 0:E1], rsc[:, 0, 0:E1], ALU.is_lt))
            dve.wait_ge(M["rexp"], 2)
            settled(V.tensor_tensor_reduce(out=rsc[:, 1, 0:E1], in0=r8[:, 8:16], in1=rsc[:, 3, 0:E1], scale=1.0, scalar=0.0,
                                           op0=ALU.mult, op1=ALU.add, accum_out=st[:, 7:8]))
            settled(V.reciprocal(st[:, 7:8], st[:, 7:8]))
            settled(V.tensor_scalar(cw[:, 0:E1], rsc[:, 1, 0:E1], st[:, 7:8], None, ALU.mult))

            def hidden(s, par, w):
                dve.wait_ge(sig_ready, s + 1)
                V.scalar_tensor_tensor(out=h_act[:, par, :], in0=PS[:, 1 + par, :], scalar=w, in1=h_sig[:, par, :],
                                       op0=ALU.mult, op1=ALU.mult).then_inc(act_ready, 1)

            def hidden_T(s, par):
                dve.wait_ge(hT_made, s + 1)
                V.tensor_copy(hT[:, par].rearrange("p c t -> p (c t)"), PS[:, 3 + par, :]).then_inc(hT_ready, 1)

            for s in range(4):
                hidden(s, s % 2, cw[:, 0:1])
                if s:
                    hidden_T(s - 1, (s + 1) % 2)
            with dve.Fori(1, E1) as e:
                for t in range(4):
                    hidden(e * 4 + t, t % 2, cw[:, bass.ds(e, 1)])
                    hidden_T(e * 4 + (t - 1), (t + 1) % 2)
            hidden_T(STEPS1 - 1, (STEPS1 - 1) % 2)

            dve.wait_ge(ring_used, C_ATT)
            settled(V.tensor_copy(xt[:], ACC))
            layer_norm(3, 6, res[:], (mid_ready, 3))
            rms_norm(res[:], 7, 4)
            copy_nT(4, PS[:, 7, :], V_LN1)
            dve.wait_ge(L["rope"], 16)

            def rotate(bank, par, read, done, n):
                src = bank.rearrange("p (h d) -> p h d", h=4)
                half = AD // 2

                def bc(a):
                    return a.rearrange("p (o d) -> p o d", o=1).to_broadcast([P, 4, a.shape[-1]])

                V.tensor_tensor(ra[:, par], src, bc(rp[:, 0, :]), ALU.mult)
                V.tensor_tensor(rb[:, par, :, 0:half], src[:, :, half:AD], bc(rp[:, 1, 0:half]), ALU.mult)
                V.tensor_tensor(rb[:, par, :, half:AD], src[:, :, 0:half], bc(rp[:, 1, half:AD]), ALU.mult).then_inc(read, 1)
                dve.wait_ge(read, n)
                V.tensor_tensor(rq[:, par], ra[:, par], rb[:, par], ALU.add).then_inc(done, 1)

            def a_rope(u):
                dve.wait_ge(ring_used, up_chunk(C_ATT + 2, u) + 1)
                if u == 1:
                    dve.wait_ge(A["kT"], 1)
                rotate(PS[:, 1 + u % 2, :], u % 2, A["ropes"], A["rope"], u + 1)

            def a_max(u):
                dve.wait_ge(A["s"], u + 1)
                for c in range(4):
                    i = V.tensor_tensor_reduce(out=asc[:, u % 2, c, :], in0=PS[:, 4 + u % 2, c * P:(c + 1) * P], in1=amask[:],
                                               scale=1.0, scalar=2 * MASKED, op0=ALU.add, op1=ALU.max,
                                               accum_out=amx[:, u % 2, c:c + 1])
                i.then_inc(A["max"], 1)
                dve.wait_ge(A["max"], u + 1)
                V.tensor_scalar(anb[:, u % 2, :], amx[:, u % 2, :], -(float(AD) ** -0.5), None, ALU.mult).then_inc(A["nb"], 1)

            def a_normalise(u):
                dve.wait_ge(A["exp"], u + 1)
                V.reciprocal(arc[:, u % 2, :], asm[:, u % 2, :]).then_inc(A["rec"], 1)
                dve.wait_ge(A["rec"], u + 1)
                V.tensor_tensor(apn[:, u % 2], apr[:, u % 2],
                                arc[:, u % 2, :].rearrange("p (h o) -> p h o", o=1).to_broadcast([P, 4, T]),
                                ALU.mult).then_inc(A["pn"], 1)

            def a_copy_pT(u):
                dve.wait_ge(A["pT"], u + 1)
                if u:
                    dve.wait_ge(A["o"], u)
                V.tensor_copy(apT[:].rearrange("p h t -> p (h t)"), PS[:, 6, :]).then_inc(A["pTs"], 1)

            dve.wait_ge(ring_used, C_ATT + 1)
            rotate(PS[:, 4, :], 1, A["kv"], A["krope"], 1)
            for s in range(UNITS + 2):
                if s == 0:
                    dve.wait_ge(A["kT"], 1)
                    V.tensor_copy(akT[:].rearrange("p g t -> p (g t)"), PS[:, 6, :]).then_inc(A["kTs"], 1)
                if s < UNITS:
                    a_rope(s)
                if s >= 2:
                    a_copy_pT(s - 2)
                if 1 <= s <= UNITS:
                    a_max(s - 1)
                    a_normalise(s - 1)

            dve.wait_ge(ring_used, C_FFN)
            V.tensor_copy(mid[:], ACC).then_inc(mid_ready, 1)
            dve.wait_ge(mid_ready, 4)
            rms_norm(mid[:], 8, 5)
            copy_nT(5, PS[:, 6, :], V_LN2)

            dve.wait_ge(A["rsig"], 1)
            settled(V.tensor_tensor(rsc[:, 1, :], rsc[:, 0, :], row[:, R_EB:R_EB + E2], ALU.add))
            settled(V.max(r8[:, 0:8], rsc[:, 1, :]))
            settled(V.match_replace(rsc[:, 2, :], r8[:, 0:8], rsc[:, 1, :], 2 * MASKED))
            settled(V.tensor_tensor(rsc[:, 3, :], rsc[:, 2, :], rsc[:, 1, :], ALU.is_lt))
            settled(V.tensor_tensor_reduce(out=rsc[:, 1, :], in0=rsc[:, 0, :], in1=rsc[:, 3, :], scale=1.0, scalar=0.0,
                                           op0=ALU.mult, op1=ALU.add, accum_out=st[:, 7:8]))
            settled(V.reciprocal(st[:, 7:8], st[:, 7:8]))
            settled(V.tensor_scalar(cw[:, 0:E2], rsc[:, 1, :], st[:, 7:8], None, ALU.mult))

            def gated(s, par, w):
                dve.wait_ge(gsig_ready, s + 1)
                V.scalar_tensor_tensor(out=h_sig[:, par, FF2:2 * FF2], in0=PS[:, 1 + par, 0:FF2], scalar=w,
                                       in1=h_sig[:, par, 0:FF2], op0=ALU.mult, op1=ALU.mult).then_inc(gs_ready, 1)
                dve.wait_ge(gs_ready, s + 1)
                V.tensor_tensor(h_act[:, par, 0:FF2], PS[:, 1 + par, FF2:2 * FF2], h_sig[:, par, FF2:2 * FF2],
                                ALU.mult).then_inc(a_ready, 1)

            def gated_T(s, par):
                dve.wait_ge(aT_made, s + 1)
                V.tensor_copy(hT[:, par, 0:2].rearrange("p c t -> p (c t)"), PS[:, 3 + par, 0:2 * P]).then_inc(aT_ready, 1)

            for s in range(5):
                gated(s, s % 2, cw[:, s:s + 1])
                if s:
                    gated_T(s - 1, (s + 1) % 2)
            with dve.Fori(0, (STEPS2 - 5) // 4) as i:
                for t in range(4):
                    gated(i * 4 + 5 + t, (5 + t) % 2, cw[:, bass.ds(i * 4 + 5 + t, 1)])
                    gated_T(i * 4 + 4 + t, t % 2)
            gated_T(STEPS2 - 1, (STEPS2 - 1) % 2)
            dve.wait_ge(ring_used, CHUNKS)
            V.tensor_copy(mid[:], ACC).then_inc(mid_ready, 1)


def kernel(**inputs):
    import numpy as np
    import concourse.bacc as bacc
    from concourse import mybir as mb
    from concourse.bass_utils import run_bass_kernel_spmd

    a = {k: np.asarray(v) for k, v in inputs.items()}
    m, f, xa = "L0_attn_", "L0_ffn_", "L0_xattn_"

    def pieces(w, n):
        k, cols = w.shape
        return w.reshape(k // P, P, cols // n, n).transpose(2, 1, 0, 3).reshape(cols // n, P, -1)

    def rows_of(w, n):
        k, cols = w.shape
        return w.reshape(k // (P * n), n, P, cols).transpose(0, 2, 1, 3).reshape(k // (P * n), P, n * cols)

    def column(v):
        return v.reshape(-1, P).T

    ctx = a["ctx_1024"]
    wk = a[xa + "Wk"].reshape(DC, XKV, XD).transpose(1, 2, 0)
    qk = np.concatenate([pieces(a[xa + "Wq"], 256), wk], axis=2)
    vo = np.concatenate([pieces(a[xa + "Wv"], XD), rows_of(a[xa + "Wo"], 2)], axis=2)
    ipw = a[m + "in_proj_w"].T

    def conv_pieces(v):
        n = v.shape[1]
        t = np.zeros((P, CC, n), np.float32)
        t[:, :XC] = v[:DI].reshape(XC, P, n).transpose(1, 0, 2)
        t[:DS, XC] = v[DI:DI + DS]
        t[:DS, XC + 1] = v[DI + DS:]
        return t.reshape(P, CC * n)

    vecs = np.concatenate([
        column(a[m + "norm_mamba_w"]), column(a[m + "norm_moe_w"]), column(a[m + "ssm_norm_w"]),
        column(a[f + "ln1_w"]), column(a[f + "ln2_w"]),
        conv_pieces(a[m + "conv_w"]), conv_pieces(a[m + "conv_b"][:, None]),
        pieces(a[m + "gate_w"].T, E1)[0], pieces(a[f + "Wr"], E2)[0],
        pieces(ipw[:, 2 * DI:], BCDT)[0]], axis=1)
    rows = np.concatenate([a[m + "dt_bias"], a[m + "A_log"], a[m + "D"], a[f + "expert_bias"]])[None]
    inv = (1.0 / 10000.0 ** (np.arange(0, AD, 2, dtype=np.float32) / AD)).astype(np.float32)
    ang = (np.arange(S, dtype=np.float32)[:, None] * inv[None]).astype(np.float32)
    ang = np.concatenate([ang, ang])
    rope = np.stack([np.concatenate([np.cos(ang), np.cos(ang)], 1), np.concatenate([-np.sin(ang), np.sin(ang)], 1)], 1)

    w1 = a[m + "w1"].reshape(E1, N1, 512, KD, P).transpose(0, 1, 4, 3, 2).reshape(STEPS1, P, CHUNK)
    w2 = a[m + "w2"].reshape(E1, D, N1, 4, P).transpose(0, 2, 4, 3, 1).reshape(STEPS1, P, CHUNK)
    g = np.concatenate([a[f + "Wg"], a[f + "Wsg"][None]]).reshape(STEPS2, KD, P, FF2)
    u = np.concatenate([a[f + "Wu"], a[f + "Wsu"][None]]).reshape(STEPS2, KD, P, FF2)
    gu = np.stack([g, u], axis=3).transpose(0, 2, 1, 3, 4).reshape(STEPS2, P, CHUNK)
    dn = np.concatenate([a[f + "Wd"], a[f + "Wsd"][None]]).reshape(STEPS2, 2, P, D).transpose(0, 2, 1, 3).reshape(STEPS2, P, 2 * D)
    arrays = {
        "x": a["x"].reshape(T, D),
        "mask": a["mask_BxS2_bf1"].reshape(1, B * S2).view(np.uint8),
        "ctx": ctx.reshape(B, SC, P, DC).transpose(2, 0, 1, 3),
        "ctxT": ctx.transpose(0, 2, 1).reshape(B, KC, P, S2).transpose(2, 0, 1, 3),
        "qk": qk, "vo": vo, "vecs": vecs, "rows": rows, "rope": rope,
        "in_w": ipw[:, :2 * DI].reshape(KD, P, 2 * DI),
        "out_w": rows_of(a[m + "out_proj_w"].T, 4),
        "w1": w1, "w2": w2,
        "wkv": np.concatenate([pieces(a[f + "Wk"], 512), pieces(a[f + "Wv"], 512)]),
        "wq": pieces(a[f + "Wq"], 512), "wo": rows_of(a[f + "Wo"], 4),
        "gu": gu, "dn": dn,
    }
    arrays = {"in_" + k: np.ascontiguousarray(v) for k, v in arrays.items()}
    nc = bacc.Bacc("TRN2", target_bir_lowering=False, num_devices=1)
    args = [nc.dram_tensor(k, v.shape, mb.dt.from_np(v.dtype), kind="ExternalInput").ap() for k, v in arrays.items()]
    out = nc.dram_tensor("out_x", (T, D), F32, kind="ExternalOutput").ap()
    build(nc, *args, out)
    r = run_bass_kernel_spmd(nc, [arrays], core_ids=[0])
    return r.results[0]["out_x"].reshape(B, S, D)
```

```python
from contextlib import ExitStack

import concourse.bass as bass
from concourse import mybir

F32 = mybir.dt.float32
F32R = mybir.dt.float32r
U8 = mybir.dt.uint8
ALU = mybir.AluOpType
ACT = mybir.ActivationFunctionType

P = 128
B, S, D = 2, 64, 512
T = B * S
KD = D // P
S2, DC = 1024, 256
KC, SC = DC // P, S2 // P
XKV, XD = 8, 128
DI, DS, MH, HP = 1024, 64, 16, 64
XC = DI // P
CC = XC + 2
TAPS = 4
PAD = S + TAPS - 1
E1, FF1 = 8, 2048
N1 = FF1 // 512
STEPS1 = E1 * N1
AH, AKV, AD = 32, 4, 128
UNITS = AH // 4
A_LAG = 3
E2, FF2 = 32, 256
STEPS2 = E2 + 1
CHUNK = 2048
SLOTS = 8
HIGHS = 4
QKW, VOW = KD * 2 * XD + DC, KC * XD + 2 * D
MASKED = -1.0e30
LN_EPS, MIX_EPS, FFN_EPS = 1e-5, 1e-6, 1e-5
A_LOG_TOP, DECAY_BOTTOM = 80.0, -120.0

C_IN, C_OUT = 0, KD
C_W1 = C_OUT + 2


C_ATT = C_W1 + 2 * STEPS1
C_FFN = C_ATT + 2 + 2 * UNITS
CHUNKS = C_FFN + 2 * STEPS2

CONV = ((DS, XC, CC, 5), (P, 0, 4, 3), (P, 4, XC, 4))

V_MIX, V_MOE, V_SSM, V_LN1, V_LN2 = 0, KD, 2 * KD, 2 * KD + XC, 3 * KD + XC
V_TAP = 4 * KD + XC
V_CB = V_TAP + CC * TAPS
V_GATE = V_CB + CC
V_ROUTE = V_GATE + KD * E1
V_BCDT = V_ROUTE + KD * E2
BCDT = 2 * DS + MH
VECS = V_BCDT + KD * BCDT
R_DT, R_A, R_D, R_EB = 0, MH, 2 * MH, 3 * MH
ROWS = 3 * MH + E2


def up_chunk(base, s, lag=2):
    return base + s if isinstance(s, int) and s < lag else base - lag + 2 * s


def down_chunk(base, s, steps, lag=2):
    return base + steps + s if isinstance(s, int) and s >= steps - lag else base + lag + 1 + 2 * s


def wq_chunk(u):
    return up_chunk(C_ATT + 2, u, A_LAG)


def wo_chunk(u):
    return down_chunk(C_ATT + 2, u, UNITS, A_LAG)


def split_count(c):
    apart = [*range(C_IN, C_IN + KD), C_OUT, C_OUT + 1, *(wo_chunk(u) for u in range(UNITS))]
    return c + 1 - sum(r < c for r in apart)


def chunk_width(c):
    half = c >= C_FFN + 3 and ((c - C_FFN) % 2 == 1 or c >= CHUNKS - 2)
    return CHUNK // 2 if half else CHUNK


def moe_next(t):
    got = [up_chunk(C_W1, t + 1)] if 1 <= t < STEPS1 - 1 else []
    got += [down_chunk(C_W1, t - 1, STEPS1)] if 1 <= t <= STEPS1 else []
    return got + ([C_ATT, C_ATT + 1] if t == STEPS1 + 1 else [])


def ffn_next(t):
    got = [up_chunk(C_FFN, t + 1)] if 1 <= t < STEPS2 - 1 else []
    return got + ([down_chunk(C_FFN, t - 1, STEPS2)] if 1 <= t <= STEPS2 else [])


def build(nc, x, mask, ctx, ctxT, qk, vo, vecs, rows, rope, in_w, out_w, w1, w2, wkv, wq, wo, gu, dn, out):
    stack = ExitStack()
    with stack:
        def sem(name):
            return stack.enter_context(nc.semaphore(name))

        def sb(name, shape, dt=F32, scope=stack):
            return scope.enter_context(nc.sbuf_tensor(name, shape, dt))

        PS = stack.enter_context(nc.psum_tensor("PS", [P, 8, 512], F32))

        with ExitStack() as scope:
            ring = sb("ring", [P, SLOTS, CHUNK], scope=scope)
            spare = sb("spare", [P, HIGHS, CHUNK], scope=scope)
        ring_low = sb("ring_low", [P, SLOTS, CHUNK], F32R)
        high = sb("high", [P, HIGHS, CHUNK], F32R)
        vec = sb("vec", [P, VECS])
        row = sb("row", [P, ROWS])
        ident = sb("ident", [P, P])
        tri = sb("tri", [P, P])
        later = sb("later", [P, P])
        amask = sb("amask", [P, P])
        xt = sb("xt", [P, D])
        res = sb("res", [P, D])
        mid = sb("mid", [P, D])
        nrm = sb("nrm", [P, D])
        junk = sb("junk", [P, D])
        nT = sb("nT", [P, KD, P])
        nTh, nTl = sb("nTh", [P, KD, P], F32R), sb("nTl", [P, KD, P], F32R)
        moments = sb("moments", [P, 2])
        var2 = sb("var2", [P, 2])
        ms = sb("ms", [P, 2])
        log_ = sb("log_", [P, 2])
        rs = sb("rs", [P, 4])
        wsum = sb("wsum", [P, 1])
        bnst = sb("bnst", [P, 6])
        epsc = sb("epsc", [P, 2])
        cw = sb("cw", [P, E2 + 1])
        r8 = sb("r8", [P, 16])
        rsc = sb("rsc", [P, 4, E2])
        xpad = sb("xpad", [P, CC, B, PAD])

        rp = sb("rp", [P, 2, AD])

        with ExitStack() as scope:
            h_sig = sb("h_sig", [P, 2, 512], scope=scope)
            h_act = sb("h_act", [P, 2, 512], scope=scope)
            hTh, hTl = sb("hTh", [P, 2, 4, P], F32R, scope), sb("hTl", [P, 2, 4, P], F32R, scope)

        with ExitStack() as scope:
            with ExitStack() as raw:
                cT = sb("cT", [P, B, KC, S2], scope=raw)
                cx = sb("cx", [P, B, SC, DC], scope=raw)
                qk_sb, vo_sb = sb("qk_sb", [P, QKW], scope=raw), sb("vo_sb", [P, VOW], scope=raw)
            cTl = sb("cTl", [P, B, KC, S2], F32R, scope)
            cxl = sb("cxl", [P, B, SC, DC], F32R, scope)
            qkl, vol = sb("qkl", [P, QKW], F32R, scope), sb("vol", [P, VOW], F32R, scope)
            cTh = high[:, 0:2, :].rearrange("p b (k s) -> p b k s", b=B, k=KC)
            madd = spare[:, 2, :].rearrange("p (b s) -> p b s", b=B)
            mask8 = spare[:, 3, 0:B * S2 // 4].bitcast(U8).rearrange("p (b s) -> p b s", b=B)
            pTh = ring_low[:, 4, :].rearrange("p (b c q) -> p b c q", b=B, c=SC)
            pTl = ring_low[:, 5, :].rearrange("p (b c q) -> p b c q", b=B, c=SC)
            cxh = ring_low[:, 6:8, :].rearrange("p b (c n) -> p b c n", b=B, c=SC)
            pr = sb("pr", [P, B, S2], scope=scope)
            qkh, voh = sb("qkh", [P, QKW], F32R, scope), sb("voh", [P, VOW], F32R, scope)
            q_sb = sb("q_sb", [P, 2 * XD], scope=scope)
            qTh, qTl = sb("qTh", [P, 2 * T], F32R, scope), sb("qTl", [P, 2 * T], F32R, scope)
            qph, qpl = sb("qph", [P, KC, B, P], F32R, scope), sb("qpl", [P, KC, B, P], F32R, scope)
            co = sb("co", [P, B, DC], scope=scope)
            coTh, coTl = sb("coTh", [P, KC, B, P], F32R, scope), sb("coTl", [P, KC, B, P], F32R, scope)
            oTh, oTl = sb("oTh", [P, 2, T], F32R, scope), sb("oTl", [P, 2, T], F32R, scope)
            xmax = sb("xmax", [P, B], scope=scope)
            nbias = sb("nbias", [P, B], scope=scope)
            xsum = sb("xsum", [P, B], scope=scope)
            xrec = sb("xrec", [P, B], scope=scope)
            xval = sb("xval", [P, B], scope=scope)
            held = sb("held", [P, 1], scope=scope)

        with ExitStack() as scope:
            zs = sb("zs", [P, DI], scope=scope)
            cacc = sb("cacc", [P, CC, T], scope=scope)
            csig = sb("csig", [P, CC, T], scope=scope)
            cact = sb("cact", [P, CC, T], scope=scope)
            xdt = sb("xdt", [P, MH, HP], scope=scope)
            xD_ = sb("xD_", [P, MH, HP], scope=scope)
            dts = sb("dts", [P, 8, MH], scope=scope)
            wdec = sb("wdec", [P, MH, T], scope=scope)
            dec = sb("dec", [P, MH, T], scope=scope)
            gm = sb("gm", [P, P], scope=scope)
            y_sb = sb("y_sb", [P, DI], scope=scope)
            ysq = sb("ysq", [P, DI], scope=scope)
            yT = sb("yT", [P, XC, P], scope=scope)

        with ExitStack() as scope:
            ra = sb("ra", [P, 2, 4, AD], scope=scope)
            rb = sb("rb", [P, 2, 4, AD], scope=scope)
            rq = sb("rq", [P, 2, 4, AD], scope=scope)
            aqTh, aqTl = sb("aqTh", [P, 4, T], F32R, scope), sb("aqTl", [P, 4, T], F32R, scope)
            akTh, akTl = sb("akTh", [P, AKV, T], F32R, scope), sb("akTl", [P, AKV, T], F32R, scope)
            avh, avl = sb("avh", [P, AKV, AD], F32R, scope), sb("avl", [P, AKV, AD], F32R, scope)
            asc = sb("asc", [P, 2, 4, T], scope=scope)
            apr = sb("apr", [P, 2, 4, T], scope=scope)
            apn = sb("apn", [P, 2, 4, T], scope=scope)
            apTh, apTl = sb("apTh", [P, 4, T], F32R, scope), sb("apTl", [P, 4, T], F32R, scope)
            aoT = sb("aoT", [P, 4, T], scope=scope)
            amx = sb("amx", [P, 2, 4], scope=scope)
            anb = sb("anb", [P, 2, 4], scope=scope)
            asm = sb("asm", [P, 2, 4], scope=scope)
            arc = sb("arc", [P, 2, 4], scope=scope)

        ACC = PS[:, 0, :]
        x_scores = [PS[:, 1:3, :].rearrange("p a n -> p (a n)"), PS[:, 3:5, :].rearrange("p a n -> p (a n)")]
        x_ctxo = [PS[:, 1, 0:DC], PS[:, 3, 0:DC]]
        x_qp = PS[:, 2, :]
        x_tr = [PS[:, 5, :], PS[:, 6, :]]
        x_ma, x_mb = PS[:, 7, 0:256], PS[:, 7, 256:512]

        L = {n: sem("ld_" + n) for n in ("x", "qk", "vo", "mask", "cT0", "cT1", "cx0", "cx1", "vec", "row", "rope")}
        ring_loaded = [sem(f"ring_loaded{i}") for i in range(SLOTS)]
        ring_used = sem("ring_used")
        hi_ready = sem("hi_ready")
        lo_ready = sem("lo_ready")
        H = {n: sem("hi_" + n) for n in ("qk", "vo", "cT", "cx", "qT", "qp", "pT", "coT", "oT", "yT", "hT", "aT", "kT", "in",
                                         "v", "aq", "ap", "ao")}
        LO = {n: sem("lo_" + n) for n in ("qk", "vo", "cT", "cx", "v", "in")}
        s_out = sem("s_out")
        s_const = sem("s_const")
        s_pool = sem("s_pool")
        s_dve = sem("s_dve")
        s_act = sem("s_act")
        norm_ready = sem("norm_ready")
        nT_made = sem("nT_made")
        nT_ready = sem("nT_ready")
        var_ready = sem("var_ready")
        rstd_ready = sem("rstd_ready")
        xt_ready = sem("xt_ready")
        mid_ready = sem("mid_ready")
        sc_ready, s_max, nb_ready, exp_done = sem("sc_ready"), sem("s_max"), sem("nb_ready"), sem("exp_done")
        q_ready, q_copied = sem("q_ready"), sem("q_copied")
        qT_ready, qT_copied = sem("qT_ready"), sem("qT_copied")
        qp_ready, qp_copied = sem("qp_ready"), sem("qp_copied")
        pT_ready, pT_copied = sem("pT_ready"), sem("pT_copied")
        co_ready, co_copied = sem("co_ready"), sem("co_copied")
        coT_ready, coT_copied = sem("coT_ready"), sem("coT_copied")
        oT_ready, oT_copied, wo_done = sem("oT_ready"), sem("oT_copied"), sem("wo_done")
        x_dve = sem("x_dve")
        M = {n: sem("m_" + n) for n in ("dt", "pre", "bcact", "xT", "bcT", "pad", "conv", "csig", "cact", "g", "gm",
                                        "expA", "abs", "expd", "u", "lnu", "wdec", "dsum", "decay", "xtok", "xdt",
                                        "zsig", "zraw", "A", "mdec", "y", "yg", "yT", "yTs", "logit", "rexp", "cw")}
        sig_ready, act_ready, hT_made, hT_ready = (sem(n) for n in ("sig_ready", "act_ready", "hT_made", "hT_ready"))
        gsig_ready, gs_ready, a_ready, aT_made, aT_ready = (sem(n) for n in ("gsig_ready", "gs_ready", "a_ready", "aT_made", "aT_ready"))
        A = {n: sem("a_" + n) for n in ("kv", "v", "krope", "kT", "kTs", "q", "ropes", "rope", "qT", "qTs", "s", "max", "nb", "exp",
                                        "rec", "pn", "pT", "pTs", "o", "os", "logit", "rsig", "cw")}

        def wait_chunk(eng, slot, lap):
            eng.wait_ge(ring_loaded[slot], lap * 16 + 16)

        block = stack.enter_context(nc.Block())

        @block.sync
        def _(sp):
            def load(dst, src, s):
                sp.dma_start(dst, src).then_inc(s, 16)

            def ring_load(c, src, lap=None, free=None):
                slot = c % SLOTS
                if c >= SLOTS:
                    sp.wait_ge(ring_used, (c - SLOTS + 1) if free is None else free)
                n = src.shape[-1]
                sp.dma_start(ring[:, slot, 0:n], src).then_inc(ring_loaded[slot], 16)

            load(xt[:], x, L["x"])
            load(row[:], rows.to_broadcast([P, ROWS]), L["row"])
            load(qk_sb[:], qk[0], L["qk"])
            load(mask8[:].rearrange("p b s -> p (b s)"), mask.to_broadcast([P, B * S2]), L["mask"])
            load(cT[:, 0], ctxT[:, 0], L["cT0"])
            load(cT[:, 1], ctxT[:, 1], L["cT1"])
            load(cx[:, 0], ctx[:, 0], L["cx0"])
            load(cx[:, 1], ctx[:, 1], L["cx1"])
            load(vo_sb[:], vo[0], L["vo"])
            load(vec[:], vecs, L["vec"])
            load(rp[:], rope, L["rope"])
            sp.wait_ge(qp_ready, 1)
            load(qk_sb[:], qk[1], L["qk"])
            stream = [in_w[k] for k in range(KD)] + [out_w[0], out_w[1]]
            stream += [w1[0], w1[1], w1[2], w2[0], w1[3], w2[1]]
            for c in range(SLOTS // 2):
                ring_load(c, stream[c])
            with sp.Fori(1, XKV - 1) as j:
                sp.wait_ge(qp_ready, j + 1)
                load(qk_sb[:], qk[bass.ds(j + 1, 1)].rearrange("a p n -> p (a n)"), L["qk"])
                sp.wait_ge(wo_done, j)
                load(vo_sb[:], vo[bass.ds(j, 1)].rearrange("a p n -> p (a n)"), L["vo"])
            sp.wait_ge(wo_done, XKV - 1)
            load(vo_sb[:], vo[XKV - 1], L["vo"])
            sp.wait_ge(co_ready, 2 * XKV)
            for c in range(SLOTS // 2, len(stream)):
                ring_load(c, stream[c])
            with sp.Fori(1, E1) as e:
                for t in range(N1):
                    c = up_chunk(C_W1, 4 + t)
                    ring_load(c, w1[bass.ds(e * 4 + t, 1)].rearrange("a p n -> p (a n)"),
                              free=(e - 1) * 8 + (c - SLOTS + 1))
                    ring_load(c + 1, w2[bass.ds(e * 4 + t - 2, 1)].rearrange("a p n -> p (a n)"),
                              free=(e - 1) * 8 + (c - SLOTS + 2))
            stream = [(down_chunk(C_W1, s, STEPS1), w2[s]) for s in (STEPS1 - 2, STEPS1 - 1)]
            stream += [(C_ATT, wkv[0]), (C_ATT + 1, wkv[1])]
            for s in range(UNITS + A_LAG):
                if s < UNITS:
                    stream.append((wq_chunk(s), wq[s]))
                if s >= A_LAG:
                    stream.append((wo_chunk(s - A_LAG), wo[s - A_LAG]))
            for s in range(5):
                stream.append((up_chunk(C_FFN, s), gu[s]))
                if s >= 2:
                    stream.append((down_chunk(C_FFN, s - 2, STEPS2), dn[s - 2]))
            for c, src in stream:
                ring_load(c, src)
            with sp.Fori(0, (STEPS2 - 5) // 4) as i:
                for t in range(4):
                    c = up_chunk(C_FFN, 5 + t)
                    ring_load(c, gu[bass.ds(i * 4 + 5 + t, 1)].rearrange("a p n -> p (a n)"),
                              free=i * 8 + (c - SLOTS + 1))
                    ring_load(c + 1, dn[bass.ds(i * 4 + 3 + t, 1)].rearrange("a p n -> p (a n)"),
                              free=i * 8 + (c - SLOTS + 2))
            for s in (STEPS2 - 2, STEPS2 - 1):
                ring_load(down_chunk(C_FFN, s, STEPS2), dn[s])
            sp.wait_ge(mid_ready, 5)
            sp.dma_start(out, mid[:]).then_inc(s_out, 16)
            sp.wait_ge(s_out, 16)

        @block.gpsimd
        def _(pool):
            nc.gpsimd.memset(ident[:], 0.0).then_inc(s_pool, 1)
            nc.gpsimd.memset(tri[:], 1.0).then_inc(s_pool, 1)
            nc.gpsimd.memset(later[:], 1.0).then_inc(s_pool, 1)
            nc.gpsimd.memset(amask[:], 0.0).then_inc(s_pool, 1)
            nc.gpsimd.memset(xpad[:], 0.0).then_inc(s_pool, 1)
            nc.gpsimd.memset(cw[:, E2:E2 + 1], 1.0).then_inc(s_pool, 1)
            nc.gpsimd.memset(epsc[:, 0:1], MIX_EPS).then_inc(s_pool, 1)
            nc.gpsimd.memset(epsc[:, 1:2], FFN_EPS).then_inc(s_pool, 1)
            pool.wait_ge(s_pool, 8)

            def select(m, cmp, fill, base, pattern, mul):
                return nc.gpsimd.affine_select(out=m, in_=m, compare_op=cmp, fill=fill, base=base,
                                               pattern=pattern, channel_multiplier=mul)

            select(ident[:], ALU.not_equal, 1.0, 0, [[-1, P]], 1).then_inc(s_const, 1)
            select(later[:], ALU.is_gt, 0.0, 0, [[-1, P]], 1).then_inc(s_const, 1)
            select(tri[:], ALU.is_ge, 0.0, 0, [[1, P]], -1).then_inc(s_pool, 1)
            select(amask[:], ALU.is_ge, MASKED, 0, [[-1, P]], 1).then_inc(s_pool, 1)
            pool.wait_ge(s_pool, 10)
            select(tri[:, S:T], ALU.is_ge, 0.0, -S, [[0, S]], 1).then_inc(s_const, 1)
            select(amask[:, 0:S], ALU.is_ge, MASKED, S - 1, [[0, S]], -1).then_inc(s_const, 1)
            for b in range(B):
                pool.wait_ge(H["cx"], b + 1)
                nc.gpsimd.tensor_tensor(cxl[:, b], cx[:, b], cxh[:, b].bitcast(F32), ALU.subtract).then_inc(LO["cx"], 1)
            for n, k in enumerate((2, 3, 0)):
                pool.wait_ge(H["in"], n + 1)
                nc.gpsimd.tensor_tensor(ring_low[:, C_IN + k, :], ring[:, C_IN + k, :], high[:, k, :].bitcast(F32),
                                        ALU.subtract).then_inc(LO["in"], 1)

        @block.tensor
        def _(pe):
            mm = nc.tensor.matmul

            def mm3(dst, still, moving, start, stop, **kw):
                (sh, sl), (mh, ml) = still, moving
                mm(dst, sl, mh, start=start, stop=False, **kw)
                mm(dst, sh, mh, start=False, stop=False, **kw)
                return mm(dst, sh, ml, start=False, stop=stop, **kw)

            def nT_(k):
                return nTh[:, k, :], nTl[:, k, :]

            def chunk_part(c, a, b):
                return high[:, c % HIGHS, a:b], ring_low[:, c % SLOTS, a:b]

            def transpose_norm(n, bank):
                pe.wait_ge(norm_ready, n)
                for k in range(KD):
                    i = nc.tensor.transpose(bank[:, k * P:(k + 1) * P], nrm[:, k * P:(k + 1) * P], ident[:])
                i.then_inc(nT_made, 1)

            def keep_warm(n, bank):
                for _ in range(n):
                    mm(bank[:, 0:P], ident[:], ident[:], start=True, stop=True)

            def x_q(j):
                pe.wait_ge(LO["qk"], j + 1)
                for k in range(KD):
                    w = qkh[:, k * 256:(k + 1) * 256], qkl[:, k * 256:(k + 1) * 256]
                    i = mm3(x_scores[0][:, 0:256], nT_(k), w, start=(k == 0), stop=(k == KD - 1))
                i.then_inc(q_ready, 1)

            def x_qT(j):
                pe.wait_ge(q_copied, j + 1)
                for h in range(2):
                    i = nc.tensor.transpose(x_ma[:, h * P:(h + 1) * P], q_sb[:, h * P:(h + 1) * P], ident[:])
                i.then_inc(qT_ready, 1)

            def x_qproj(j):
                pe.wait_ge(qT_copied, j + 1)
                for kc in range(KC):
                    w = slice(KD * 256 + kc * P, KD * 256 + (kc + 1) * P)
                    i = mm3(x_qp[:, kc * 256:(kc + 1) * 256].rearrange("p (b h q) -> p b h q", b=B, h=2),
                            (qkh[:, w], qkl[:, w]),
                            [a[:].rearrange("p (h b q) -> p b h q", b=B, h=2) for a in (qTh, qTl)], start=True, stop=True)
                i.then_inc(qp_ready, 1)

            def x_score(j, b):
                for n in range(2):
                    for kc in range(KC):
                        part = slice(n * 512, (n + 1) * 512)
                        i = mm3(x_scores[b][:, part], (qph[:, kc, b, :], qpl[:, kc, b, :]),
                                (cTh[:, b, kc, part], cTl[:, b, kc, part]), start=(kc == 0), stop=(kc == KC - 1))
                i.then_inc(sc_ready, 1)

            def x_probT(j, b):
                pe.wait_ge(exp_done, j * 2 + b + 1)
                if b or not isinstance(j, int) or j:
                    pe.wait_ge(pT_copied, j * 4 + 2 * b)
                for n in range(2):
                    for c in range(4):
                        s = n * 4 + c
                        i = nc.tensor.transpose(x_tr[n][:, c * P:(c + 1) * P], pr[:, b, s * P:(s + 1) * P], ident[:])
                    i.then_inc(pT_ready, 1)

            def x_mix(j, b, half):
                for s in range(half * 4, half * 4 + 4):
                    if s % 4 == 0:
                        pe.wait_ge(pT_copied, j * 4 + 2 * b + 1 + s // 4)
                    i = mm3(x_ctxo[b], (pTh[:, b, s, :], pTl[:, b, s, :]), (cxh[:, b, s, :], cxl[:, b, s, :]), start=(s == 0), stop=(s == SC - 1))
                if half:
                    i.then_inc(co_ready, 1)

            def x_coT(j, b):
                pe.wait_ge(co_copied, j * 2 + b + 1)
                dst = x_mb if b else x_ma
                for kc in range(KC):
                    i = nc.tensor.transpose(dst[:, kc * P:(kc + 1) * P], co[:, b, kc * P:(kc + 1) * P], ident[:])
                i.then_inc(coT_ready, 1)

            def x_value(j):
                pe.wait_ge(coT_copied, j * 2 + 2)
                pe.wait_ge(LO["vo"], j + 1)
                for kc in range(KC):
                    i = mm3(x_ma.rearrange("p (h b q) -> p h b q", h=2, b=B),
                            (voh[:, kc * P:(kc + 1) * P], vol[:, kc * P:(kc + 1) * P]),
                            [a[:, kc].rearrange("p b (h q) -> p h b q", h=2) for a in (coTh, coTl)], start=(kc == 0), stop=(kc == KC - 1))
                i.then_inc(oT_ready, 1)

            def x_out(j, last=False):
                pe.wait_ge(oT_copied, j + 1)
                for h in range(2):
                    w = slice(KC * P + h * D, KC * P + (h + 1) * D)
                    i = mm3(ACC, (oTh[:, h, :], oTl[:, h, :]), (voh[:, w], vol[:, w]), start=False,
                            stop=last and h == 1, skip_group_check=True)
                i.then_inc(wo_done, 1)

            def x_head(j, prev, nxt):
                pe.wait_ge(qp_copied, j + 1)
                if not prev:
                    pe.wait_ge(LO["cT"], 1)
                x_score(j, 0)
                if prev:
                    pe.wait_ge(coT_copied, j * 2 - 1)
                    x_coT(j - 1, 1)
                else:
                    pe.wait_ge(LO["cT"], 2)
                x_score(j, 1)
                if prev:
                    x_value(j - 1)
                if nxt:
                    pe.wait_ge(s_max, j * 2 + 1)
                    x_q(j + 1)
                x_probT(j, 0)
                if prev:
                    x_out(j - 1)
                if nxt:
                    x_qT(j + 1)
                if not prev:
                    pe.wait_ge(LO["cx"], 1)
                x_mix(j, 0, 0)
                x_probT(j, 1)
                x_mix(j, 0, 1)
                if nxt:
                    x_qproj(j + 1)
                if not prev:
                    pe.wait_ge(LO["cx"], 2)
                x_mix(j, 1, 0)
                x_mix(j, 1, 1)
                x_coT(j, 0)

            pe.wait_ge(s_const, 4)
            keep_warm(10, PS[:, 5, :])
            transpose_norm(1, PS[:, 1, :])
            mm(ACC, ident[:], xt[:], start=True, stop=False, skip_group_check=True)
            keep_warm(5, PS[:, 5, :])
            pe.wait_ge(nT_ready, 2)
            x_q(0)
            keep_warm(3, PS[:, 5, :])
            x_qT(0)
            keep_warm(4, PS[:, 5, :])
            x_qproj(0)
            keep_warm(6, PS[:, 5, :])
            x_head(0, False, True)
            with pe.Fori(1, XKV - 1) as j:
                x_head(j, True, True)
            x_head(XKV - 1, True, False)
            pe.wait_ge(coT_copied, XKV * 2 - 1)
            x_coT(XKV - 1, 1)
            x_value(XKV - 1)
            x_out(XKV - 1, last=True)

            keep_warm(18, PS[:, 1, :])
            transpose_norm(2, PS[:, 7, :])
            keep_warm(9, PS[:, 1, :])
            pe.wait_ge(nT_ready, 4)
            pe.wait_ge(L["vec"], 16)
            w0 = [V_BCDT + k * BCDT for k in range(KD)]
            for k in range(KD):
                i = mm(PS[:, 6, 0:MH], nT[:, k, :], vec[:, w0[k] + 2 * DS:w0[k] + BCDT], start=(k == 0), stop=(k == KD - 1))
            i.then_inc(M["dt"], 1)
            for n in range(2):
                for k in range(KD):
                    i = mm(PS[0:DS, 5, n * P:(n + 1) * P], vec[:, w0[k] + n * DS:w0[k] + (n + 1) * DS], nT[:, k, :],
                           start=(k == 0), stop=(k == KD - 1))
            i.then_inc(M["bcT"], 1)
            pe.wait_ge(LO["in"], KD)
            for f in range(XC):
                for k in range(KD):
                    i = mm3(PS[:, 3 + f // 4, (f % 4) * P:(f % 4 + 1) * P], chunk_part(C_IN + k, DI + f * P, DI + (f + 1) * P),
                            nT_(k), start=(k == 0), stop=(k == KD - 1))
                if f % 4 == 3:
                    i.then_inc(M["xT"], 1)
            pe.wait_ge(M["wdec"], 1)
            for n in range(4):
                if n >= 2:
                    pe.wait_ge(M["decay"], n - 1)
                i = mm(PS[:, 6 + n % 2, :], later[:], wdec[:, n * 4:(n + 1) * 4, :], start=True, stop=True)
                i.then_inc(M["dsum"], 1)

            def m_z(n):
                for k in range(KD):
                    i = mm3(PS[:, 1 + n, :], nT_(k), chunk_part(C_IN + k, n * 512, (n + 1) * 512),
                            start=(k == 0), stop=(k == KD - 1))
                    if n:
                        i.then_inc(ring_used, 1)

            m_z(0)
            pe.wait_ge(M["bcact"], 1)
            mm(PS[:, 5, 0:P], cact[0:DS, XC, :], cact[0:DS, XC + 1, :], start=True, stop=True).then_inc(M["g"], 1)
            m_z(1)
            for n in range(2):
                pe.wait_ge(M["cact"], n + 1)
                for c in range(4):
                    i = nc.tensor.transpose(PS[:, 3 + n, c * P:(c + 1) * P], cact[:, n * 4 + c, :], ident[:])
                i.then_inc(M["xtok"], 1)
            pe.wait_ge(M["xdt"], 2)
            pe.wait_ge(M["mdec"], 1)
            for h in range(MH):
                i = mm(PS[:, 6 + h // 8, (h % 8) * HP:(h % 8 + 1) * HP], dec[:, h, :], xdt[:, h, :], start=True, stop=True)
                if h % 8 == 7:
                    i.then_inc(M["y"], 1)
            for n in range(2):
                pe.wait_ge(M["yg"], n + 1)
                for c in range(4):
                    f = n * 4 + c
                    i = nc.tensor.transpose(PS[:, 3 + n, c * P:(c + 1) * P], y_sb[:, f * P:(f + 1) * P], ident[:])
                i.then_inc(M["yT"], 1)
            for n in range(2):
                wait_chunk(pe, C_OUT + n, 0)
                pe.wait_ge(M["yTs"], n + 1)
                for c in range(4):
                    i = mm(PS[:, 5, :], yT[:, n * 4 + c, :], ring[:, C_OUT + n, c * D:(c + 1) * D],
                           start=(n == 0 and c == 0), stop=(n == 1 and c == 3))
                i.then_inc(ring_used, 1)

            pe.wait_ge(xt_ready, 1)
            mm(ACC, ident[:], xt[:], start=True, stop=False, skip_group_check=True)
            pe.wait_ge(mid_ready, 2)
            mm(ACC, ident[:], mid[:], start=False, stop=False, skip_group_check=True)
            keep_warm(6, PS[:, 1, :])
            transpose_norm(3, PS[:, 6, :])
            keep_warm(6, PS[:, 1, :])
            pe.wait_ge(nT_ready, 6)
            for k in range(KD):
                i = mm(PS[:, 7, 0:E1], nT[:, k, :], vec[:, V_GATE + k * E1:V_GATE + (k + 1) * E1],
                       start=(k == 0), stop=(k == KD - 1))
            i.then_inc(M["logit"], 1)

            def up(par, c, lap):
                pe.wait_ge(lo_ready, lap * SLOTS + split_count(c))
                for k in range(KD):
                    i = mm3(PS[:, 1 + par, :], nT_(k), chunk_part(c, k * 512, (k + 1) * 512),
                            start=(k == 0), stop=(k == KD - 1))
                i.then_inc(ring_used, 1)

            def down(s, par, c, lap, last=False):
                pe.wait_ge(lo_ready, lap * SLOTS + split_count(c))
                pe.wait_ge(hT_ready, s + 1)
                for n in range(4):
                    i = mm3(ACC, (hTh[:, par, n, :], hTl[:, par, n, :]), chunk_part(c, n * D, (n + 1) * D), start=False,
                            stop=last and n == 3, skip_group_check=True)
                i.then_inc(ring_used, 1)

            def turn(s, par):
                pe.wait_ge(act_ready, s + 1)
                for c in range(4):
                    i = nc.tensor.transpose(PS[:, 3 + par, c * P:(c + 1) * P], h_act[:, par, c * P:(c + 1) * P], ident[:])
                i.then_inc(hT_made, 1)

            def moe_step(s, t, i=0):
                cu, cd = up_chunk(C_W1, t), down_chunk(C_W1, t - 2, STEPS1)
                if t < STEPS1:
                    up(t % 2, cu, i)
                if t >= 2:
                    down(s - 2, t % 2, cd, i, last=(t == STEPS1 + 1))
                if 1 <= t <= STEPS1:
                    turn(s - 1, (t + 1) % 2)

            for s in range(4):
                moe_step(s, s)
            with pe.Fori(1, E1) as e:
                for t in range(4):
                    moe_step(e * 4 + t, 4 + t, e - 1)
            for s in (STEPS1, STEPS1 + 1):
                moe_step(s, s)

            transpose_norm(4, PS[:, 7, :])
            pe.wait_ge(mid_ready, 3)
            pe.wait_ge(xt_ready, 2)
            mm(ACC, ident[:], res[:], start=True, stop=False, skip_group_check=True)
            pe.wait_ge(nT_ready, 8)
            for n in range(2):
                pe.wait_ge(lo_ready, split_count(C_ATT + n))
                for k in range(KD):
                    i = mm3(PS[:, 4 + n, :], nT_(k), chunk_part(C_ATT + n, k * 512, (k + 1) * 512),
                            start=(k == 0), stop=(k == KD - 1))
                i.then_inc(ring_used, 1)

            def a_q(u):
                c0 = wq_chunk(u)
                pe.wait_ge(lo_ready, split_count(c0))
                if u >= 2:
                    pe.wait_ge(A["ropes"], u)
                for k in range(KD):
                    i = mm3(PS[:, 1 + u % 2, :], nT_(k), chunk_part(c0, k * 512, (k + 1) * 512),
                            start=(k == 0), stop=(k == KD - 1))
                i.then_inc(ring_used, 1)

            def a_kT():
                pe.wait_ge(A["krope"], 1)
                for c in range(AKV):
                    i = nc.tensor.transpose(PS[:, 6, c * P:(c + 1) * P], rq[:, 1, c, :], ident[:])
                i.then_inc(A["kT"], 1)

            def a_qT(u):
                pe.wait_ge(A["rope"], u + 1)
                if u:
                    pe.wait_ge(A["qTs"], u)
                for c in range(4):
                    i = nc.tensor.transpose(PS[:, 3, c * P:(c + 1) * P], rq[:, u % 2, c, :], ident[:])
                i.then_inc(A["qT"], 1)

            def a_scores(u):
                pe.wait_ge(A["qTs"], u + 1)
                pe.wait_ge(A["kTs"], 1)
                if u < 2:
                    pe.wait_ge(LO["v"], 1)
                for c in range(4):
                    i = mm3(PS[:, 4 + u % 2, c * P:(c + 1) * P], (aqTh[:, c, :], aqTl[:, c, :]),
                            (akTh[:, u // 2, :], akTl[:, u // 2, :]), start=True, stop=True)
                i.then_inc(A["s"], 1)

            def a_probT(u):
                pe.wait_ge(A["pn"], u + 1)
                pe.wait_ge(A["kTs"], 1)
                if u:
                    pe.wait_ge(A["pTs"], u)
                for c in range(4):
                    i = nc.tensor.transpose(PS[:, 6, c * P:(c + 1) * P], apn[:, u % 2, c, :], ident[:])
                i.then_inc(A["pT"], 1)

            def a_value(u):
                pe.wait_ge(A["pTs"], u + 1)
                if u:
                    pe.wait_ge(A["os"], u)
                mm3(PS[:, 7, :], (avh[:, u // 2, :], avl[:, u // 2, :]), (apTh[:], apTl[:]), start=True,
                    stop=True).then_inc(A["o"], 1)

            def a_out(u):
                c0 = wo_chunk(u)
                wait_chunk(pe, c0 % SLOTS, c0 // SLOTS)
                pe.wait_ge(A["os"], u + 1)
                for c in range(4):
                    i = mm(ACC, aoT[:, c, :], ring[:, c0 % SLOTS, c * D:(c + 1) * D], start=False,
                           stop=(u == UNITS - 1 and c == 3), skip_group_check=True)
                i.then_inc(ring_used, 1)

            for s in range(UNITS + A_LAG):
                if 1 <= s <= UNITS:
                    a_qT(s - 1)
                if s < UNITS:
                    a_q(s)
                if s == 0:
                    a_kT()
                if 2 <= s < UNITS + 2:
                    a_probT(s - 2)
                if 1 <= s <= UNITS:
                    a_scores(s - 1)
                if s >= A_LAG:
                    a_out(s - A_LAG)
                if 2 <= s < UNITS + 2:
                    a_value(s - 2)

            transpose_norm(5, PS[:, 6, :])
            mm(ACC, ident[:], xt[:], start=True, stop=False, skip_group_check=True)
            pe.wait_ge(mid_ready, 4)
            mm(ACC, ident[:], mid[:], start=False, stop=False, skip_group_check=True)
            pe.wait_ge(nT_ready, 10)
            for k in range(KD):
                i = mm(PS[:, 7, 0:E2], nT[:, k, :], vec[:, V_ROUTE + k * E2:V_ROUTE + (k + 1) * E2],
                       start=(k == 0), stop=(k == KD - 1))
            i.then_inc(A["logit"], 1)

            def ffn_step(s, t, i=0):
                if t < STEPS2:
                    c = up_chunk(C_FFN, t)
                    pe.wait_ge(lo_ready, i * SLOTS + split_count(c))
                    for k in range(KD):
                        x_ = mm3(PS[:, 1 + t % 2, :], nT_(k), chunk_part(c, k * 512, (k + 1) * 512),
                                 start=(k == 0), stop=(k == KD - 1))
                    x_.then_inc(ring_used, 1)
                if t >= 2:
                    c = down_chunk(C_FFN, t - 2, STEPS2)
                    pe.wait_ge(lo_ready, i * SLOTS + split_count(c))
                    pe.wait_ge(aT_ready, s - 1)
                    for n in range(2):
                        x_ = mm3(ACC, (hTh[:, t % 2, n, :], hTl[:, t % 2, n, :]), chunk_part(c, n * D, (n + 1) * D), start=False,
                                 stop=(t == STEPS2 + 1 and n == 1), skip_group_check=True)
                    x_.then_inc(ring_used, 1)
                if 1 <= t <= STEPS2:
                    pe.wait_ge(a_ready, s)
                    for n in range(2):
                        x_ = nc.tensor.transpose(PS[:, 3 + (t + 1) % 2, n * P:(n + 1) * P],
                                                 h_act[:, (t + 1) % 2, n * P:(n + 1) * P], ident[:])
                    x_.then_inc(aT_made, 1)

            for s in range(5):
                ffn_step(s, s)
            with pe.Fori(0, (STEPS2 - 5) // 4) as i:
                for t in range(4):
                    ffn_step(i * 4 + 5 + t, 5 + t, i)
            for s in (STEPS2, STEPS2 + 1):
                ffn_step(s, s)

        @block.scalar
        def _(act):
            steps = [0]
            act_fn = nc.scalar.activation

            def settled(ins):
                steps[0] += 1
                ins.then_inc(s_act, 1)
                act.wait_ge(s_act, steps[0])

            def chunk_high(c, lap=0):
                wait_chunk(act, c % SLOTS, lap + c // SLOTS)
                if c >= HIGHS:
                    act.wait_ge(ring_used, lap * SLOTS + (c - HIGHS + 1))
                n = chunk_width(c)
                nc.scalar.copy(high[:, c % HIGHS, 0:n], ring[:, c % SLOTS, 0:n]).then_inc(hi_ready, 1)

            XS = float(XD) ** -0.5

            def root(n, dst, src, **kw):
                act.wait_ge(var_ready, n)
                settled(act_fn(log_[:, 0:src.shape[-1]], src, ACT.Ln, **kw))
                act_fn(dst, log_[:, 0:src.shape[-1]], ACT.Exp, scale=-0.5).then_inc(rstd_ready, 1)

            def in_high(k):
                wait_chunk(act, C_IN + k, 0)
                nc.scalar.copy(high[:, k, :], ring[:, C_IN + k, :]).then_inc(H["in"], 1)

            def qk_high(j):
                act.wait_ge(L["qk"], j * 16 + 16)
                nc.scalar.copy(qkh[:], qk_sb[:]).then_inc(H["qk"], 1)

            def vo_high(j):
                act.wait_ge(L["vo"], j * 16 + 16)
                nc.scalar.copy(voh[:], vo_sb[:]).then_inc(H["vo"], 1)

            def x_pT_high(j, b):
                for n in range(2):
                    act.wait_ge(pT_ready, j * 4 + 2 * b + n + 1)
                    nc.scalar.copy(pTh[:, b, n * 4:(n + 1) * 4, :].rearrange("p c q -> p (c q)"), x_tr[n]).then_inc(H["pT"], 1)

            def x_coT_high(j, b):
                act.wait_ge(coT_ready, j * 2 + b + 1)
                nc.scalar.copy(coTh[:, :, b, :], (x_mb if b else x_ma).rearrange("p (k q) -> p k q", k=KC)).then_inc(H["coT"], 1)

            def x_oT_high(j):
                act.wait_ge(oT_ready, j + 1)
                nc.scalar.copy(oTh[:].rearrange("p h t -> p (h t)"), x_ma).then_inc(H["oT"], 1)

            def x_exp(j, b):
                act.wait_ge(nb_ready, j * 2 + b + 1)
                act_fn(pr[:, b, :], pr[:, b, :], ACT.Exp, bias=nbias[:, b:b + 1], scale=XS,
                       accum_out=xsum[:, b:b + 1]).then_inc(exp_done, 1)

            def x_copies(j, what):
                if what == 0:
                    act.wait_ge(q_ready, j + 1)
                    nc.scalar.copy(q_sb[:], x_scores[0][:, 0:256]).then_inc(q_copied, 1)
                if what == 1:
                    act.wait_ge(qT_ready, j + 1)
                    nc.scalar.copy(qTh[:], x_ma).then_inc(H["qT"], 1)
                if what == 2:
                    act.wait_ge(qp_ready, j + 1)
                    nc.scalar.copy(qph[:].rearrange("p a b q -> p (a b q)"), x_qp).then_inc(H["qp"], 1)

            root(1, rs[:, 0:1], var2[:, 0:1])
            def cT_high(b):
                act.wait_ge(L[f"cT{b}"], 16)
                nc.scalar.copy(cTh[:, b], cT[:, b]).then_inc(H["cT"], 1)

            qk_high(0)
            cT_high(0)
            for w in range(3):
                x_copies(0, w)
            cT_high(1)
            for b in range(B):
                act.wait_ge(L[f"cx{b}"], 16)
                nc.scalar.copy(cxh[:, b], cx[:, b]).then_inc(H["cx"], 1)

            def x_head(j, prev, nxt):
                if nxt:
                    qk_high(j + 1)
                if prev:
                    x_coT_high(j - 1, 1)
                x_exp(j, 0)
                if prev:
                    x_oT_high(j - 1)
                x_exp(j, 1)
                if nxt:
                    x_copies(j + 1, 0)
                x_pT_high(j, 0)
                if nxt:
                    x_copies(j + 1, 1)
                else:
                    act.wait_ge(s_max, XKV * 2)
                    in_high(2)
                x_pT_high(j, 1)
                if nxt:
                    x_copies(j + 1, 2)
                vo_high(j)
                if not nxt:
                    in_high(3)
                x_coT_high(j, 0)

            x_head(0, False, True)
            with act.Fori(1, XKV - 1) as j:
                x_head(j, True, True)
            x_head(XKV - 1, True, False)
            x_coT_high(XKV - 1, 1)
            x_oT_high(XKV - 1)

            act.wait_ge(sc_ready, XKV * 2)
            in_high(0)
            root(2, rs[:, 0:2], var2[:])
            in_high(1)
            act.wait_ge(L["row"], 16)
            act.wait_ge(M["expA"], 1)
            act_fn(dts[:, 0, :], dts[:, 0, :], ACT.Exp).then_inc(M["A"], 1)
            act.wait_ge(M["abs"], 1)
            act_fn(dts[:, 3, :], dts[:, 2, :], ACT.Exp, scale=-1.0).then_inc(M["expd"], 1)
            act.wait_ge(M["u"], 1)
            act_fn(dts[:, 5, :], dts[:, 4, :], ACT.Ln).then_inc(M["lnu"], 1)
            act.wait_ge(s_const, 4)
            for g, (rows_, c0, c1, bank) in enumerate(CONV):
                act.wait_ge(M["xT"] if g else M["bcT"], g if g else 1)
                nc.scalar.copy(xpad[0:rows_, c0:c1, :, TAPS - 1:PAD],
                               PS[0:rows_, bank, 0:(c1 - c0) * P].rearrange("p (c b t) -> p c b t", c=c1 - c0, b=B))
                for c in range(c0, c1):
                    w = V_TAP + c * TAPS + TAPS - 1
                    i = act_fn(cacc[0:rows_, c, :], PS[0:rows_, bank, (c - c0) * P:(c - c0 + 1) * P], ACT.Identity,
                               bias=vec[0:rows_, V_CB + c:V_CB + c + 1], scale=vec[0:rows_, w:w + 1])
                i.then_inc(M["pre"], 1)
            for n in range(4):
                act.wait_ge(M["dsum"], n + 1)
                act_fn(dec[:, n * 4:(n + 1) * 4, :], PS[:, 6 + n % 2, :].rearrange("p (h t) -> p h t", h=4),
                       ACT.Exp).then_inc(M["decay"], 1)
            for g, (rows_, c0, c1, _) in enumerate(CONV):
                act.wait_ge(M["conv"], g + 1)
                act_fn(csig[0:rows_, c0:c1, :], cacc[0:rows_, c0:c1, :], ACT.Sigmoid).then_inc(M["csig"], 1)
            act.wait_ge(ring_used, KD)
            act_fn(zs[:], PS[:, 1:3, :].rearrange("p a n -> p (a n)"), ACT.Sigmoid).then_inc(M["zraw"], 1)
            for c in range(C_W1, SLOTS):
                chunk_high(c)
            root(3, rs[:, 3:4], ms[:, 1:2], bias=epsc[:, 0:1])
            root(4, rs[:, 2:3], ms[:, 0:1], bias=epsc[:, 0:1])
            act.wait_ge(M["rexp"], 1)
            act_fn(r8[:, 8:16], rsc[:, 1, 0:8], ACT.Exp).then_inc(M["rexp"], 1)

            def hidden_T_high(s, par):
                act.wait_ge(hT_made, s + 1)
                nc.scalar.copy(hTh[:, par].rearrange("p c t -> p (c t)"), PS[:, 3 + par, :]).then_inc(H["hT"], 1)

            def moe_step(s, t, i=0):
                if t >= 2:
                    hidden_T_high(s - 2, t % 2)
                for c in moe_next(t):
                    chunk_high(c, i)
                if t < STEPS1:
                    hidden_sigmoid(s, t % 2)

            def hidden_sigmoid(s, par):
                act.wait_ge(ring_used, up_chunk(C_W1, s) + 1)
                act_fn(h_sig[:, par, :], PS[:, 1 + par, :], ACT.Sigmoid).then_inc(sig_ready, 1)

            for s in range(4):
                moe_step(s, s)
            with act.Fori(1, E1 - 1) as e:
                for t in range(4):
                    moe_step(e * 4 + t, 4 + t, e - 1)
            for s in range(STEPS1 - 4, STEPS1 + 2):
                moe_step(s, s)

            root(5, rs[:, 0:2], var2[:])
            chunk_high(C_ATT + 2)
            chunk_high(C_ATT + 3)
            act.wait_ge(ring_used, C_ATT + 2)
            nc.scalar.copy(avh[:].rearrange("p g d -> p (g d)"), PS[:, 5, :]).then_inc(H["v"], 1)
            act.wait_ge(A["kT"], 1)
            nc.scalar.copy(akTh[:].rearrange("p g t -> p (g t)"), PS[:, 6, :]).then_inc(H["kT"], 1)
            AS = float(AD) ** -0.5

            def a_exp(u):
                act.wait_ge(A["nb"], u + 1)
                for c in range(4):
                    i = act_fn(apr[:, u % 2, c, :], asc[:, u % 2, c, :], ACT.Exp, bias=anb[:, u % 2, c:c + 1], scale=AS,
                               accum_out=asm[:, u % 2, c:c + 1])
                i.then_inc(A["exp"], 1)

            def a_copy_T(u):
                act.wait_ge(A["qT"], u + 1)
                nc.scalar.copy(aqTh[:].rearrange("p h t -> p (h t)"), PS[:, 3, :]).then_inc(H["aq"], 1)

            def a_copy_pT(u):
                act.wait_ge(A["pT"], u + 1)
                nc.scalar.copy(apTh[:].rearrange("p h t -> p (h t)"), PS[:, 6, :]).then_inc(H["ap"], 1)

            def a_copy_o(u):
                act.wait_ge(A["o"], u + 1)
                nc.scalar.copy(aoT[:].rearrange("p h t -> p (h t)"), PS[:, 7, :]).then_inc(A["os"], 1)

            for s in range(UNITS + A_LAG):
                if 1 <= s <= UNITS:
                    a_copy_T(s - 1)
                if 2 <= s < UNITS + 2:
                    a_copy_pT(s - 2)
                if s + 2 < UNITS:
                    chunk_high(wq_chunk(s + 2))
                if s > UNITS:
                    chunk_high(C_FFN + s - UNITS - 1)
                if 1 <= s <= UNITS:
                    a_exp(s - 1)
                if 2 <= s < UNITS + 2:
                    a_copy_o(s - 2)
            root(6, rs[:, 2:3], ms[:, 0:1], bias=epsc[:, 1:2])

            act.wait_ge(A["logit"], 1)
            act_fn(rsc[:, 0, :], PS[:, 7, 0:E2], ACT.Sigmoid).then_inc(A["rsig"], 1)

            def gated_T_high(s, par):
                act.wait_ge(aT_made, s + 1)
                nc.scalar.copy(hTh[:, par, 0:2].rearrange("p c t -> p (c t)"), PS[:, 3 + par, 0:2 * P]).then_inc(H["aT"], 1)

            def ffn_step(s, t, i=0):
                if t >= 2:
                    gated_T_high(s - 2, t % 2)
                for c in ffn_next(t):
                    chunk_high(c, i)
                if t < STEPS2:
                    gate_sigmoid(s, t % 2)

            def gate_sigmoid(s, par):
                act.wait_ge(ring_used, up_chunk(C_FFN, s) + 1)
                act_fn(h_sig[:, par, 0:FF2], PS[:, 1 + par, 0:FF2], ACT.Sigmoid).then_inc(gsig_ready, 1)

            for s in range(5):
                ffn_step(s, s)
            with act.Fori(0, (STEPS2 - 5) // 4 - 1) as i:
                for t in range(4):
                    ffn_step(i * 4 + 5 + t, 5 + t, i)
            for s in range(STEPS2 - 4, STEPS2 + 2):
                ffn_step(s, s)

        @block.vector
        def _(dve):
            V = nc.vector
            steps = [0]

            def settled(ins):
                steps[0] += 1
                ins.then_inc(s_dve, 1)
                dve.wait_ge(s_dve, steps[0])

            def layer_norm(n, src, dst, done, eps=None):
                settled(V.bn_stats(bnst[:], src))
                settled(V.bn_aggr(moments[:], bnst[:]))
                if eps is not None:
                    V.tensor_scalar(var2[:, 1:2], moments[:, 1:2], 1.0 + eps, LN_EPS * eps, ALU.mult, ALU.add)
                V.tensor_scalar(var2[:, 0:1], moments[:, 1:2], LN_EPS, None, ALU.add).then_inc(var_ready, 1)
                dve.wait_ge(rstd_ready, n)
                if eps is not None:
                    V.tensor_scalar(nrm[:], src, moments[:, 0:1], rs[:, 1:2], ALU.subtract, ALU.mult).then_inc(norm_ready, 1)
                V.tensor_scalar(dst, src, moments[:, 0:1], rs[:, 0:1], ALU.subtract, ALU.mult).then_inc(done, 1)

            def mean_square(src, squares, n):
                V.tensor_tensor_reduce(out=squares, in0=src, in1=src, scale=1.0 / src.shape[-1], scalar=0.0, op0=ALU.mult,
                                       op1=ALU.add, accum_out=ms[:, n:n + 1]).then_inc(var_ready, 1)

            def rms_norm(n, src):
                mean_square(src, junk[:], 0)
                dve.wait_ge(rstd_ready, n)
                V.tensor_scalar(nrm[:], src, rs[:, 2:3], None, ALU.mult).then_inc(norm_ready, 1)

            def copy_nT(n, bank, v):
                dve.wait_ge(nT_made, n)
                src = bank.rearrange("p (k t) -> p k t", k=KD)
                if v is None:
                    settled(V.tensor_copy(nT[:], src))
                else:
                    settled(V.tensor_tensor(nT[:], src, vec[:, v:v + KD].rearrange("p (k o) -> p k o", o=1).to_broadcast([P, KD, T]),
                                            ALU.mult))
                V.tensor_copy(nTh[:], nT[:]).then_inc(nT_ready, 1)
                dve.wait_ge(nT_ready, 2 * n - 1)
                V.tensor_tensor(nTl[:], nT[:], nTh[:].bitcast(F32), ALU.subtract).then_inc(nT_ready, 1)

            def low(dst, src, hi):
                return V.tensor_tensor(dst, src, hi.bitcast(F32), ALU.subtract)

            def chunk_low(c, lap=0):
                dve.wait_ge(hi_ready, lap * SLOTS + split_count(c))
                n = chunk_width(c)
                low(ring_low[:, c % SLOTS, 0:n], ring[:, c % SLOTS, 0:n], high[:, c % HIGHS, 0:n]).then_inc(lo_ready, 1)

            dve.wait_ge(L["x"], 16)
            layer_norm(1, xt[:], nrm[:], norm_ready)
            XS = float(XD) ** -0.5

            def x_max(j, b):
                dve.wait_ge(sc_ready, j * 2 + b + 1)
                V.memset(held[:], 0.0)
                V.tensor_tensor_reduce(out=pr[:, b, :], in0=x_scores[b], in1=madd[:, b, :], scale=1.0, scalar=2 * MASKED,
                                       op0=ALU.add, op1=ALU.max, accum_out=xmax[:, b:b + 1]).then_inc(s_max, 1)
                dve.wait_ge(s_max, j * 2 + b + 1)
                V.tensor_scalar(nbias[:, b:b + 1], xmax[:, b:b + 1], -XS, None, ALU.mult).then_inc(nb_ready, 1)

            def x_recip(j, b):
                dve.wait_ge(exp_done, j * 2 + b + 1)
                V.reciprocal(xrec[:, b:b + 1], xsum[:, b:b + 1]).then_inc(x_dve, 1)
                V.tensor_scalar(xval[:, b:b + 1], xmax[:, b:b + 1], MASKED / 2, None, ALU.is_gt).then_inc(x_dve, 1)

            def x_pT(j, b):
                for n in range(2):
                    dve.wait_ge(H["pT"], j * 4 + 2 * b + n + 1)
                    part = (slice(None), b, slice(n * 4, (n + 1) * 4))
                    low(pTl[part].rearrange("p c q -> p (c q)"), x_tr[n],
                        pTh[part].rearrange("p c q -> p (c q)")).then_inc(pT_copied, 1)

            def x_co(j, b):
                dve.wait_ge(co_ready, j * 2 + b + 1)
                dve.wait_ge(x_dve, j * 4 + 2 * b + 2)
                V.tensor_scalar(co[:, b, :], x_ctxo[b], xrec[:, b:b + 1], xval[:, b:b + 1], ALU.mult,
                                ALU.mult).then_inc(co_copied, 1)

            def x_coT(j, b):
                dve.wait_ge(H["coT"], j * 2 + b + 1)
                low(coTl[:, :, b, :], (x_mb if b else x_ma).rearrange("p (k q) -> p k q", k=KC),
                    coTh[:, :, b, :]).then_inc(coT_copied, 1)

            def x_oT(j):
                dve.wait_ge(H["oT"], j + 1)
                low(oTl[:].rearrange("p h t -> p (h t)"), x_ma, oTh[:].rearrange("p h t -> p (h t)")).then_inc(oT_copied, 1)

            def qk_low(j):
                dve.wait_ge(H["qk"], j + 1)
                low(qkl[:], qk_sb[:], qkh[:]).then_inc(LO["qk"], 1)

            def vo_low(j):
                dve.wait_ge(H["vo"], j + 1)
                low(vol[:], vo_sb[:], voh[:]).then_inc(LO["vo"], 1)

            def x_qT(j):
                dve.wait_ge(H["qT"], j + 1)
                low(qTl[:], x_ma, qTh[:]).then_inc(qT_copied, 1)

            def x_qp_(j):
                dve.wait_ge(H["qp"], j + 1)
                low(qpl[:].rearrange("p a b q -> p (a b q)"), x_qp, qph[:].rearrange("p a b q -> p (a b q)")).then_inc(qp_copied, 1)

            def x_head(j, prev, nxt):
                if nxt:
                    qk_low(j + 1)
                x_max(j, 0)
                if prev:
                    x_coT(j - 1, 1)
                x_max(j, 1)
                if prev:
                    x_oT(j - 1)
                x_recip(j, 0)
                x_pT(j, 0)
                if nxt:
                    x_qT(j + 1)
                x_recip(j, 1)
                x_pT(j, 1)
                x_co(j, 0)
                if nxt:
                    x_qp_(j + 1)
                vo_low(j)
                x_co(j, 1)
                x_coT(j, 0)

            def cT_low(b):
                dve.wait_ge(H["cT"], b + 1)
                low(cTl[:, b], cT[:, b], cTh[:, b]).then_inc(LO["cT"], 1)

            qk_low(0)
            copy_nT(1, PS[:, 1, :], None)
            cT_low(0)
            x_qT(0)
            x_qp_(0)
            cT_low(1)
            dve.wait_ge(L["mask"], 16)
            settled(V.tensor_scalar(madd, mask8, -MASKED, MASKED, ALU.mult, ALU.add))
            x_head(0, False, True)
            with dve.Fori(1, XKV - 1) as j:
                x_head(j, True, True)
            x_head(XKV - 1, True, False)
            x_coT(XKV - 1, 1)
            x_oT(XKV - 1)

            dve.wait_ge(wo_done, XKV)
            layer_norm(2, ACC, res[:], mid_ready, MIX_EPS)
            V.tensor_copy(xt[:], ACC).then_inc(xt_ready, 1)
            dve.wait_ge(L["vec"], 16)
            copy_nT(2, PS[:, 7, :], V_MIX)
            dve.wait_ge(H["in"], KD)
            low(ring_low[:, C_IN + 1, :], ring[:, C_IN + 1, :], high[:, 1, :]).then_inc(LO["in"], 1)
            dve.wait_ge(L["row"], 16)
            V.tensor_scalar(dts[:, 0, :], row[:, R_A:R_A + MH], A_LOG_TOP, None, ALU.min).then_inc(M["expA"], 1)
            dve.wait_ge(M["dt"], 1)
            settled(V.tensor_tensor(dts[:, 1, :], PS[:, 6, 0:MH], row[:, R_DT:R_DT + MH], ALU.add))
            settled(V.tensor_scalar(dts[:, 2, :], dts[:, 1, :], -1.0, None, ALU.mult))
            V.tensor_tensor(dts[:, 2, :], dts[:, 1, :], dts[:, 2, :], ALU.max).then_inc(M["abs"], 1)
            dve.wait_ge(M["expd"], 1)
            V.tensor_scalar(dts[:, 4, :], dts[:, 3, :], 1.0, None, ALU.add).then_inc(M["u"], 1)
            dve.wait_ge(M["u"], 1)
            settled(V.tensor_scalar(dts[:, 6, :], dts[:, 4, :], -1.0, None, ALU.add))
            settled(V.tensor_scalar(dts[:, 2, :], dts[:, 6, :], 0.0, None, ALU.is_equal))
            settled(V.tensor_tensor(dts[:, 6, :], dts[:, 6, :], dts[:, 2, :], ALU.add))
            settled(V.reciprocal(dts[:, 6, :], dts[:, 6, :]))
            dve.wait_ge(M["lnu"], 1)
            dve.wait_ge(M["A"], 1)
            settled(V.tensor_tensor(dts[:, 5, :], dts[:, 5, :], dts[:, 2, :], ALU.add))
            settled(V.tensor_tensor(dts[:, 5, :], dts[:, 5, :], dts[:, 6, :], ALU.mult))
            settled(V.tensor_tensor(dts[:, 5, :], dts[:, 5, :], dts[:, 3, :], ALU.mult))
            settled(V.scalar_tensor_tensor(out=dts[:, 1, :], in0=dts[:, 1, :], scalar=0.0, in1=dts[:, 5, :], op0=ALU.max,
                                           op1=ALU.add))
            settled(V.tensor_tensor(dts[:, 7, :], dts[:, 1, :], dts[:, 0, :], ALU.mult))
            settled(V.tensor_scalar(dts[:, 7, :], dts[:, 7, :], -1.0, DECAY_BOTTOM, ALU.mult, ALU.max))
            dve.wait_ge(s_const, 4)
            V.tensor_tensor(wdec[:], tri[:].rearrange("p (o t) -> p o t", o=1).to_broadcast([P, MH, T]),
                            dts[:, 7, :].rearrange("p (h o) -> p h o", o=1).to_broadcast([P, MH, T]),
                            ALU.mult).then_inc(M["wdec"], 1)
            for g, (rows_, c0, c1, _) in enumerate(CONV):
                dve.wait_ge(M["pre"], g + 1)
                for k in range(TAPS - 1):
                    for c in range(c0, c1):
                        acc = cacc[0:rows_, c, :].rearrange("p (b t) -> p b t", b=B)
                        w = V_TAP + c * TAPS + k
                        i = V.scalar_tensor_tensor(out=acc, in0=xpad[0:rows_, c, :, k:k + S], scalar=vec[0:rows_, w:w + 1],
                                                   in1=acc, op0=ALU.mult, op1=ALU.add)
                    if k < TAPS - 2:
                        settled(i)
                i.then_inc(M["conv"], 1)
            for g, (rows_, c0, c1, _) in enumerate(CONV):
                dve.wait_ge(M["csig"], g + 1)
                V.tensor_tensor(cact[0:rows_, c0:c1, :], cacc[0:rows_, c0:c1, :], csig[0:rows_, c0:c1, :],
                                ALU.mult).then_inc(M["cact"] if g else M["bcact"], 1)
            dve.wait_ge(M["g"], 1)
            V.tensor_tensor(gm[:], PS[:, 5, 0:P], tri[:], ALU.mult).then_inc(M["gm"], 1)
            dve.wait_ge(M["gm"], 1)
            dve.wait_ge(M["decay"], 4)
            V.tensor_tensor(dec[:], dec[:], gm[:].rearrange("p (o t) -> p o t", o=1).to_broadcast([P, MH, T]),
                            ALU.mult).then_inc(M["mdec"], 1)

            def x_times(dst, n, w):
                dve.wait_ge(M["xtok"], n + 1)
                return V.tensor_tensor(dst[:, n * 8:(n + 1) * 8, :], PS[:, 3 + n, :].rearrange("p (h d) -> p h d", h=8),
                                       w[:, n * 8:(n + 1) * 8].rearrange("p (h o) -> p h o", o=1).to_broadcast([P, 8, HP]),
                                       ALU.mult)

            for n in range(2):
                x_times(xdt, n, dts[:, 1, :]).then_inc(M["xdt"], 1)
            for n in range(2):
                settled(x_times(xD_, n, row[:, R_D:R_D + MH]))
            dve.wait_ge(M["zraw"], 1)
            V.tensor_tensor(zs[:], zs[:], PS[:, 1:3, :].rearrange("p a n -> p (a n)"), ALU.mult).then_inc(M["zsig"], 1)
            dve.wait_ge(M["zsig"], 1)
            for n in range(2):
                dve.wait_ge(M["y"], n + 1)
                h = slice(n * 512, (n + 1) * 512)
                settled(V.tensor_tensor(y_sb[:, h], PS[:, 6 + n, :], xD_[:, n * 8:(n + 1) * 8, :].rearrange("p h d -> p (h d)"),
                                        ALU.add))
                V.tensor_tensor(y_sb[:, h], y_sb[:, h], zs[:, h], ALU.mult).then_inc(M["yg"], 1)
            dve.wait_ge(M["yg"], 2)
            for n in range(2):
                dve.wait_ge(M["yT"], n + 1)
                V.tensor_tensor(yT[:, n * 4:(n + 1) * 4, :], PS[:, 3 + n, :].rearrange("p (c t) -> p c t", c=4),
                                vec[:, V_SSM + n * 4:V_SSM + (n + 1) * 4].rearrange("p (c o) -> p c o", o=1).to_broadcast([P, 4, T]),
                                ALU.mult).then_inc(M["yTs"], 1)
            mean_square(y_sb[:], ysq[:], 1)
            for c in range(C_W1, SLOTS):
                chunk_low(c)
            dve.wait_ge(rstd_ready, 3)
            dve.wait_ge(ring_used, C_OUT + 2)
            V.scalar_tensor_tensor(out=mid[:], in0=PS[:, 5, :], scalar=rs[:, 3:4], in1=res[:], op0=ALU.mult,
                                   op1=ALU.add).then_inc(mid_ready, 1)
            dve.wait_ge(mid_ready, 2)
            rms_norm(4, mid[:])
            copy_nT(3, PS[:, 6, :], V_MOE)

            dve.wait_ge(M["logit"], 1)
            settled(V.memset(rsc[:, 0, :], MASKED))
            settled(V.tensor_copy(rsc[:, 0, 0:E1], PS[:, 7, 0:E1]))
            settled(V.max(r8[:, 0:8], rsc[:, 0, 0:E1]))
            V.tensor_scalar(rsc[:, 1, 0:E1], rsc[:, 0, 0:E1], r8[:, 0:1], None, ALU.subtract).then_inc(M["rexp"], 1)
            settled(V.memset(r8[:, 2:8], MASKED))
            settled(V.match_replace(rsc[:, 2, 0:16], r8[:, 0:8], rsc[:, 0, 0:16], 2 * MASKED))
            settled(V.tensor_tensor(rsc[:, 3, 0:E1], rsc[:, 2, 0:E1], rsc[:, 0, 0:E1], ALU.is_lt))
            dve.wait_ge(M["rexp"], 2)
            settled(V.tensor_tensor_reduce(out=rsc[:, 1, 0:E1], in0=r8[:, 8:16], in1=rsc[:, 3, 0:E1], scale=1.0, scalar=0.0,
                                           op0=ALU.mult, op1=ALU.add, accum_out=wsum[:]))
            settled(V.reciprocal(wsum[:], wsum[:]))
            settled(V.tensor_scalar(cw[:, 0:E1], rsc[:, 1, 0:E1], wsum[:], None, ALU.mult))

            def hidden(s, par, w):
                dve.wait_ge(sig_ready, s + 1)
                V.scalar_tensor_tensor(out=h_act[:, par, :], in0=PS[:, 1 + par, :], scalar=w, in1=h_sig[:, par, :],
                                       op0=ALU.mult, op1=ALU.mult).then_inc(act_ready, 1)

            def hidden_T(s, par):
                dve.wait_ge(H["hT"], s + 1)
                low(hTl[:, par].rearrange("p c t -> p (c t)"), PS[:, 3 + par, :],
                    hTh[:, par].rearrange("p c t -> p (c t)")).then_inc(hT_ready, 1)

            def moe_step(s, t, w, i=0):
                if t >= 2:
                    hidden_T(s - 2, t % 2)
                for c in moe_next(t):
                    chunk_low(c, i)
                if t < STEPS1:
                    hidden(s, t % 2, w)

            for s in range(4):
                moe_step(s, s, cw[:, 0:1])
            with dve.Fori(1, E1 - 1) as e:
                for t in range(4):
                    moe_step(e * 4 + t, 4 + t, cw[:, bass.ds(e, 1)], e - 1)
            for s in range(STEPS1 - 4, STEPS1 + 2):
                moe_step(s, s, cw[:, E1 - 1:E1])

            dve.wait_ge(ring_used, C_ATT)
            layer_norm(5, ACC, res[:], mid_ready, FFN_EPS)
            V.tensor_copy(xt[:], ACC).then_inc(xt_ready, 1)
            copy_nT(4, PS[:, 7, :], V_LN1)
            chunk_low(C_ATT + 2)
            chunk_low(C_ATT + 3)
            dve.wait_ge(L["rope"], 16)

            def rotate(bank, par, read, done, n):
                src = bank.rearrange("p (h d) -> p h d", h=4)
                half = AD // 2

                def bc(a):
                    return a.rearrange("p (o d) -> p o d", o=1).to_broadcast([P, 4, a.shape[-1]])

                V.tensor_tensor(ra[:, par], src, bc(rp[:, 0, :]), ALU.mult)
                V.tensor_tensor(rb[:, par, :, 0:half], src[:, :, half:AD], bc(rp[:, 1, 0:half]), ALU.mult)
                V.tensor_tensor(rb[:, par, :, half:AD], src[:, :, 0:half], bc(rp[:, 1, half:AD]), ALU.mult).then_inc(read, 1)
                dve.wait_ge(read, n)
                V.tensor_tensor(rq[:, par], ra[:, par], rb[:, par], ALU.add).then_inc(done, 1)

            def a_rope(u):
                dve.wait_ge(ring_used, wq_chunk(u) + 1)
                if u == 1:
                    dve.wait_ge(A["kT"], 1)
                rotate(PS[:, 1 + u % 2, :], u % 2, A["ropes"], A["rope"], u + 1)

            def a_max(u):
                dve.wait_ge(A["s"], u + 1)
                for c in range(4):
                    i = V.tensor_tensor_reduce(out=asc[:, u % 2, c, :], in0=PS[:, 4 + u % 2, c * P:(c + 1) * P], in1=amask[:],
                                               scale=1.0, scalar=2 * MASKED, op0=ALU.add, op1=ALU.max,
                                               accum_out=amx[:, u % 2, c:c + 1])
                i.then_inc(A["max"], 1)
                dve.wait_ge(A["max"], u + 1)
                V.tensor_scalar(anb[:, u % 2, :], amx[:, u % 2, :], -(float(AD) ** -0.5), None, ALU.mult).then_inc(A["nb"], 1)

            def a_normalise(u):
                dve.wait_ge(A["exp"], u + 1)
                V.reciprocal(arc[:, u % 2, :], asm[:, u % 2, :]).then_inc(A["rec"], 1)
                dve.wait_ge(A["rec"], u + 1)
                V.tensor_tensor(apn[:, u % 2], apr[:, u % 2],
                                arc[:, u % 2, :].rearrange("p (h o) -> p h o", o=1).to_broadcast([P, 4, T]),
                                ALU.mult).then_inc(A["pn"], 1)

            def flat(a):
                return a.rearrange("p h t -> p (h t)")

            def a_copy_pT(u):
                dve.wait_ge(H["ap"], u + 1)
                low(flat(apTl[:]), PS[:, 6, :], flat(apTh[:])).then_inc(A["pTs"], 1)

            def a_copy_qT(u):
                dve.wait_ge(H["aq"], u + 1)
                low(flat(aqTl[:]), PS[:, 3, :], flat(aqTh[:])).then_inc(A["qTs"], 1)

            dve.wait_ge(ring_used, C_ATT + 1)
            rotate(PS[:, 4, :], 1, A["kv"], A["krope"], 1)
            for s in range(UNITS + A_LAG):
                if s == 0:
                    dve.wait_ge(H["kT"], 1)
                    low(flat(akTl[:]), PS[:, 6, :], flat(akTh[:])).then_inc(A["kTs"], 1)
                    dve.wait_ge(H["v"], 1)
                    low(flat(avl[:]), PS[:, 5, :], flat(avh[:])).then_inc(LO["v"], 1)
                if 1 <= s <= UNITS:
                    a_copy_qT(s - 1)
                if 2 <= s < UNITS + 2:
                    a_normalise(s - 2)
                if 1 <= s < UNITS - 1:
                    chunk_low(wq_chunk(s + 1))
                if s > UNITS:
                    chunk_low(C_FFN + s - UNITS - 1)
                if s < UNITS:
                    a_rope(s)
                if 2 <= s < UNITS + 2:
                    a_copy_pT(s - 2)
                if 1 <= s <= UNITS:
                    a_max(s - 1)

            dve.wait_ge(ring_used, C_FFN)
            V.tensor_copy(mid[:], ACC).then_inc(mid_ready, 1)
            dve.wait_ge(mid_ready, 4)
            rms_norm(6, mid[:])
            copy_nT(5, PS[:, 6, :], V_LN2)

            dve.wait_ge(A["rsig"], 1)
            settled(V.tensor_tensor(rsc[:, 1, :], rsc[:, 0, :], row[:, R_EB:R_EB + E2], ALU.add))
            settled(V.max(r8[:, 0:8], rsc[:, 1, :]))
            settled(V.match_replace(rsc[:, 2, :], r8[:, 0:8], rsc[:, 1, :], 2 * MASKED))
            settled(V.tensor_tensor(rsc[:, 3, :], rsc[:, 2, :], rsc[:, 1, :], ALU.is_lt))
            settled(V.tensor_tensor_reduce(out=rsc[:, 1, :], in0=rsc[:, 0, :], in1=rsc[:, 3, :], scale=1.0, scalar=0.0,
                                           op0=ALU.mult, op1=ALU.add, accum_out=wsum[:]))
            settled(V.reciprocal(wsum[:], wsum[:]))
            settled(V.tensor_scalar(cw[:, 0:E2], rsc[:, 1, :], wsum[:], None, ALU.mult))

            def gated(s, par, w):
                dve.wait_ge(gsig_ready, s + 1)
                V.scalar_tensor_tensor(out=h_sig[:, par, FF2:2 * FF2], in0=PS[:, 1 + par, 0:FF2], scalar=w,
                                       in1=h_sig[:, par, 0:FF2], op0=ALU.mult, op1=ALU.mult).then_inc(gs_ready, 1)
                dve.wait_ge(gs_ready, s + 1)
                V.tensor_tensor(h_act[:, par, 0:FF2], PS[:, 1 + par, FF2:2 * FF2], h_sig[:, par, FF2:2 * FF2],
                                ALU.mult).then_inc(a_ready, 1)

            def gated_T(s, par):
                dve.wait_ge(H["aT"], s + 1)
                low(hTl[:, par, 0:2].rearrange("p c t -> p (c t)"), PS[:, 3 + par, 0:2 * P],
                    hTh[:, par, 0:2].rearrange("p c t -> p (c t)")).then_inc(aT_ready, 1)

            def ffn_step(s, t, w, i=0):
                if t >= 2:
                    gated_T(s - 2, t % 2)
                for c in ffn_next(t):
                    chunk_low(c, i)
                if t < STEPS2:
                    gated(s, t % 2, w)

            for s in range(5):
                ffn_step(s, s, cw[:, s:s + 1])
            with dve.Fori(0, (STEPS2 - 5) // 4 - 1) as i:
                for t in range(4):
                    ffn_step(i * 4 + 5 + t, 5 + t, cw[:, bass.ds(i * 4 + 5 + t, 1)], i)
            for s in range(STEPS2 - 4, STEPS2 + 2):
                ffn_step(s, s, cw[:, s:s + 1] if s < STEPS2 else None)
            dve.wait_ge(ring_used, CHUNKS)
            V.tensor_copy(mid[:], ACC).then_inc(mid_ready, 1)


def kernel(**inputs):
    import numpy as np
    import concourse.bacc as bacc
    from concourse import mybir as mb
    from concourse.bass_utils import run_bass_kernel_spmd

    a = {k: np.asarray(v) for k, v in inputs.items()}
    m, f, xa = "L0_attn_", "L0_ffn_", "L0_xattn_"

    def pieces(w, n):
        k, cols = w.shape
        return w.reshape(k // P, P, cols // n, n).transpose(2, 1, 0, 3).reshape(cols // n, P, -1)

    def rows_of(w, n):
        k, cols = w.shape
        return w.reshape(k // (P * n), n, P, cols).transpose(0, 2, 1, 3).reshape(k // (P * n), P, n * cols)

    def column(v):
        return v.reshape(-1, P).T

    ctx = a["ctx_1024"]
    wk = a[xa + "Wk"].reshape(DC, XKV, XD).transpose(1, 2, 0)
    qk = np.concatenate([pieces(a[xa + "Wq"], 256), wk], axis=2)
    vo = np.concatenate([pieces(a[xa + "Wv"], XD), rows_of(a[xa + "Wo"], 2)], axis=2)
    ipw = a[m + "in_proj_w"].T

    def conv_pieces(v):
        n = v.shape[1]
        t = np.zeros((P, CC, n), np.float32)
        t[:, :XC] = v[:DI].reshape(XC, P, n).transpose(1, 0, 2)
        t[:DS, XC] = v[DI:DI + DS]
        t[:DS, XC + 1] = v[DI + DS:]
        return t.reshape(P, CC * n)

    vecs = np.concatenate([
        column(a[m + "norm_mamba_w"]), column(a[m + "norm_moe_w"]), column(a[m + "ssm_norm_w"]),
        column(a[f + "ln1_w"]), column(a[f + "ln2_w"]),
        conv_pieces(a[m + "conv_w"]), conv_pieces(a[m + "conv_b"][:, None]),
        pieces(a[m + "gate_w"].T, E1)[0], pieces(a[f + "Wr"], E2)[0],
        pieces(ipw[:, 2 * DI:], BCDT)[0]], axis=1)
    rows = np.concatenate([a[m + "dt_bias"], a[m + "A_log"], a[m + "D"], a[f + "expert_bias"]])[None]
    inv = (1.0 / 10000.0 ** (np.arange(0, AD, 2, dtype=np.float32) / AD)).astype(np.float32)
    ang = (np.arange(S, dtype=np.float32)[:, None] * inv[None]).astype(np.float32)
    ang = np.concatenate([ang, ang])
    rope = np.stack([np.concatenate([np.cos(ang), np.cos(ang)], 1), np.concatenate([-np.sin(ang), np.sin(ang)], 1)], 1)

    w1 = a[m + "w1"].reshape(E1, N1, 512, KD, P).transpose(0, 1, 4, 3, 2).reshape(STEPS1, P, CHUNK)
    w2 = a[m + "w2"].reshape(E1, D, N1, 4, P).transpose(0, 2, 4, 3, 1).reshape(STEPS1, P, CHUNK)
    g = np.concatenate([a[f + "Wg"], a[f + "Wsg"][None]]).reshape(STEPS2, KD, P, FF2)
    u = np.concatenate([a[f + "Wu"], a[f + "Wsu"][None]]).reshape(STEPS2, KD, P, FF2)
    gu = np.stack([g, u], axis=3).transpose(0, 2, 1, 3, 4).reshape(STEPS2, P, CHUNK)
    dn = np.concatenate([a[f + "Wd"], a[f + "Wsd"][None]]).reshape(STEPS2, 2, P, D).transpose(0, 2, 1, 3).reshape(STEPS2, P, 2 * D)
    arrays = {
        "x": a["x"].reshape(T, D),
        "mask": a["mask_BxS2_bf1"].reshape(1, B * S2).view(np.uint8),
        "ctx": ctx.reshape(B, SC, P, DC).transpose(2, 0, 1, 3),
        "ctxT": ctx.transpose(0, 2, 1).reshape(B, KC, P, S2).transpose(2, 0, 1, 3),
        "qk": qk, "vo": vo, "vecs": vecs, "rows": rows, "rope": rope,
        "in_w": ipw[:, :2 * DI].reshape(KD, P, 2 * DI),
        "out_w": rows_of(a[m + "out_proj_w"].T, 4),
        "w1": w1, "w2": w2,
        "wkv": np.concatenate([pieces(a[f + "Wk"], 512), pieces(a[f + "Wv"], 512)]),
        "wq": pieces(a[f + "Wq"], 512), "wo": rows_of(a[f + "Wo"], 4),
        "gu": gu, "dn": dn,
    }
    arrays = {"in_" + k: np.ascontiguousarray(v) for k, v in arrays.items()}
    nc = bacc.Bacc("TRN2", target_bir_lowering=False, num_devices=1)
    args = [nc.dram_tensor(k, v.shape, mb.dt.from_np(v.dtype), kind="ExternalInput").ap() for k, v in arrays.items()]
    out = nc.dram_tensor("out_x", (T, D), F32, kind="ExternalOutput").ap()
    build(nc, *args, out)
    r = run_bass_kernel_spmd(nc, [arrays], core_ids=[0])
    return r.results[0]["out_x"].reshape(B, S, D)
```

```python
from contextlib import ExitStack

import concourse.bass as bass
from concourse import mybir

F32 = mybir.dt.float32
F32R = mybir.dt.float32r
U8 = mybir.dt.uint8
ALU = mybir.AluOpType
ACT = mybir.ActivationFunctionType

P = 128
B, S, D = 2, 64, 512
T = B * S
KD = D // P
S2, DC = 1024, 256
KC, SC = DC // P, S2 // P
XKV, XD = 8, 128
DI, DS, MH, HP = 1024, 64, 16, 64
XC = DI // P
CC = XC + 2
TAPS = 4
PAD = S + TAPS - 1
E1, FF1 = 8, 2048
N1 = FF1 // 512
STEPS1 = E1 * N1
AH, AKV, AD = 32, 4, 128
UNITS = AH // 4
A_LAG = 3
E2, FF2 = 32, 256
STEPS2 = E2 + 1
CHUNK = 2048
SLOTS = 8
HIGHS = 4
QKW, VOW = KD * 2 * XD + DC, KC * XD + 2 * D
MASKED = -1.0e30
LN_EPS, MIX_EPS, FFN_EPS = 1e-5, 1e-6, 1e-5
A_LOG_TOP, DECAY_BOTTOM = 80.0, -120.0

IN_ORDER = (2, 3, 0, 1)

C_IN, C_W1 = 0, KD
C_ATT = C_W1 + 2 * STEPS1
C_FFN = C_ATT + 2 + 2 * UNITS
CHUNKS = C_FFN + 2 * STEPS2

CONV = ((DS, XC, CC, 5), (P, 0, 4, 3), (P, 4, XC, 4))

V_MIX, V_MOE, V_SSM, V_LN1, V_LN2 = 0, KD, 2 * KD, 2 * KD + XC, 3 * KD + XC
V_TAP = 4 * KD + XC
V_CB = V_TAP + CC * TAPS
V_GATE = V_CB + CC
V_ROUTE = V_GATE + KD * E1
V_BCDT = V_ROUTE + KD * E2
BCDT = 2 * DS + MH
VECS = V_BCDT + KD * BCDT
R_DT, R_A, R_D, R_EB = 0, MH, 2 * MH, 3 * MH
ROWS = 3 * MH + E2


def up_chunk(base, s, lag=2):
    return base + s if isinstance(s, int) and s < lag else base - lag + 2 * s


def down_chunk(base, s, steps, lag=2):
    return base + steps + s if isinstance(s, int) and s >= steps - lag else base + lag + 1 + 2 * s


def wq_chunk(u):
    return up_chunk(C_ATT + 2, u, A_LAG)


def wo_chunk(u):
    return down_chunk(C_ATT + 2, u, UNITS, A_LAG)


def split_count(c):
    apart = [*range(C_IN, C_IN + KD), *(wo_chunk(u) for u in range(UNITS))]
    return c + 1 - sum(r < c for r in apart)


def chunk_width(c):
    half = c >= C_FFN + 3 and ((c - C_FFN) % 2 == 1 or c >= CHUNKS - 2)
    return CHUNK // 2 if half else CHUNK


def up_ahead(base, t, steps):
    return [up_chunk(base, t + 2)] if 1 <= t < steps - 2 else []


def build(nc, x, mask, ctx, ctxT, qk, vo, vecs, rows, rope, in_w, out_w, w1, w2, wkv, wq, wo, gu, dn, out):
    stack = ExitStack()
    with stack:
        def sem(name):
            return stack.enter_context(nc.semaphore(name))

        def sb(name, shape, dt=F32, scope=stack):
            return scope.enter_context(nc.sbuf_tensor(name, shape, dt))

        PS = stack.enter_context(nc.psum_tensor("PS", [P, 8, 512], F32))

        with ExitStack() as scope:
            ring = sb("ring", [P, SLOTS, CHUNK], scope=scope)
            spare = sb("spare", [P, HIGHS, CHUNK], scope=scope)
        ring_low = sb("ring_low", [P, SLOTS, CHUNK], F32R)
        high = sb("high", [P, HIGHS, CHUNK], F32R)
        vec = sb("vec", [P, VECS])
        row = sb("row", [P, ROWS])
        ident = sb("ident", [P, P])
        tri = sb("tri", [P, P])
        later = sb("later", [P, P])
        amask = sb("amask", [P, P])
        xt = sb("xt", [P, D])
        res = sb("res", [P, D])
        mid = sb("mid", [P, D])
        nrm = sb("nrm", [P, D])
        junk = sb("junk", [P, D])
        nT = sb("nT", [P, KD, P])
        nTh, nTl = sb("nTh", [P, KD, P], F32R), sb("nTl", [P, KD, P], F32R)
        moments = sb("moments", [P, 2])
        var2 = sb("var2", [P, 2])
        ms = sb("ms", [P, 2])
        log_ = sb("log_", [P, 2])
        rs = sb("rs", [P, 4])
        wsum = sb("wsum", [P, 1])
        bnst = sb("bnst", [P, 6])
        epsc = sb("epsc", [P, 2])
        cw = sb("cw", [P, E2 + 1])
        r8 = sb("r8", [P, 16])
        rsc = sb("rsc", [P, 4, E2])
        xpad = sb("xpad", [P, CC, B, PAD])

        rp = sb("rp", [P, 2, AD])
        rpn = sb("rpn", [P, 2, AD])

        with ExitStack() as scope:
            h_silu = sb("h_silu", [P, 2, 512], scope=scope)
            h_act = sb("h_act", [P, 2, 512], scope=scope)
            hTh, hTl = sb("hTh", [P, 2, 4, P], F32R, scope), sb("hTl", [P, 2, 4, P], F32R, scope)

        with ExitStack() as scope:
            with ExitStack() as raw:
                cT = sb("cT", [P, B, KC, S2], scope=raw)
                cx = sb("cx", [P, B, SC, DC], scope=raw)
                qk_sb, vo_sb = sb("qk_sb", [P, QKW], scope=raw), sb("vo_sb", [P, VOW], scope=raw)
            cTl = sb("cTl", [P, B, KC, S2], F32R, scope)
            cxl = sb("cxl", [P, B, SC, DC], F32R, scope)
            qkl, vol = sb("qkl", [P, QKW], F32R, scope), sb("vol", [P, VOW], F32R, scope)
            cTh = high[:, 0:2, :].rearrange("p b (k s) -> p b k s", b=B, k=KC)
            madd = spare[:, 2, :].rearrange("p (b s) -> p b s", b=B)
            mask8 = spare[:, 3, 0:B * S2 // 4].bitcast(U8).rearrange("p (b s) -> p b s", b=B)
            pTh = ring_low[:, 4, :].rearrange("p (b c q) -> p b c q", b=B, c=SC)
            pTl = ring_low[:, 5, :].rearrange("p (b c q) -> p b c q", b=B, c=SC)
            cxh = ring_low[:, 6:8, :].rearrange("p b (c n) -> p b c n", b=B, c=SC)
            pr = sb("pr", [P, B, S2], scope=scope)
            qkh, voh = sb("qkh", [P, QKW], F32R, scope), sb("voh", [P, VOW], F32R, scope)
            q_sb = sb("q_sb", [P, 2 * XD], scope=scope)
            qTh, qTl = sb("qTh", [P, 2 * T], F32R, scope), sb("qTl", [P, 2 * T], F32R, scope)
            qph, qpl = sb("qph", [P, KC, B, P], F32R, scope), sb("qpl", [P, KC, B, P], F32R, scope)
            co = sb("co", [P, B, DC], scope=scope)
            coTh, coTl = sb("coTh", [P, KC, B, P], F32R, scope), sb("coTl", [P, KC, B, P], F32R, scope)
            oTh, oTl = sb("oTh", [P, 2, T], F32R, scope), sb("oTl", [P, 2, T], F32R, scope)
            xmax = sb("xmax", [P, B], scope=scope)
            nbias = sb("nbias", [P, B], scope=scope)
            xsum = sb("xsum", [P, B], scope=scope)
            xrec = sb("xrec", [P, B], scope=scope)
            xval = sb("xval", [P, B], scope=scope)
            held = sb("held", [P, 1], scope=scope)

        with ExitStack() as scope:
            out_sb = sb("out_sb", [P, 2, CHUNK], scope=scope)
            zs = sb("zs", [P, DI], scope=scope)
            cacc = sb("cacc", [P, CC, T], scope=scope)
            cact = sb("cact", [P, CC, T], scope=scope)
            xdt = sb("xdt", [P, MH, HP], scope=scope)
            xD_ = sb("xD_", [P, MH, HP], scope=scope)
            dts = sb("dts", [P, 8, MH], scope=scope)
            wdec = sb("wdec", [P, MH, T], scope=scope)
            dec = sb("dec", [P, MH, T], scope=scope)
            gm = sb("gm", [P, P], scope=scope)
            y_sb = sb("y_sb", [P, DI], scope=scope)
            ysq = sb("ysq", [P, DI], scope=scope)
            yT = sb("yT", [P, XC, P], scope=scope)

        with ExitStack() as scope:
            ra = sb("ra", [P, 2, 4, AD], scope=scope)
            rb = sb("rb", [P, 2, 4, AD], scope=scope)
            rq = sb("rq", [P, 2, 4, AD], scope=scope)
            aqTh, aqTl = sb("aqTh", [P, 4, T], F32R, scope), sb("aqTl", [P, 4, T], F32R, scope)
            akTh, akTl = sb("akTh", [P, AKV, T], F32R, scope), sb("akTl", [P, AKV, T], F32R, scope)
            avh, avl = sb("avh", [P, AKV, AD], F32R, scope), sb("avl", [P, AKV, AD], F32R, scope)
            asc = sb("asc", [P, 2, 4, T], scope=scope)
            apr = sb("apr", [P, 2, 4, T], scope=scope)
            apn = sb("apn", [P, 2, 4, T], scope=scope)
            apTh, apTl = sb("apTh", [P, 4, T], F32R, scope), sb("apTl", [P, 4, T], F32R, scope)
            aoT = sb("aoT", [P, 4, T], scope=scope)
            amx = sb("amx", [P, 2, 4], scope=scope)
            anb = sb("anb", [P, 2, 4], scope=scope)
            asm = sb("asm", [P, 2, 4], scope=scope)
            arc = sb("arc", [P, 2, 4], scope=scope)

        ACC = PS[:, 0, :]
        x_scores = [PS[:, 1:3, :].rearrange("p a n -> p (a n)"), PS[:, 3:5, :].rearrange("p a n -> p (a n)")]
        x_ctxo = [PS[:, 1, 0:DC], PS[:, 3, 0:DC]]
        x_qp = PS[:, 2, :]
        x_tr = [PS[:, 5, :], PS[:, 6, :]]
        x_ma, x_mb = PS[:, 7, 0:256], PS[:, 7, 256:512]

        L = {n: sem("ld_" + n) for n in ("x", "qk", "vo", "mask", "cT0", "cT1", "cx0", "cx1", "vec", "row", "rope", "out")}
        ring_loaded = [sem(f"ring_loaded{i}") for i in range(SLOTS)]
        ring_used = sem("ring_used")
        hi_ready = sem("hi_ready")
        lo_ready = sem("lo_ready")
        H = {n: sem("hi_" + n) for n in ("qk", "vo", "cT", "cx", "qT", "qp", "pT", "coT", "oT", "hT", "aT", "kT", "in",
                                         "v", "aq", "ap")}
        LO = {n: sem("lo_" + n) for n in ("qk", "vo", "cT", "cx", "v", "in", "in1")}
        s_out = sem("s_out")
        s_const = sem("s_const")
        s_pool = sem("s_pool")
        s_dve = sem("s_dve")
        s_act = sem("s_act")
        norm_ready = sem("norm_ready")
        nT_made = sem("nT_made")
        nT_ready = sem("nT_ready")
        var_ready = sem("var_ready")
        rstd_ready = sem("rstd_ready")
        xt_ready = sem("xt_ready")
        mid_ready = sem("mid_ready")
        sc_ready, s_max, nb_ready, exp_done = sem("sc_ready"), sem("s_max"), sem("nb_ready"), sem("exp_done")
        q_ready, q_copied = sem("q_ready"), sem("q_copied")
        qT_ready, qT_copied = sem("qT_ready"), sem("qT_copied")
        qp_ready, qp_copied = sem("qp_ready"), sem("qp_copied")
        pT_ready, pT_copied = sem("pT_ready"), sem("pT_copied")
        co_ready, co_copied = sem("co_ready"), sem("co_copied")
        coT_ready, coT_copied = sem("coT_ready"), sem("coT_copied")
        oT_ready, oT_copied, wo_done = sem("oT_ready"), sem("oT_copied"), sem("wo_done")
        x_dve = sem("x_dve")
        M = {n: sem("m_" + n) for n in ("dt", "xm", "xc", "pre", "bcact", "xT", "bcT", "conv", "cact", "g", "gm",
                                        "expA", "abs", "expd", "u", "lnu", "wdec", "dsum", "decay", "xtok",
                                        "zsilu", "A", "mdec", "y", "outp", "yg", "yT", "yTs", "logit", "rexp")}
        silu_ready, act_ready, hT_made, hT_ready = (sem(n) for n in ("silu_ready", "act_ready", "hT_made", "hT_ready"))
        gsilu_ready, a_ready, aT_made, aT_ready = (sem(n) for n in ("gsilu_ready", "a_ready", "aT_made", "aT_ready"))
        A = {n: sem("a_" + n) for n in ("kv", "krope", "kT", "kTs", "ropes", "rope", "qT", "qTs", "s", "max", "nb", "exp",
                                        "rec", "pn", "pT", "pTs", "o", "os", "logit", "rsig")}

        def wait_chunk(eng, slot, lap):
            eng.wait_ge(ring_loaded[slot], lap * 16 + 16)

        block = stack.enter_context(nc.Block())

        @block.sync
        def _(sp):
            def load(dst, src, s):
                sp.dma_start(dst, src).then_inc(s, 16)

            def ring_load(c, src, lap=None, free=None):
                slot = c % SLOTS
                if c >= SLOTS:
                    sp.wait_ge(ring_used, (c - SLOTS + 1) if free is None else free)
                n = src.shape[-1]
                sp.dma_start(ring[:, slot, 0:n], src).then_inc(ring_loaded[slot], 16)

            load(xt[:], x, L["x"])
            load(row[:], rows.to_broadcast([P, ROWS]), L["row"])
            load(qk_sb[:], qk[0], L["qk"])
            load(mask8[:].rearrange("p b s -> p (b s)"), mask.to_broadcast([P, B * S2]), L["mask"])
            load(cT[:, 0], ctxT[:, 0], L["cT0"])
            load(cT[:, 1], ctxT[:, 1], L["cT1"])
            load(cx[:, 0], ctx[:, 0], L["cx0"])
            load(cx[:, 1], ctx[:, 1], L["cx1"])
            load(vo_sb[:], vo[0], L["vo"])
            load(vec[:], vecs, L["vec"])
            load(rp[:], rope, L["rope"])
            sp.wait_ge(qp_ready, 1)
            load(qk_sb[:], qk[1], L["qk"])
            stream = [in_w[k] for k in range(KD)]
            stream += [w1[0], w1[1], w1[2], w2[0], w1[3], w2[1]]
            for c in range(SLOTS // 2):
                ring_load(c, stream[c])
            with sp.Fori(1, XKV - 1) as j:
                sp.wait_ge(qp_ready, j + 1)
                load(qk_sb[:], qk[bass.ds(j + 1, 1)].rearrange("a p n -> p (a n)"), L["qk"])
                sp.wait_ge(wo_done, j)
                load(vo_sb[:], vo[bass.ds(j, 1)].rearrange("a p n -> p (a n)"), L["vo"])
            sp.wait_ge(wo_done, XKV - 1)
            load(vo_sb[:], vo[XKV - 1], L["vo"])
            sp.wait_ge(co_ready, 2 * XKV)
            for c in range(SLOTS // 2, SLOTS):
                ring_load(c, stream[c])
            sp.wait_ge(wo_done, XKV)
            load(out_sb[:, 0], out_w[0], L["out"])
            load(out_sb[:, 1], out_w[1], L["out"])
            for c in range(SLOTS, len(stream)):
                ring_load(c, stream[c])
            with sp.Fori(1, E1) as e:
                for t in range(N1):
                    c = up_chunk(C_W1, 4 + t)
                    ring_load(c, w1[bass.ds(e * 4 + t, 1)].rearrange("a p n -> p (a n)"),
                              free=(e - 1) * 8 + (c - SLOTS + 1))
                    ring_load(c + 1, w2[bass.ds(e * 4 + t - 2, 1)].rearrange("a p n -> p (a n)"),
                              free=(e - 1) * 8 + (c - SLOTS + 2))
            stream = [(down_chunk(C_W1, s, STEPS1), w2[s]) for s in (STEPS1 - 2, STEPS1 - 1)]
            stream += [(C_ATT, wkv[0]), (C_ATT + 1, wkv[1])]
            for s in range(UNITS + A_LAG):
                if s < UNITS:
                    stream.append((wq_chunk(s), wq[s]))
                if s >= A_LAG:
                    stream.append((wo_chunk(s - A_LAG), wo[s - A_LAG]))
            for s in range(5):
                stream.append((up_chunk(C_FFN, s), gu[s]))
                if s >= 2:
                    stream.append((down_chunk(C_FFN, s - 2, STEPS2), dn[s - 2]))
            for c, src in stream:
                ring_load(c, src)
            with sp.Fori(0, (STEPS2 - 5) // 4) as i:
                for t in range(4):
                    c = up_chunk(C_FFN, 5 + t)
                    ring_load(c, gu[bass.ds(i * 4 + 5 + t, 1)].rearrange("a p n -> p (a n)"),
                              free=i * 8 + (c - SLOTS + 1))
                    ring_load(c + 1, dn[bass.ds(i * 4 + 3 + t, 1)].rearrange("a p n -> p (a n)"),
                              free=i * 8 + (c - SLOTS + 2))
            for s in (STEPS2 - 2, STEPS2 - 1):
                ring_load(down_chunk(C_FFN, s, STEPS2), dn[s])
            sp.wait_ge(mid_ready, 5)
            sp.dma_start(out, mid[:]).then_inc(s_out, 16)
            sp.wait_ge(s_out, 16)

        @block.gpsimd
        def _(pool):
            nc.gpsimd.memset(ident[:], 0.0).then_inc(s_pool, 1)
            nc.gpsimd.memset(tri[:], 1.0).then_inc(s_pool, 1)
            nc.gpsimd.memset(later[:], 1.0).then_inc(s_pool, 1)
            nc.gpsimd.memset(amask[:], 0.0).then_inc(s_pool, 1)
            nc.gpsimd.memset(xpad[:], 0.0).then_inc(s_pool, 1)
            nc.gpsimd.memset(epsc[:, 0:1], MIX_EPS).then_inc(s_pool, 1)
            nc.gpsimd.memset(epsc[:, 1:2], FFN_EPS).then_inc(s_pool, 1)
            pool.wait_ge(s_pool, 7)

            def select(m, cmp, fill, base, pattern, mul):
                return nc.gpsimd.affine_select(out=m, in_=m, compare_op=cmp, fill=fill, base=base,
                                               pattern=pattern, channel_multiplier=mul)

            select(ident[:], ALU.not_equal, 1.0, 0, [[-1, P]], 1).then_inc(s_const, 1)
            select(later[:], ALU.is_gt, 0.0, 0, [[-1, P]], 1).then_inc(s_const, 1)
            select(tri[:], ALU.is_ge, 0.0, 0, [[1, P]], -1).then_inc(s_pool, 1)
            select(amask[:], ALU.is_ge, MASKED, 0, [[-1, P]], 1).then_inc(s_pool, 1)
            pool.wait_ge(s_pool, 9)
            select(tri[:, S:T], ALU.is_ge, 0.0, -S, [[0, S]], 1).then_inc(s_const, 1)
            select(amask[:, 0:S], ALU.is_ge, MASKED, S - 1, [[0, S]], -1).then_inc(s_const, 1)
            for b in range(B):
                pool.wait_ge(H["cx"], b + 1)
                nc.gpsimd.tensor_tensor(cxl[:, b], cx[:, b], cxh[:, b].bitcast(F32), ALU.subtract).then_inc(LO["cx"], 1)
            for n, k in enumerate(IN_ORDER[:3]):
                pool.wait_ge(H["in"], n + 1)
                nc.gpsimd.tensor_tensor(ring_low[:, C_IN + k, :], ring[:, C_IN + k, :], high[:, k, :].bitcast(F32),
                                        ALU.subtract).then_inc(LO["in"], 1)

        @block.tensor
        def _(pe):
            mm = nc.tensor.matmul

            def mm3(dst, still, moving, start, stop, **kw):
                (sh, sl), (mh, ml) = still, moving
                mm(dst, sl, mh, start=start, stop=False, **kw)
                mm(dst, sh, mh, start=False, stop=False, **kw)
                return mm(dst, sh, ml, start=False, stop=stop, **kw)

            def nT_(k):
                return nTh[:, k, :], nTl[:, k, :]

            def chunk_part(c, a, b):
                return high[:, c % HIGHS, a:b], ring_low[:, c % SLOTS, a:b]

            def to_features(bank, src, ready, n):
                pe.wait_ge(ready, n)
                for k in range(KD):
                    i = nc.tensor.transpose(bank[:, k * P:(k + 1) * P], src[:, k * P:(k + 1) * P], ident[:])
                i.then_inc(nT_made, 1)

            def keep_warm(n, bank):
                for _ in range(n):
                    mm(bank[:, 0:P], ident[:], ident[:], start=True, stop=True)

            def x_q(j):
                pe.wait_ge(LO["qk"], j + 1)
                for k in range(KD):
                    w = qkh[:, k * 256:(k + 1) * 256], qkl[:, k * 256:(k + 1) * 256]
                    i = mm3(x_scores[0][:, 0:256], nT_(k), w, start=(k == 0), stop=(k == KD - 1))
                i.then_inc(q_ready, 1)

            def x_qT(j):
                pe.wait_ge(q_copied, j + 1)
                for h in range(2):
                    i = nc.tensor.transpose(x_ma[:, h * P:(h + 1) * P], q_sb[:, h * P:(h + 1) * P], ident[:])
                i.then_inc(qT_ready, 1)

            def x_qproj(j):
                pe.wait_ge(qT_copied, j + 1)
                for kc in range(KC):
                    w = slice(KD * 256 + kc * P, KD * 256 + (kc + 1) * P)
                    i = mm3(x_qp[:, kc * 256:(kc + 1) * 256].rearrange("p (b h q) -> p b h q", b=B, h=2),
                            (qkh[:, w], qkl[:, w]),
                            [a[:].rearrange("p (h b q) -> p b h q", b=B, h=2) for a in (qTh, qTl)], start=True, stop=True)
                i.then_inc(qp_ready, 1)

            def x_score(j, b):
                for n in range(2):
                    for kc in range(KC):
                        part = slice(n * 512, (n + 1) * 512)
                        i = mm3(x_scores[b][:, part], (qph[:, kc, b, :], qpl[:, kc, b, :]),
                                (cTh[:, b, kc, part], cTl[:, b, kc, part]), start=(kc == 0), stop=(kc == KC - 1))
                i.then_inc(sc_ready, 1)

            def x_probT(j, b):
                pe.wait_ge(exp_done, j * 2 + b + 1)
                if b or not isinstance(j, int) or j:
                    pe.wait_ge(pT_copied, j * 4 + 2 * b)
                for n in range(2):
                    for c in range(4):
                        s = n * 4 + c
                        i = nc.tensor.transpose(x_tr[n][:, c * P:(c + 1) * P], pr[:, b, s * P:(s + 1) * P], ident[:])
                    i.then_inc(pT_ready, 1)

            def x_mix(j, b, half):
                for s in range(half * 4, half * 4 + 4):
                    if s % 4 == 0:
                        pe.wait_ge(pT_copied, j * 4 + 2 * b + 1 + s // 4)
                    i = mm3(x_ctxo[b], (pTh[:, b, s, :], pTl[:, b, s, :]), (cxh[:, b, s, :], cxl[:, b, s, :]), start=(s == 0), stop=(s == SC - 1))
                if half:
                    i.then_inc(co_ready, 1)

            def x_coT(j, b):
                pe.wait_ge(co_copied, j * 2 + b + 1)
                dst = x_mb if b else x_ma
                for kc in range(KC):
                    i = nc.tensor.transpose(dst[:, kc * P:(kc + 1) * P], co[:, b, kc * P:(kc + 1) * P], ident[:])
                i.then_inc(coT_ready, 1)

            def x_value(j):
                pe.wait_ge(coT_copied, j * 2 + 2)
                pe.wait_ge(LO["vo"], j + 1)
                for kc in range(KC):
                    i = mm3(x_ma.rearrange("p (h b q) -> p h b q", h=2, b=B),
                            (voh[:, kc * P:(kc + 1) * P], vol[:, kc * P:(kc + 1) * P]),
                            [a[:, kc].rearrange("p b (h q) -> p h b q", h=2) for a in (coTh, coTl)], start=(kc == 0), stop=(kc == KC - 1))
                i.then_inc(oT_ready, 1)

            def x_out(j, last=False):
                pe.wait_ge(oT_copied, j + 1)
                for h in range(2):
                    w = slice(KC * P + h * D, KC * P + (h + 1) * D)
                    i = mm3(ACC, (oTh[:, h, :], oTl[:, h, :]), (voh[:, w], vol[:, w]), start=False,
                            stop=last and h == 1, skip_group_check=True)
                i.then_inc(wo_done, 1)

            def x_head(j, prev, nxt):
                pe.wait_ge(qp_copied, j + 1)
                if not prev:
                    pe.wait_ge(LO["cT"], 1)
                x_score(j, 0)
                if prev:
                    pe.wait_ge(coT_copied, j * 2 - 1)
                    x_coT(j - 1, 1)
                else:
                    pe.wait_ge(LO["cT"], 2)
                x_score(j, 1)
                if prev:
                    x_value(j - 1)
                else:
                    keep_warm(3, PS[:, 7, :])
                    x_probT(j, 0)
                    keep_warm(9, PS[:, 7, :])
                if nxt:
                    pe.wait_ge(s_max, j * 2 + 1)
                    x_q(j + 1)
                if prev:
                    x_probT(j, 0)
                    x_out(j - 1)
                if nxt:
                    x_qT(j + 1)
                if not prev:
                    pe.wait_ge(LO["cx"], 1)
                x_mix(j, 0, 0)
                x_probT(j, 1)
                x_mix(j, 0, 1)
                if nxt:
                    x_qproj(j + 1)
                if not prev:
                    pe.wait_ge(LO["cx"], 2)
                x_mix(j, 1, 0)
                x_mix(j, 1, 1)
                x_coT(j, 0)

            pe.wait_ge(s_const, 4)
            keep_warm(10, PS[:, 5, :])
            to_features(PS[:, 1, :], nrm, norm_ready, 1)
            mm(ACC, ident[:], xt[:], start=True, stop=False, skip_group_check=True)
            keep_warm(5, PS[:, 5, :])
            pe.wait_ge(nT_ready, 2)
            x_q(0)
            keep_warm(3, PS[:, 5, :])
            x_qT(0)
            keep_warm(4, PS[:, 5, :])
            x_qproj(0)
            keep_warm(6, PS[:, 5, :])
            x_head(0, False, True)
            with pe.Fori(1, XKV - 1) as j:
                x_head(j, True, True)
            x_head(XKV - 1, True, False)
            keep_warm(4, PS[:, 5, :])
            pe.wait_ge(coT_copied, XKV * 2 - 1)
            x_coT(XKV - 1, 1)
            keep_warm(5, PS[:, 5, :])
            x_value(XKV - 1)
            keep_warm(5, PS[:, 5, :])
            x_out(XKV - 1, last=True)

            keep_warm(15, PS[:, 1, :])
            to_features(PS[:, 7, :], nrm, norm_ready, 2)
            keep_warm(11, PS[:, 1, :])
            pe.wait_ge(nT_ready, 4)
            pe.wait_ge(L["vec"], 16)
            w0 = [V_BCDT + k * BCDT for k in range(KD)]
            for k in range(KD):
                i = mm(PS[:, 6, 0:MH], nT[:, k, :], vec[:, w0[k] + 2 * DS:w0[k] + BCDT], start=(k == 0), stop=(k == KD - 1))
            i.then_inc(M["dt"], 1)
            for n in range(2):
                for k in range(KD):
                    i = mm(PS[0:DS, 5, n * P:(n + 1) * P], vec[:, w0[k] + n * DS:w0[k] + (n + 1) * DS], nT[:, k, :],
                           start=(k == 0), stop=(k == KD - 1))
            i.then_inc(M["bcT"], 1)

            def m_x(half):
                for n, k in enumerate(IN_ORDER):
                    if half == 0:
                        pe.wait_ge(LO["in"], min(n + 1, 3))
                    if n == 3:
                        pe.wait_ge(LO["in1"], 1)
                    i = mm3(PS[:, 3 + half, :], nT_(k), chunk_part(C_IN + k, DI + half * 512, DI + (half + 1) * 512),
                            start=(n == 0), stop=(n == KD - 1))
                i.then_inc(M["xm"], 1)

            def m_xT(half):
                pe.wait_ge(M["xc"], half + 1)
                for c in range(4):
                    f = half * 4 + c
                    i = nc.tensor.transpose(PS[:, 3 + half, c * P:(c + 1) * P], y_sb[:, f * P:(f + 1) * P], ident[:])
                i.then_inc(M["xT"], 1)

            def m_decay(n):
                if n == 0:
                    pe.wait_ge(M["wdec"], 1)
                if n >= 2:
                    pe.wait_ge(M["decay"], n - 1)
                mm(PS[:, 6 + n % 2, :], later[:], wdec[:, n * 4:(n + 1) * 4, :], start=True, stop=True).then_inc(M["dsum"], 1)

            m_x(0)
            m_x(1)
            m_xT(0)
            m_xT(1)
            m_decay(0)
            m_decay(1)

            def m_z(n):
                for k in range(KD):
                    i = mm3(PS[:, 1 + n, :], nT_(k), chunk_part(C_IN + k, n * 512, (n + 1) * 512),
                            start=(k == 0), stop=(k == KD - 1))
                    if n:
                        i.then_inc(ring_used, 1)

            m_z(0)
            m_decay(2)
            m_decay(3)
            m_z(1)
            pe.wait_ge(M["bcact"], 1)
            mm(PS[:, 5, 0:P], cact[0:DS, XC, :], cact[0:DS, XC + 1, :], start=True, stop=True).then_inc(M["g"], 1)
            for n in range(2):
                pe.wait_ge(M["cact"], n + 1)
                for c in range(4):
                    i = nc.tensor.transpose(PS[:, 3 + n, c * P:(c + 1) * P], cact[:, n * 4 + c, :], ident[:])
                i.then_inc(M["xtok"], 1)
            pe.wait_ge(xt_ready, 1)
            keep_warm(6, ACC)
            for h in range(MH):
                if h % 8 == 0:
                    pe.wait_ge(M["mdec"], h // 8 + 1)
                i = mm(PS[:, 6 + h // 8, (h % 8) * HP:(h % 8 + 1) * HP], dec[:, h, :], xdt[:, h, :], start=True, stop=True)
                if h % 8 == 7:
                    i.then_inc(M["y"], 1)
            keep_warm(6, ACC)
            for n in range(2):
                pe.wait_ge(M["yg"], n + 1)
                for c in range(4):
                    f = n * 4 + c
                    i = nc.tensor.transpose(PS[:, 3 + n, c * P:(c + 1) * P], y_sb[:, f * P:(f + 1) * P], ident[:])
                i.then_inc(M["yT"], 1)
            for n in range(2):
                pe.wait_ge(L["out"], 32)
                pe.wait_ge(M["yTs"], n + 1)
                for c in range(4):
                    i = mm(PS[:, 5, :], yT[:, n * 4 + c, :], out_sb[:, n, c * D:(c + 1) * D],
                           start=(n == 0 and c == 0), stop=(n == 1 and c == 3))
            i.then_inc(M["outp"], 1)

            mm(ACC, ident[:], xt[:], start=True, stop=False, skip_group_check=True)
            keep_warm(2, PS[:, 1, :])
            to_features(PS[:, 6, :], mid, mid_ready, 2)
            mm(ACC, ident[:], mid[:], start=False, stop=False, skip_group_check=True)
            keep_warm(4, PS[:, 1, :])
            pe.wait_ge(nT_ready, 6)
            for k in range(KD):
                i = mm(PS[:, 7, 0:E1], nT[:, k, :], vec[:, V_GATE + k * E1:V_GATE + (k + 1) * E1],
                       start=(k == 0), stop=(k == KD - 1))
            i.then_inc(M["logit"], 1)

            def up(par, c, lap):
                pe.wait_ge(lo_ready, lap * SLOTS + split_count(c))
                for k in range(KD):
                    i = mm3(PS[:, 1 + par, :], nT_(k), chunk_part(c, k * 512, (k + 1) * 512),
                            start=(k == 0), stop=(k == KD - 1))
                i.then_inc(ring_used, 1)

            def down(s, par, c, lap):
                pe.wait_ge(lo_ready, lap * SLOTS + split_count(c))
                pe.wait_ge(hT_ready, s + 1)
                for n in range(4):
                    i = mm3(ACC, (hTh[:, par, n, :], hTl[:, par, n, :]), chunk_part(c, n * D, (n + 1) * D), start=False,
                            stop=False, skip_group_check=True)
                i.then_inc(ring_used, 1)

            def down_last(par, c, pieces):
                pe.wait_ge(hi_ready, split_count(c))
                for n in range(pieces):
                    w = high[:, c % HIGHS, n * D:(n + 1) * D]
                    mm(ACC, hTl[:, par, n, :], w, start=False, stop=False, skip_group_check=True)
                    mm(ACC, hTh[:, par, n, :], w, start=False, stop=False, skip_group_check=True)
                pe.wait_ge(lo_ready, split_count(c))
                for n in range(pieces):
                    i = mm(ACC, hTh[:, par, n, :], ring_low[:, c % SLOTS, n * D:(n + 1) * D], start=False,
                           stop=(n == pieces - 1), skip_group_check=True)
                i.then_inc(ring_used, 1)

            def turn(s, par):
                pe.wait_ge(act_ready, s + 1)
                for c in range(4):
                    i = nc.tensor.transpose(PS[:, 3 + par, c * P:(c + 1) * P], h_act[:, par, c * P:(c + 1) * P], ident[:])
                i.then_inc(hT_made, 1)

            def moe_step(s, t, i=0):
                cu, cd = up_chunk(C_W1, t), down_chunk(C_W1, t - 2, STEPS1)
                up(t % 2, cu, i)
                if t >= 2:
                    down(s - 2, t % 2, cd, i)
                if t >= 1:
                    turn(s - 1, (t + 1) % 2)

            for s in range(4):
                moe_step(s, s)
            with pe.Fori(1, E1) as e:
                for t in range(4):
                    moe_step(e * 4 + t, 4 + t, e - 1)
            turn(STEPS1 - 1, (STEPS1 - 1) % 2)
            down(STEPS1 - 2, STEPS1 % 2, down_chunk(C_W1, STEPS1 - 2, STEPS1), 0)
            pe.wait_ge(hT_ready, STEPS1)
            down_last((STEPS1 - 1) % 2, down_chunk(C_W1, STEPS1 - 1, STEPS1), 4)

            keep_warm(10, PS[:, 1, :])
            to_features(PS[:, 7, :], nrm, norm_ready, 3)
            keep_warm(8, PS[:, 1, :])
            pe.wait_ge(nT_ready, 8)
            for n in range(2):
                pe.wait_ge(lo_ready, split_count(C_ATT + n))
                for k in range(KD):
                    i = mm3(PS[:, 4 + n, :], nT_(k), chunk_part(C_ATT + n, k * 512, (k + 1) * 512),
                            start=(k == 0), stop=(k == KD - 1))
                i.then_inc(ring_used, 1)

            pe.wait_ge(mid_ready, 3)
            pe.wait_ge(xt_ready, 2)
            mm(ACC, ident[:], res[:], start=True, stop=False, skip_group_check=True)

            def a_q(u):
                c0 = wq_chunk(u)
                if u >= 2:
                    pe.wait_ge(A["ropes"], u)
                if u == 3:
                    keep_warm(5, PS[:, 2, :])
                pe.wait_ge(lo_ready, split_count(c0))
                for k in range(KD):
                    i = mm3(PS[:, 1 + u % 2, :], nT_(k), chunk_part(c0, k * 512, (k + 1) * 512),
                            start=(k == 0), stop=(k == KD - 1))
                i.then_inc(ring_used, 1)

            def a_kT():
                pe.wait_ge(A["krope"], 1)
                for c in range(AKV):
                    i = nc.tensor.transpose(PS[:, 6, c * P:(c + 1) * P], rq[:, 1, c, :], ident[:])
                i.then_inc(A["kT"], 1)

            def a_qT(u):
                pe.wait_ge(A["rope"], u + 1)
                if u:
                    pe.wait_ge(A["qTs"], u)
                for c in range(4):
                    i = nc.tensor.transpose(PS[:, 3, c * P:(c + 1) * P], rq[:, u % 2, c, :], ident[:])
                i.then_inc(A["qT"], 1)

            def a_scores(u):
                pe.wait_ge(A["qTs"], u + 1)
                pe.wait_ge(A["kTs"], 1)
                if u < 2:
                    pe.wait_ge(LO["v"], 1)
                for c in range(4):
                    i = mm3(PS[:, 4 + u % 2, c * P:(c + 1) * P], (aqTh[:, c, :], aqTl[:, c, :]),
                            (akTh[:, u // 2, :], akTl[:, u // 2, :]), start=True, stop=True)
                i.then_inc(A["s"], 1)

            def a_probT(u):
                pe.wait_ge(A["pn"], u + 1)
                pe.wait_ge(A["kTs"], 1)
                if u:
                    pe.wait_ge(A["pTs"], u)
                for c in range(4):
                    i = nc.tensor.transpose(PS[:, 6, c * P:(c + 1) * P], apn[:, u % 2, c, :], ident[:])
                i.then_inc(A["pT"], 1)

            def a_value(u):
                pe.wait_ge(A["pTs"], u + 1)
                if u:
                    pe.wait_ge(A["os"], u)
                mm3(PS[:, 7, :], (avh[:, u // 2, :], avl[:, u // 2, :]), (apTh[:], apTl[:]), start=True,
                    stop=True).then_inc(A["o"], 1)

            def a_out(u):
                c0 = wo_chunk(u)
                wait_chunk(pe, c0 % SLOTS, c0 // SLOTS)
                pe.wait_ge(A["os"], u + 1)
                for c in range(4):
                    i = mm(ACC, aoT[:, c, :], ring[:, c0 % SLOTS, c * D:(c + 1) * D], start=False,
                           stop=(u == UNITS - 1 and c == 3), skip_group_check=True)
                i.then_inc(ring_used, 1)

            for s in range(UNITS + A_LAG):
                if 2 <= s <= UNITS:
                    a_qT(s - 1)
                if s < UNITS:
                    a_q(s)
                if s == 0:
                    a_kT()
                if s == 1:
                    a_qT(0)
                if 1 <= s <= UNITS:
                    if s in (1, UNITS):
                        keep_warm(12, PS[:, 7 if s == 1 else 1, :])
                    a_scores(s - 1)
                if 2 <= s < UNITS + 2:
                    a_probT(s - 2)
                if s >= A_LAG:
                    a_out(s - A_LAG)
                if s == 2:
                    keep_warm(8, PS[:, 7, :])
                if 2 <= s < UNITS + 2:
                    a_value(s - 2)

            keep_warm(4, PS[:, 1, :])
            to_features(PS[:, 6, :], mid, mid_ready, 4)
            mm(ACC, ident[:], xt[:], start=True, stop=False, skip_group_check=True)
            mm(ACC, ident[:], mid[:], start=False, stop=False, skip_group_check=True)
            pe.wait_ge(nT_ready, 10)
            for k in range(KD):
                i = mm(PS[:, 7, 0:E2], nT[:, k, :], vec[:, V_ROUTE + k * E2:V_ROUTE + (k + 1) * E2],
                       start=(k == 0), stop=(k == KD - 1))
            i.then_inc(A["logit"], 1)

            def ffn_down(s, t, i=0):
                c = down_chunk(C_FFN, t - 2, STEPS2)
                pe.wait_ge(lo_ready, i * SLOTS + split_count(c))
                pe.wait_ge(aT_ready, s - 1)
                for n in range(2):
                    x_ = mm3(ACC, (hTh[:, t % 2, n, :], hTl[:, t % 2, n, :]), chunk_part(c, n * D, (n + 1) * D), start=False,
                             stop=False, skip_group_check=True)
                x_.then_inc(ring_used, 1)

            def ffn_turn(s, t):
                pe.wait_ge(a_ready, s)
                for n in range(2):
                    x_ = nc.tensor.transpose(PS[:, 3 + (t + 1) % 2, n * P:(n + 1) * P],
                                             h_act[:, (t + 1) % 2, n * P:(n + 1) * P], ident[:])
                x_.then_inc(aT_made, 1)

            def ffn_step(s, t, i=0):
                c = up_chunk(C_FFN, t)
                pe.wait_ge(lo_ready, i * SLOTS + split_count(c))
                for k in range(KD):
                    x_ = mm3(PS[:, 1 + t % 2, :], nT_(k), chunk_part(c, k * 512, (k + 1) * 512),
                             start=(k == 0), stop=(k == KD - 1))
                x_.then_inc(ring_used, 1)
                if t >= 2:
                    ffn_down(s, t, i)
                if t >= 1:
                    ffn_turn(s, t)


            for s in range(5):
                ffn_step(s, s)
            with pe.Fori(0, (STEPS2 - 5) // 4) as i:
                for t in range(4):
                    ffn_step(i * 4 + 5 + t, 5 + t, i)
            ffn_turn(STEPS2, STEPS2)
            ffn_down(STEPS2, STEPS2)
            pe.wait_ge(aT_ready, STEPS2)
            down_last((STEPS2 - 1) % 2, down_chunk(C_FFN, STEPS2 - 1, STEPS2), 2)

        @block.scalar
        def _(act):
            steps = [0]
            act_fn = nc.scalar.activation

            def settled(ins):
                steps[0] += 1
                ins.then_inc(s_act, 1)
                act.wait_ge(s_act, steps[0])

            def chunk_high(c, lap=0, free=None):
                wait_chunk(act, c % SLOTS, lap + c // SLOTS)
                act.wait_ge(ring_used, free or lap * SLOTS + (c - HIGHS + 1))
                n = chunk_width(c)
                nc.scalar.copy(high[:, c % HIGHS, 0:n], ring[:, c % SLOTS, 0:n]).then_inc(hi_ready, 1)

            XS = float(XD) ** -0.5

            def root(n, dst, src, **kw):
                act.wait_ge(var_ready, n)
                settled(act_fn(log_[:, 0:src.shape[-1]], src, ACT.Ln, **kw))
                act_fn(dst, log_[:, 0:src.shape[-1]], ACT.Exp, scale=-0.5).then_inc(rstd_ready, 1)

            def in_high(k):
                wait_chunk(act, C_IN + k, 0)
                nc.scalar.copy(high[:, k, :], ring[:, C_IN + k, :]).then_inc(H["in"], 1)

            def qk_high(j):
                act.wait_ge(L["qk"], j * 16 + 16)
                nc.scalar.copy(qkh[:], qk_sb[:]).then_inc(H["qk"], 1)

            def vo_high(j):
                act.wait_ge(L["vo"], j * 16 + 16)
                nc.scalar.copy(voh[:], vo_sb[:]).then_inc(H["vo"], 1)

            def x_pT_high(j, b):
                for n in range(2):
                    act.wait_ge(pT_ready, j * 4 + 2 * b + n + 1)
                    nc.scalar.copy(pTh[:, b, n * 4:(n + 1) * 4, :].rearrange("p c q -> p (c q)"), x_tr[n]).then_inc(H["pT"], 1)

            def x_coT_high(j, b):
                act.wait_ge(coT_ready, j * 2 + b + 1)
                nc.scalar.copy(coTh[:, :, b, :], (x_mb if b else x_ma).rearrange("p (k q) -> p k q", k=KC)).then_inc(H["coT"], 1)

            def x_oT_high(j):
                act.wait_ge(oT_ready, j + 1)
                nc.scalar.copy(oTh[:].rearrange("p h t -> p (h t)"), x_ma).then_inc(H["oT"], 1)

            def x_exp(j, b):
                act.wait_ge(nb_ready, j * 2 + b + 1)
                act_fn(pr[:, b, :], pr[:, b, :], ACT.Exp, bias=nbias[:, b:b + 1], scale=XS,
                       accum_out=xsum[:, b:b + 1]).then_inc(exp_done, 1)

            def x_copies(j, what):
                if what == 0:
                    act.wait_ge(q_ready, j + 1)
                    nc.scalar.copy(q_sb[:], x_scores[0][:, 0:256]).then_inc(q_copied, 1)
                if what == 1:
                    act.wait_ge(qT_ready, j + 1)
                    nc.scalar.copy(qTh[:], x_ma).then_inc(H["qT"], 1)
                if what == 2:
                    act.wait_ge(qp_ready, j + 1)
                    nc.scalar.copy(qph[:].rearrange("p a b q -> p (a b q)"), x_qp).then_inc(H["qp"], 1)

            root(1, rs[:, 0:1], var2[:, 0:1])
            def cT_high(b):
                act.wait_ge(L[f"cT{b}"], 16)
                nc.scalar.copy(cTh[:, b], cT[:, b]).then_inc(H["cT"], 1)

            qk_high(0)
            cT_high(0)
            for w in range(3):
                x_copies(0, w)
            cT_high(1)
            for b in range(B):
                act.wait_ge(L[f"cx{b}"], 16)
                nc.scalar.copy(cxh[:, b], cx[:, b]).then_inc(H["cx"], 1)

            def x_head(j, prev, nxt):
                if not prev:
                    x_exp(j, 0)
                if nxt:
                    qk_high(j + 1)
                if prev:
                    x_coT_high(j - 1, 1)
                    x_exp(j, 0)
                    x_oT_high(j - 1)
                x_exp(j, 1)
                if not prev:
                    x_pT_high(j, 0)
                if nxt:
                    x_copies(j + 1, 0)
                if prev:
                    x_pT_high(j, 0)
                if nxt:
                    x_copies(j + 1, 1)
                else:
                    act.wait_ge(s_max, XKV * 2)
                    in_high(2)
                x_pT_high(j, 1)
                if nxt:
                    x_copies(j + 1, 2)
                vo_high(j)
                if not nxt:
                    in_high(3)
                x_coT_high(j, 0)

            x_head(0, False, True)
            with act.Fori(1, XKV - 1) as j:
                x_head(j, True, True)
            x_head(XKV - 1, True, False)
            x_coT_high(XKV - 1, 1)
            x_oT_high(XKV - 1)

            act.wait_ge(sc_ready, XKV * 2)
            in_high(0)
            root(2, rs[:, 0:2], var2[:])
            in_high(1)
            act.wait_ge(L["row"], 16)
            act.wait_ge(M["expA"], 1)
            act_fn(dts[:, 0, :], dts[:, 0, :], ACT.Exp).then_inc(M["A"], 1)
            act.wait_ge(M["abs"], 1)
            act_fn(dts[:, 3, :], dts[:, 2, :], ACT.Exp, scale=-1.0).then_inc(M["expd"], 1)
            act.wait_ge(M["u"], 1)
            act_fn(dts[:, 5, :], dts[:, 4, :], ACT.Ln).then_inc(M["lnu"], 1)

            def m_exp(n):
                act.wait_ge(M["dsum"], n + 1)
                act_fn(dec[:, n * 4:(n + 1) * 4, :], PS[:, 6 + n % 2, :].rearrange("p (h t) -> p h t", h=4),
                       ACT.Exp).then_inc(M["decay"], 1)

            act.wait_ge(s_const, 4)
            for g, (rows_, c0, c1, bank) in enumerate(CONV):
                if g == 1:
                    for half in range(2):
                        act.wait_ge(M["xm"], half + 1)
                        nc.scalar.copy(y_sb[:, half * 512:(half + 1) * 512], PS[:, 3 + half, :]).then_inc(M["xc"], 1)
                act.wait_ge(M["xT"] if g else M["bcT"], g if g else 1)
                nc.scalar.copy(xpad[0:rows_, c0:c1, :, TAPS - 1:PAD],
                               PS[0:rows_, bank, 0:(c1 - c0) * P].rearrange("p (c b t) -> p c b t", c=c1 - c0, b=B))
                for c in range(c0, c1):
                    w = V_TAP + c * TAPS + TAPS - 1
                    i = act_fn(cacc[0:rows_, c, :], PS[0:rows_, bank, (c - c0) * P:(c - c0 + 1) * P], ACT.Identity,
                               bias=vec[0:rows_, V_CB + c:V_CB + c + 1], scale=vec[0:rows_, w:w + 1])
                i.then_inc(M["pre"], 1)
            for n in range(4):
                m_exp(n)
            for g, (rows_, c0, c1, _) in enumerate(CONV):
                act.wait_ge(M["conv"], g + 1)
                act_fn(cact[0:rows_, c0:c1, :], cacc[0:rows_, c0:c1, :], ACT.Silu).then_inc(M["cact"] if g else M["bcact"], 1)
            act.wait_ge(ring_used, KD)
            act_fn(zs[:], PS[:, 1:3, :].rearrange("p a n -> p (a n)"), ACT.Silu).then_inc(M["zsilu"], 1)
            for c in range(C_W1, C_W1 + 4):
                chunk_high(c, free=KD)
            root(3, rs[:, 3:4], ms[:, 1:2], bias=epsc[:, 0:1])
            root(4, rs[:, 2:3], ms[:, 0:1], bias=epsc[:, 0:1])
            act.wait_ge(rstd_ready, 4)
            act.wait_ge(M["rexp"], 1)
            act_fn(r8[:, 8:16], rsc[:, 1, 0:8], ACT.Exp).then_inc(M["rexp"], 1)

            def hidden_T_high(s, par):
                act.wait_ge(hT_made, s + 1)
                nc.scalar.copy(hTh[:, par].rearrange("p c t -> p (c t)"), PS[:, 3 + par, :]).then_inc(H["hT"], 1)

            def moe_step(s, t, i=0):
                hidden_silu(s, t % 2)
                if t == 1:
                    hidden_T_high(0, 0)
                for c in up_ahead(C_W1, t, STEPS1):
                    chunk_high(c, i)
                if t > 1:
                    hidden_T_high(s - 1, (t + 1) % 2)
                if t == STEPS1 - 1:
                    hidden_T_high(s, t % 2)
                if t >= 1:
                    chunk_high(down_chunk(C_W1, t, STEPS1), i)

            def hidden_silu(s, par):
                act.wait_ge(ring_used, up_chunk(C_W1, s) + 1)
                act_fn(h_silu[:, par, :], PS[:, 1 + par, :], ACT.Silu, scale=rs[:, 2:3]).then_inc(silu_ready, 1)

            for s in range(4):
                moe_step(s, s)
            with act.Fori(1, E1 - 1) as e:
                for t in range(4):
                    moe_step(e * 4 + t, 4 + t, e - 1)
            for s in range(STEPS1 - 4, STEPS1):
                moe_step(s, s)
            chunk_high(C_ATT)
            chunk_high(C_ATT + 1)

            root(5, rs[:, 0:2], var2[:])
            chunk_high(C_ATT + 2)
            chunk_high(C_ATT + 3)
            act.wait_ge(ring_used, C_ATT + 2)
            act.wait_ge(rstd_ready, 5)
            act_fn(avh[:].rearrange("p g d -> p (g d)"), PS[:, 5, :], ACT.Copy, scale=rs[:, 1:2]).then_inc(H["v"], 1)
            act.wait_ge(A["kT"], 1)
            nc.scalar.copy(akTh[:].rearrange("p g t -> p (g t)"), PS[:, 6, :]).then_inc(H["kT"], 1)
            AS = float(AD) ** -0.5

            def a_exp(u):
                act.wait_ge(A["nb"], u + 1)
                for c in range(4):
                    i = act_fn(apr[:, u % 2, c, :], asc[:, u % 2, c, :], ACT.Exp, bias=anb[:, u % 2, c:c + 1], scale=AS,
                               accum_out=asm[:, u % 2, c:c + 1])
                i.then_inc(A["exp"], 1)

            def a_copy_T(u):
                act.wait_ge(A["qT"], u + 1)
                nc.scalar.copy(aqTh[:].rearrange("p h t -> p (h t)"), PS[:, 3, :]).then_inc(H["aq"], 1)

            def a_copy_pT(u):
                act.wait_ge(A["pT"], u + 1)
                nc.scalar.copy(apTh[:].rearrange("p h t -> p (h t)"), PS[:, 6, :]).then_inc(H["ap"], 1)

            def a_copy_o(u):
                act.wait_ge(A["o"], u + 1)
                nc.scalar.copy(aoT[:].rearrange("p h t -> p (h t)"), PS[:, 7, :]).then_inc(A["os"], 1)

            for s in range(UNITS + A_LAG):
                if 1 <= s <= UNITS and s != 2:
                    a_copy_T(s - 1)
                if s >= 3:
                    a_copy_o(s - 3)
                if s + 2 < UNITS:
                    chunk_high(wq_chunk(s + 2))
                if 2 <= s < UNITS + 2:
                    a_copy_pT(s - 2)
                if s == 1:
                    a_copy_T(1)
                if 1 <= s <= UNITS:
                    a_exp(s - 1)
                if s >= UNITS:
                    chunk_high(C_FFN + s - UNITS, free=wq_chunk(UNITS - 1) + 1)
            chunk_high(C_FFN + 3, free=wq_chunk(UNITS - 1) + 1)
            root(6, rs[:, 2:3], ms[:, 0:1], bias=epsc[:, 1:2])
            act.wait_ge(rstd_ready, 6)

            act.wait_ge(A["logit"], 1)
            act_fn(rsc[:, 0, :], PS[:, 7, 0:E2], ACT.Sigmoid, scale=rs[:, 2:3]).then_inc(A["rsig"], 1)

            def gated_T_high(s, par):
                act.wait_ge(aT_made, s + 1)
                nc.scalar.copy(hTh[:, par, 0:2].rearrange("p c t -> p (c t)"), PS[:, 3 + par, 0:2 * P]).then_inc(H["aT"], 1)

            def ffn_step(s, t, i=0):
                gate_silu(s, t % 2)
                if t == 1:
                    gated_T_high(0, 0)
                for c in up_ahead(C_FFN, t, STEPS2):
                    chunk_high(c, i)
                if t > 1:
                    gated_T_high(s - 1, (t + 1) % 2)
                if t == STEPS2 - 1:
                    gated_T_high(s, t % 2)
                if t >= 1:
                    chunk_high(down_chunk(C_FFN, t, STEPS2), i)

            def gate_silu(s, par):
                act.wait_ge(ring_used, up_chunk(C_FFN, s) + 1)
                act_fn(h_silu[:, par, 0:FF2], PS[:, 1 + par, 0:FF2], ACT.Silu, scale=rs[:, 2:3]).then_inc(gsilu_ready, 1)

            for s in range(5):
                ffn_step(s, s)
            with act.Fori(0, (STEPS2 - 5) // 4 - 1) as i:
                for t in range(4):
                    ffn_step(i * 4 + 5 + t, 5 + t, i)
            for s in range(STEPS2 - 4, STEPS2):
                ffn_step(s, s)

        @block.vector
        def _(dve):
            V = nc.vector
            steps = [0]

            def settled(ins):
                steps[0] += 1
                ins.then_inc(s_dve, 1)
                dve.wait_ge(s_dve, steps[0])

            def variance(src, eps=None):
                settled(V.bn_stats(bnst[:], src))
                settled(V.bn_aggr(moments[:], bnst[:]))
                if eps is not None:
                    V.tensor_scalar(var2[:, 1:2], moments[:, 1:2], 1.0 + eps, LN_EPS * eps, ALU.mult, ALU.add)
                V.tensor_scalar(var2[:, 0:1], moments[:, 1:2], LN_EPS, None, ALU.add).then_inc(var_ready, 1)

            def layer_norm(n, src, dst, done, eps=None):
                variance(src, eps)
                dve.wait_ge(rstd_ready, n)
                if eps is not None:
                    V.tensor_scalar(nrm[:], src, moments[:, 0:1], rs[:, 1:2], ALU.subtract, ALU.mult).then_inc(norm_ready, 1)
                V.tensor_scalar(dst, src, moments[:, 0:1], rs[:, 0:1], ALU.subtract, ALU.mult).then_inc(done, 1)

            def mean_square(src, squares, n):
                V.tensor_tensor_reduce(out=squares, in0=src, in1=src, scale=1.0 / src.shape[-1], scalar=0.0, op0=ALU.mult,
                                       op1=ALU.add, accum_out=ms[:, n:n + 1]).then_inc(var_ready, 1)

            def copy_nT(n, bank, v):
                dve.wait_ge(nT_made, n)
                src = bank.rearrange("p (k t) -> p k t", k=KD)
                if v is None:
                    settled(V.tensor_copy(nT[:], src))
                else:
                    settled(V.tensor_tensor(nT[:], src, vec[:, v:v + KD].rearrange("p (k o) -> p k o", o=1).to_broadcast([P, KD, T]),
                                            ALU.mult))
                V.tensor_copy(nTh[:], nT[:]).then_inc(nT_ready, 1)
                dve.wait_ge(nT_ready, 2 * n - 1)
                V.tensor_tensor(nTl[:], nT[:], nTh[:].bitcast(F32), ALU.subtract).then_inc(nT_ready, 1)

            def low(dst, src, hi):
                return V.tensor_tensor(dst, src, hi.bitcast(F32), ALU.subtract)

            def chunk_low(c, lap=0):
                dve.wait_ge(hi_ready, lap * SLOTS + split_count(c))
                n = chunk_width(c)
                low(ring_low[:, c % SLOTS, 0:n], ring[:, c % SLOTS, 0:n], high[:, c % HIGHS, 0:n]).then_inc(lo_ready, 1)

            dve.wait_ge(L["x"], 16)
            layer_norm(1, xt[:], nrm[:], norm_ready)
            XS = float(XD) ** -0.5

            def x_max(j, b):
                dve.wait_ge(sc_ready, j * 2 + b + 1)
                V.memset(held[:], 0.0)
                V.tensor_tensor_reduce(out=pr[:, b, :], in0=x_scores[b], in1=madd[:, b, :], scale=1.0, scalar=2 * MASKED,
                                       op0=ALU.add, op1=ALU.max, accum_out=xmax[:, b:b + 1]).then_inc(s_max, 1)
                dve.wait_ge(s_max, j * 2 + b + 1)
                V.tensor_scalar(nbias[:, b:b + 1], xmax[:, b:b + 1], -XS, None, ALU.mult).then_inc(nb_ready, 1)

            def x_recip(j, b):
                dve.wait_ge(exp_done, j * 2 + b + 1)
                V.reciprocal(xrec[:, b:b + 1], xsum[:, b:b + 1]).then_inc(x_dve, 1)
                V.tensor_scalar(xval[:, b:b + 1], xmax[:, b:b + 1], MASKED / 2, None, ALU.is_gt).then_inc(x_dve, 1)

            def x_pT(j, b):
                for n in range(2):
                    dve.wait_ge(H["pT"], j * 4 + 2 * b + n + 1)
                    part = (slice(None), b, slice(n * 4, (n + 1) * 4))
                    low(pTl[part].rearrange("p c q -> p (c q)"), x_tr[n],
                        pTh[part].rearrange("p c q -> p (c q)")).then_inc(pT_copied, 1)

            def x_co(j, b):
                dve.wait_ge(co_ready, j * 2 + b + 1)
                dve.wait_ge(x_dve, j * 4 + 2 * b + 2)
                V.tensor_scalar(co[:, b, :], x_ctxo[b], xrec[:, b:b + 1], xval[:, b:b + 1], ALU.mult,
                                ALU.mult).then_inc(co_copied, 1)

            def x_coT(j, b):
                dve.wait_ge(H["coT"], j * 2 + b + 1)
                low(coTl[:, :, b, :], (x_mb if b else x_ma).rearrange("p (k q) -> p k q", k=KC),
                    coTh[:, :, b, :]).then_inc(coT_copied, 1)

            def x_oT(j):
                dve.wait_ge(H["oT"], j + 1)
                low(oTl[:].rearrange("p h t -> p (h t)"), x_ma, oTh[:].rearrange("p h t -> p (h t)")).then_inc(oT_copied, 1)

            def qk_low(j):
                dve.wait_ge(H["qk"], j + 1)
                low(qkl[:], qk_sb[:], qkh[:]).then_inc(LO["qk"], 1)

            def vo_low(j):
                dve.wait_ge(H["vo"], j + 1)
                low(vol[:], vo_sb[:], voh[:]).then_inc(LO["vo"], 1)

            def x_qT(j):
                dve.wait_ge(H["qT"], j + 1)
                low(qTl[:], x_ma, qTh[:]).then_inc(qT_copied, 1)

            def x_qp_(j):
                dve.wait_ge(H["qp"], j + 1)
                low(qpl[:].rearrange("p a b q -> p (a b q)"), x_qp, qph[:].rearrange("p a b q -> p (a b q)")).then_inc(qp_copied, 1)

            def x_head(j, prev, nxt):
                if prev:
                    if nxt:
                        qk_low(j + 1)
                    x_max(j, 0)
                    x_coT(j - 1, 1)
                    x_max(j, 1)
                    x_oT(j - 1)
                else:
                    x_max(j, 0)
                    x_max(j, 1)
                    qk_low(j + 1)
                x_recip(j, 0)
                x_pT(j, 0)
                if nxt:
                    x_qT(j + 1)
                x_recip(j, 1)
                x_pT(j, 1)
                x_co(j, 0)
                if nxt:
                    x_qp_(j + 1)
                vo_low(j)
                x_co(j, 1)
                x_coT(j, 0)

            def cT_low(b):
                dve.wait_ge(H["cT"], b + 1)
                low(cTl[:, b], cT[:, b], cTh[:, b]).then_inc(LO["cT"], 1)

            qk_low(0)
            copy_nT(1, PS[:, 1, :], None)
            cT_low(0)
            x_qT(0)
            dve.wait_ge(L["mask"], 16)
            settled(V.tensor_scalar(madd, mask8, -MASKED, MASKED, ALU.mult, ALU.add))
            x_qp_(0)
            cT_low(1)
            x_head(0, False, True)
            with dve.Fori(1, XKV - 1) as j:
                x_head(j, True, True)
            x_head(XKV - 1, True, False)
            x_coT(XKV - 1, 1)
            x_oT(XKV - 1)

            dve.wait_ge(wo_done, XKV)
            layer_norm(2, ACC, res[:], mid_ready, MIX_EPS)
            V.tensor_copy(xt[:], ACC).then_inc(xt_ready, 1)
            dve.wait_ge(L["vec"], 16)
            copy_nT(2, PS[:, 7, :], V_MIX)
            dve.wait_ge(H["in"], KD)
            low(ring_low[:, C_IN + 1, :], ring[:, C_IN + 1, :], high[:, 1, :]).then_inc(LO["in1"], 1)
            dve.wait_ge(L["row"], 16)
            V.tensor_scalar(dts[:, 0, :], row[:, R_A:R_A + MH], A_LOG_TOP, None, ALU.min).then_inc(M["expA"], 1)
            dve.wait_ge(M["dt"], 1)
            settled(V.tensor_tensor(dts[:, 1, :], PS[:, 6, 0:MH], row[:, R_DT:R_DT + MH], ALU.add))
            settled(V.tensor_scalar(dts[:, 2, :], dts[:, 1, :], -1.0, None, ALU.mult))
            V.tensor_tensor(dts[:, 2, :], dts[:, 1, :], dts[:, 2, :], ALU.max).then_inc(M["abs"], 1)
            dve.wait_ge(M["expd"], 1)
            V.tensor_scalar(dts[:, 4, :], dts[:, 3, :], 1.0, None, ALU.add).then_inc(M["u"], 1)
            dve.wait_ge(M["u"], 1)
            settled(V.tensor_scalar(dts[:, 6, :], dts[:, 4, :], -1.0, None, ALU.add))
            settled(V.tensor_scalar(dts[:, 2, :], dts[:, 6, :], 0.0, None, ALU.is_equal))
            settled(V.tensor_tensor(dts[:, 6, :], dts[:, 6, :], dts[:, 2, :], ALU.add))
            settled(V.reciprocal(dts[:, 6, :], dts[:, 6, :]))
            dve.wait_ge(M["lnu"], 1)
            dve.wait_ge(M["A"], 1)
            settled(V.tensor_tensor(dts[:, 5, :], dts[:, 5, :], dts[:, 2, :], ALU.add))
            settled(V.tensor_tensor(dts[:, 5, :], dts[:, 5, :], dts[:, 6, :], ALU.mult))
            settled(V.tensor_tensor(dts[:, 5, :], dts[:, 5, :], dts[:, 3, :], ALU.mult))
            settled(V.scalar_tensor_tensor(out=dts[:, 1, :], in0=dts[:, 1, :], scalar=0.0, in1=dts[:, 5, :], op0=ALU.max,
                                           op1=ALU.add))
            settled(V.tensor_tensor(dts[:, 7, :], dts[:, 1, :], dts[:, 0, :], ALU.mult))
            settled(V.tensor_scalar(dts[:, 7, :], dts[:, 7, :], -1.0, DECAY_BOTTOM, ALU.mult, ALU.max))
            dve.wait_ge(s_const, 4)
            V.tensor_tensor(wdec[:], tri[:].rearrange("p (o t) -> p o t", o=1).to_broadcast([P, MH, T]),
                            dts[:, 7, :].rearrange("p (h o) -> p h o", o=1).to_broadcast([P, MH, T]),
                            ALU.mult).then_inc(M["wdec"], 1)
            for g, (rows_, c0, c1, _) in enumerate(CONV):
                dve.wait_ge(M["pre"], g + 1)
                for k in range(TAPS - 1):
                    for c in range(c0, c1):
                        acc = cacc[0:rows_, c, :].rearrange("p (b t) -> p b t", b=B)
                        w = V_TAP + c * TAPS + k
                        i = V.scalar_tensor_tensor(out=acc, in0=xpad[0:rows_, c, :, k:k + S], scalar=vec[0:rows_, w:w + 1],
                                                   in1=acc, op0=ALU.mult, op1=ALU.add)
                    if k < TAPS - 2:
                        settled(i)
                i.then_inc(M["conv"], 1)
            dve.wait_ge(M["g"], 1)
            V.tensor_tensor(gm[:], PS[:, 5, 0:P], tri[:], ALU.mult).then_inc(M["gm"], 1)

            def x_times(dst, n, w):
                dve.wait_ge(M["xtok"], n + 1)
                return V.tensor_tensor(dst[:, n * 8:(n + 1) * 8, :], PS[:, 3 + n, :].rearrange("p (h d) -> p h d", h=8),
                                       w[:, n * 8:(n + 1) * 8].rearrange("p (h o) -> p h o", o=1).to_broadcast([P, 8, HP]),
                                       ALU.mult)

            dve.wait_ge(M["gm"], 1)
            dve.wait_ge(M["decay"], 4)
            for n in range(2):
                x_times(xdt, n, dts[:, 1, :])
                part = dec[:, n * 8:(n + 1) * 8, :]
                V.tensor_tensor(part, part, gm[:].rearrange("p (o t) -> p o t", o=1).to_broadcast([P, 8, T]),
                                ALU.mult).then_inc(M["mdec"], 1)
            for n in range(2):
                settled(x_times(xD_, n, row[:, R_D:R_D + MH]))
            dve.wait_ge(M["zsilu"], 1)
            for n in range(2):
                dve.wait_ge(M["y"], n + 1)
                h = slice(n * 512, (n + 1) * 512)
                settled(V.tensor_tensor(y_sb[:, h], PS[:, 6 + n, :], xD_[:, n * 8:(n + 1) * 8, :].rearrange("p h d -> p (h d)"),
                                        ALU.add))
                V.tensor_tensor(y_sb[:, h], y_sb[:, h], zs[:, h], ALU.mult).then_inc(M["yg"], 1)
            dve.wait_ge(M["yg"], 2)
            for n in range(2):
                dve.wait_ge(M["yT"], n + 1)
                V.tensor_tensor(yT[:, n * 4:(n + 1) * 4, :], PS[:, 3 + n, :].rearrange("p (c t) -> p c t", c=4),
                                vec[:, V_SSM + n * 4:V_SSM + (n + 1) * 4].rearrange("p (c o) -> p c o", o=1).to_broadcast([P, 4, T]),
                                ALU.mult).then_inc(M["yTs"], 1)
            mean_square(y_sb[:], ysq[:], 1)
            for c in range(C_W1, C_W1 + 2):
                chunk_low(c)
            dve.wait_ge(rstd_ready, 3)
            dve.wait_ge(M["outp"], 1)
            V.scalar_tensor_tensor(out=mid[:], in0=PS[:, 5, :], scalar=rs[:, 3:4], in1=res[:], op0=ALU.mult,
                                   op1=ALU.add).then_inc(mid_ready, 1)
            dve.wait_ge(mid_ready, 2)
            mean_square(mid[:], junk[:], 0)
            copy_nT(3, PS[:, 6, :], V_MOE)
            chunk_low(C_W1 + 2)

            dve.wait_ge(M["logit"], 1)
            settled(V.memset(rsc[:, 0, :], MASKED))
            dve.wait_ge(rstd_ready, 4)
            settled(V.tensor_scalar(rsc[:, 0, 0:E1], PS[:, 7, 0:E1], rs[:, 2:3], None, ALU.mult))
            settled(V.max(r8[:, 0:8], rsc[:, 0, 0:E1]))
            V.tensor_scalar(rsc[:, 1, 0:E1], rsc[:, 0, 0:E1], r8[:, 0:1], None, ALU.subtract).then_inc(M["rexp"], 1)
            settled(V.memset(r8[:, 2:8], MASKED))
            settled(V.match_replace(rsc[:, 2, 0:16], r8[:, 0:8], rsc[:, 0, 0:16], 2 * MASKED))
            settled(V.tensor_tensor(rsc[:, 3, 0:E1], rsc[:, 2, 0:E1], rsc[:, 0, 0:E1], ALU.is_lt))
            dve.wait_ge(M["rexp"], 2)
            settled(V.tensor_tensor_reduce(out=rsc[:, 1, 0:E1], in0=r8[:, 8:16], in1=rsc[:, 3, 0:E1], scale=1.0, scalar=0.0,
                                           op0=ALU.mult, op1=ALU.add, accum_out=wsum[:]))
            settled(V.reciprocal(wsum[:], wsum[:]))
            settled(V.tensor_scalar(cw[:, 0:E1], rsc[:, 1, 0:E1], wsum[:], None, ALU.mult))

            def hidden(s, par, w):
                dve.wait_ge(silu_ready, s + 1)
                V.tensor_scalar(h_act[:, par, :], h_silu[:, par, :], w, None, ALU.mult).then_inc(act_ready, 1)

            def hidden_T(s, par):
                dve.wait_ge(H["hT"], s + 1)
                low(hTl[:, par].rearrange("p c t -> p (c t)"), PS[:, 3 + par, :],
                    hTh[:, par].rearrange("p c t -> p (c t)")).then_inc(hT_ready, 1)

            def moe_step(s, t, w, i=0):
                hidden(s, t % 2, w)
                if t >= 2:
                    chunk_low(down_chunk(C_W1, t - 1, STEPS1), i)
                if t >= 1:
                    hidden_T(s - 1, (t + 1) % 2)
                for c in up_ahead(C_W1, t, STEPS1):
                    chunk_low(c, i)

            for s in range(4):
                moe_step(s, s, cw[:, 0:1])
                if s == 0:
                    chunk_low(C_W1 + 3)
            with dve.Fori(1, E1 - 1) as e:
                for t in range(4):
                    moe_step(e * 4 + t, 4 + t, cw[:, bass.ds(e, 1)], e - 1)
            for s in range(STEPS1 - 4, STEPS1):
                moe_step(s, s, cw[:, E1 - 1:E1])
            hidden_T(STEPS1 - 1, (STEPS1 - 1) % 2)
            chunk_low(down_chunk(C_W1, STEPS1 - 1, STEPS1))
            chunk_low(C_ATT)

            dve.wait_ge(ring_used, C_ATT)
            variance(ACC, FFN_EPS)
            V.tensor_scalar(nrm[:], ACC, moments[:, 0:1], None, ALU.subtract).then_inc(norm_ready, 1)
            V.tensor_copy(xt[:], ACC).then_inc(xt_ready, 1)
            copy_nT(4, PS[:, 7, :], V_LN1)
            chunk_low(C_ATT + 1)
            dve.wait_ge(rstd_ready, 5)
            dve.wait_ge(norm_ready, 3)
            V.tensor_scalar(res[:], nrm[:], rs[:, 0:1], None, ALU.mult).then_inc(mid_ready, 1)
            dve.wait_ge(L["rope"], 16)
            settled(V.tensor_scalar(rpn[:], rp[:], rs[:, 1:2], None, ALU.mult))
            chunk_low(C_ATT + 2)

            def rotate(bank, par, read, done, n):
                src = bank.rearrange("p (h d) -> p h d", h=4)
                half = AD // 2

                def bc(a):
                    return a.rearrange("p (o d) -> p o d", o=1).to_broadcast([P, 4, a.shape[-1]])

                V.tensor_tensor(ra[:, par], src, bc(rpn[:, 0, :]), ALU.mult)
                V.tensor_tensor(rb[:, par, :, 0:half], src[:, :, half:AD], bc(rpn[:, 1, 0:half]), ALU.mult)
                V.tensor_tensor(rb[:, par, :, half:AD], src[:, :, 0:half], bc(rpn[:, 1, half:AD]), ALU.mult).then_inc(read, 1)
                dve.wait_ge(read, n)
                V.tensor_tensor(rq[:, par], ra[:, par], rb[:, par], ALU.add).then_inc(done, 1)

            def a_rope(u):
                dve.wait_ge(ring_used, wq_chunk(u) + 1)
                if u == 1:
                    dve.wait_ge(A["kT"], 1)
                rotate(PS[:, 1 + u % 2, :], u % 2, A["ropes"], A["rope"], u + 1)

            def a_max(u):
                dve.wait_ge(A["s"], u + 1)
                for c in range(4):
                    i = V.tensor_tensor_reduce(out=asc[:, u % 2, c, :], in0=PS[:, 4 + u % 2, c * P:(c + 1) * P], in1=amask[:],
                                               scale=1.0, scalar=2 * MASKED, op0=ALU.add, op1=ALU.max,
                                               accum_out=amx[:, u % 2, c:c + 1])
                i.then_inc(A["max"], 1)
                dve.wait_ge(A["max"], u + 1)
                V.tensor_scalar(anb[:, u % 2, :], amx[:, u % 2, :], -(float(AD) ** -0.5), None, ALU.mult).then_inc(A["nb"], 1)

            def a_normalise(u):
                dve.wait_ge(A["exp"], u + 1)
                V.reciprocal(arc[:, u % 2, :], asm[:, u % 2, :]).then_inc(A["rec"], 1)
                dve.wait_ge(A["rec"], u + 1)
                V.tensor_tensor(apn[:, u % 2], apr[:, u % 2],
                                arc[:, u % 2, :].rearrange("p (h o) -> p h o", o=1).to_broadcast([P, 4, T]),
                                ALU.mult).then_inc(A["pn"], 1)

            def flat(a):
                return a.rearrange("p h t -> p (h t)")

            def a_copy_pT(u):
                dve.wait_ge(H["ap"], u + 1)
                low(flat(apTl[:]), PS[:, 6, :], flat(apTh[:])).then_inc(A["pTs"], 1)

            def a_copy_qT(u):
                dve.wait_ge(H["aq"], u + 1)
                low(flat(aqTl[:]), PS[:, 3, :], flat(aqTh[:])).then_inc(A["qTs"], 1)

            dve.wait_ge(ring_used, C_ATT + 1)
            rotate(PS[:, 4, :], 1, A["kv"], A["krope"], 1)
            chunk_low(C_ATT + 3)
            dve.wait_ge(H["v"], 1)
            V.scalar_tensor_tensor(out=flat(avl[:]), in0=PS[:, 5, :], scalar=rs[:, 1:2], in1=flat(avh[:]).bitcast(F32),
                                   op0=ALU.mult, op1=ALU.subtract).then_inc(LO["v"], 1)
            a_rope(0)
            dve.wait_ge(H["kT"], 1)
            low(flat(akTl[:]), PS[:, 6, :], flat(akTh[:])).then_inc(A["kTs"], 1)
            a_rope(1)
            a_copy_qT(0)
            chunk_low(wq_chunk(2))
            a_max(0)
            a_copy_qT(1)
            a_normalise(0)
            a_rope(2)
            a_copy_pT(0)
            a_max(1)
            chunk_low(wq_chunk(3))
            for s in range(3, UNITS + A_LAG):
                if s <= UNITS:
                    a_copy_qT(s - 1)
                if s < UNITS + 2:
                    a_normalise(s - 2)
                if s < UNITS - 1:
                    chunk_low(wq_chunk(s + 1))
                if s <= UNITS:
                    a_max(s - 1)
                if s < UNITS + 2:
                    a_copy_pT(s - 2)
                if s < UNITS:
                    a_rope(s)
                if s > UNITS:
                    chunk_low(C_FFN + s - UNITS - 1)

            dve.wait_ge(ring_used, C_FFN)
            V.tensor_copy(mid[:], ACC).then_inc(mid_ready, 1)
            dve.wait_ge(mid_ready, 4)
            mean_square(mid[:], junk[:], 0)
            copy_nT(5, PS[:, 6, :], V_LN2)
            chunk_low(C_FFN + 2)

            dve.wait_ge(A["rsig"], 1)
            settled(V.tensor_tensor(rsc[:, 1, :], rsc[:, 0, :], row[:, R_EB:R_EB + E2], ALU.add))
            settled(V.max(r8[:, 0:8], rsc[:, 1, :]))
            settled(V.match_replace(rsc[:, 2, :], r8[:, 0:8], rsc[:, 1, :], 2 * MASKED))
            settled(V.tensor_tensor(rsc[:, 3, :], rsc[:, 2, :], rsc[:, 1, :], ALU.is_lt))
            settled(V.tensor_tensor_reduce(out=rsc[:, 1, :], in0=rsc[:, 0, :], in1=rsc[:, 3, :], scale=1.0, scalar=0.0,
                                           op0=ALU.mult, op1=ALU.add, accum_out=wsum[:]))
            settled(V.reciprocal(wsum[:], wsum[:]))
            dve.wait_ge(rstd_ready, 6)
            settled(V.tensor_copy(cw[:, E2:E2 + 1], rs[:, 2:3]))
            settled(V.tensor_scalar(cw[:, 0:E2], rsc[:, 1, :], wsum[:], rs[:, 2:3], ALU.mult, ALU.mult))
            chunk_low(C_FFN + 3)

            def gated(s, par, w):
                dve.wait_ge(gsilu_ready, s + 1)
                V.scalar_tensor_tensor(out=h_act[:, par, 0:FF2], in0=PS[:, 1 + par, FF2:2 * FF2], scalar=w,
                                       in1=h_silu[:, par, 0:FF2], op0=ALU.mult, op1=ALU.mult).then_inc(a_ready, 1)

            def gated_T(s, par):
                dve.wait_ge(H["aT"], s + 1)
                low(hTl[:, par, 0:2].rearrange("p c t -> p (c t)"), PS[:, 3 + par, 0:2 * P],
                    hTh[:, par, 0:2].rearrange("p c t -> p (c t)")).then_inc(aT_ready, 1)

            def ffn_step(s, t, w, i=0):
                gated(s, t % 2, w)
                if t >= 2:
                    chunk_low(down_chunk(C_FFN, t - 1, STEPS2), i)
                if t >= 1:
                    gated_T(s - 1, (t + 1) % 2)
                for c in up_ahead(C_FFN, t, STEPS2):
                    chunk_low(c, i)

            for s in range(5):
                ffn_step(s, s, cw[:, s:s + 1])
            with dve.Fori(0, (STEPS2 - 5) // 4 - 1) as i:
                for t in range(4):
                    ffn_step(i * 4 + 5 + t, 5 + t, cw[:, bass.ds(i * 4 + 5 + t, 1)], i)
            for s in range(STEPS2 - 4, STEPS2):
                ffn_step(s, s, cw[:, s:s + 1])
            gated_T(STEPS2 - 1, (STEPS2 - 1) % 2)
            chunk_low(down_chunk(C_FFN, STEPS2 - 1, STEPS2))
            dve.wait_ge(ring_used, CHUNKS)
            V.tensor_copy(mid[:], ACC).then_inc(mid_ready, 1)


def kernel(**inputs):
    import numpy as np
    import concourse.bacc as bacc
    from concourse import mybir as mb
    from concourse.bass_utils import run_bass_kernel_spmd

    a = {k: np.asarray(v) for k, v in inputs.items()}
    m, f, xa = "L0_attn_", "L0_ffn_", "L0_xattn_"

    def pieces(w, n):
        k, cols = w.shape
        return w.reshape(k // P, P, cols // n, n).transpose(2, 1, 0, 3).reshape(cols // n, P, -1)

    def rows_of(w, n):
        k, cols = w.shape
        return w.reshape(k // (P * n), n, P, cols).transpose(0, 2, 1, 3).reshape(k // (P * n), P, n * cols)

    def column(v):
        return v.reshape(-1, P).T

    ctx = a["ctx_1024"]
    wk = a[xa + "Wk"].reshape(DC, XKV, XD).transpose(1, 2, 0)
    qk = np.concatenate([pieces(a[xa + "Wq"], 256), wk], axis=2)
    vo = np.concatenate([pieces(a[xa + "Wv"], XD), rows_of(a[xa + "Wo"], 2)], axis=2)
    ipw = a[m + "in_proj_w"].T

    def conv_pieces(v):
        n = v.shape[1]
        t = np.zeros((P, CC, n), np.float32)
        t[:, :XC] = v[:DI].reshape(XC, P, n).transpose(1, 0, 2)
        t[:DS, XC] = v[DI:DI + DS]
        t[:DS, XC + 1] = v[DI + DS:]
        return t.reshape(P, CC * n)

    vecs = np.concatenate([
        column(a[m + "norm_mamba_w"]), column(a[m + "norm_moe_w"]), column(a[m + "ssm_norm_w"]),
        column(a[f + "ln1_w"]), column(a[f + "ln2_w"]),
        conv_pieces(a[m + "conv_w"]), conv_pieces(a[m + "conv_b"][:, None]),
        pieces(a[m + "gate_w"].T, E1)[0], pieces(a[f + "Wr"], E2)[0],
        pieces(ipw[:, 2 * DI:], BCDT)[0]], axis=1)
    rows = np.concatenate([a[m + "dt_bias"], a[m + "A_log"], a[m + "D"], a[f + "expert_bias"]])[None]
    inv = (1.0 / 10000.0 ** (np.arange(0, AD, 2, dtype=np.float32) / AD)).astype(np.float32)
    ang = (np.arange(S, dtype=np.float32)[:, None] * inv[None]).astype(np.float32)
    ang = np.concatenate([ang, ang])
    rope = np.stack([np.concatenate([np.cos(ang), np.cos(ang)], 1), np.concatenate([-np.sin(ang), np.sin(ang)], 1)], 1)

    w1 = a[m + "w1"].reshape(E1, N1, 512, KD, P).transpose(0, 1, 4, 3, 2).reshape(STEPS1, P, CHUNK)
    w2 = a[m + "w2"].reshape(E1, D, N1, 4, P).transpose(0, 2, 4, 3, 1).reshape(STEPS1, P, CHUNK)
    g = np.concatenate([a[f + "Wg"], a[f + "Wsg"][None]]).reshape(STEPS2, KD, P, FF2)
    u = np.concatenate([a[f + "Wu"], a[f + "Wsu"][None]]).reshape(STEPS2, KD, P, FF2)
    gu = np.stack([g, u], axis=3).transpose(0, 2, 1, 3, 4).reshape(STEPS2, P, CHUNK)
    dn = np.concatenate([a[f + "Wd"], a[f + "Wsd"][None]]).reshape(STEPS2, 2, P, D).transpose(0, 2, 1, 3).reshape(STEPS2, P, 2 * D)
    arrays = {
        "x": a["x"].reshape(T, D),
        "mask": a["mask_BxS2_bf1"].reshape(1, B * S2).view(np.uint8),
        "ctx": ctx.reshape(B, SC, P, DC).transpose(2, 0, 1, 3),
        "ctxT": ctx.transpose(0, 2, 1).reshape(B, KC, P, S2).transpose(2, 0, 1, 3),
        "qk": qk, "vo": vo, "vecs": vecs, "rows": rows, "rope": rope,
        "in_w": ipw[:, :2 * DI].reshape(KD, P, 2 * DI),
        "out_w": rows_of(a[m + "out_proj_w"].T, 4),
        "w1": w1, "w2": w2,
        "wkv": np.concatenate([pieces(a[f + "Wk"], 512), pieces(a[f + "Wv"], 512)]),
        "wq": pieces(a[f + "Wq"], 512), "wo": rows_of(a[f + "Wo"], 4),
        "gu": gu, "dn": dn,
    }
    arrays = {"in_" + k: np.ascontiguousarray(v) for k, v in arrays.items()}
    nc = bacc.Bacc("TRN2", target_bir_lowering=False, num_devices=1)
    args = [nc.dram_tensor(k, v.shape, mb.dt.from_np(v.dtype), kind="ExternalInput").ap() for k, v in arrays.items()]
    out = nc.dram_tensor("out_x", (T, D), F32, kind="ExternalOutput").ap()
    build(nc, *args, out)
    r = run_bass_kernel_spmd(nc, [arrays], core_ids=[0])
    return r.results[0]["out_x"].reshape(B, S, D)
```
